# Optimizing a Trainium2 kernel written in Bass

```python
import numpy as np
import jax
import jax.numpy as jnp

def _softmax(x, axis=-1):
    return jax.nn.softmax(x, axis=axis)

def _gelu(x):
    return jax.nn.gelu(x, approximate=True)

def _silu(x):
    return jax.nn.silu(x)

def _sigmoid(x):
    return jax.nn.sigmoid(x)

def _layernorm(x, axis=-1, eps=1e-05):
    m = jnp.mean(x, axis=axis, keepdims=True)
    v = jnp.var(x, axis=axis, keepdims=True)
    return (x - m) / jnp.sqrt(v + eps)

def _scatter_add(tgt, idx, src, axis=0):
    return tgt.at[idx].add(src)

def _segment_sum(src, seg, n):
    return jax.ops.segment_sum(src, seg, n)
kernel_name = 'mk_gnn_resnorm_d4_gnn_r8_589de8'

def setup_inputs(seed: int=0):
    np.random.seed(seed)
    _w = jnp.asarray

    def _rec_inputs():
        import jax
        import jax.numpy as jnp
        _gk = jax.random.key(seed)
        x = -0.000202 + 1 * jax.random.normal(jax.random.fold_in(_gk, 1), (6250, 128), jnp.float32)
        _s = jax.random.randint(jax.random.fold_in(_gk, 2), (100000,), 0, 6250, jnp.int32)
        _d = jax.random.randint(jax.random.fold_in(_gk, 3), (100000,), 0, 6250, jnp.int32)
        _loop = jnp.arange(6250, dtype=jnp.int32)
        src = jnp.concatenate([_s, _d, _loop])
        dst = jnp.concatenate([_d, _s, _loop])
        _o = jnp.argsort(dst, stable=True)
        src = src[_o]
        dst = dst[_o]
        edge_weight = jax.random.uniform(jax.random.fold_in(_gk, 13), (206250,), jnp.float32, 0.0, 0.999998)
        edge_weight1 = jax.random.uniform(jax.random.fold_in(_gk, 14), (206250, 1), jnp.float32, 0.0, 0.999998)
        return (x, src, dst, edge_weight, edge_weight1)
    x, src, dst, edge_weight, edge_weight1 = _rec_inputs()

    def _L0_gnn_setup():
        import jax, jax.numpy as jnp
        import numpy as np
        N = 6250
        E = 100000
        F = 128
        UNITS = 128
        ATT_UNITS = 128
        HEADS = 8

        def segment_softmax(scores, seg, num_segments):
            smax = jax.ops.segment_max(scores, seg, num_segments=num_segments)
            sexp = jnp.exp(scores - smax[seg])
            ssum = jax.ops.segment_sum(sexp, seg, num_segments=num_segments)
            return sexp / ssum[seg]
        key = jax.random.key(seed)
        ks = jax.random.split(key, 6)
        s = 1.0 / np.sqrt(F).astype(np.float32)
        return {'x': jax.random.normal(ks[0], (N, F), dtype=jnp.float32), 'edge_index': jax.random.randint(ks[1], (2, E), 0, N, dtype=jnp.int32), 'query_kernel': jax.random.normal(ks[2], (F, ATT_UNITS), dtype=jnp.float32) * s, 'query_bias': jnp.zeros((ATT_UNITS,), jnp.float32), 'key_kernel': jax.random.normal(ks[3], (F, ATT_UNITS), dtype=jnp.float32) * s, 'key_bias': jnp.zeros((ATT_UNITS,), jnp.float32), 'kernel': jax.random.normal(ks[4], (F, UNITS), dtype=jnp.float32) * s, 'bias': jnp.zeros((UNITS,), jnp.float32)}
    _L0_gnn_all = _L0_gnn_setup()
    _L0_gnn_in = {k: v for k, v in _L0_gnn_all.items() if k in ('query_kernel', 'query_bias', 'key_kernel', 'key_bias', 'kernel', 'bias')}
    del _L0_gnn_all

    def _L1_gnn_setup():
        import jax, jax.numpy as jnp
        import numpy as np
        N, E, C = (12500, 200000, 128)
        EPS = 1e-05

        def _bn(x, g, b):
            mu = jnp.mean(x, axis=0)
            var = jnp.mean((x - mu) ** 2, axis=0)
            return g * (x - mu) * jax.lax.rsqrt(var + EPS) + b
        key = jax.random.key(seed)
        ks = jax.random.split(key, 8)
        s = 1.0 / np.sqrt(C)
        return {'h': jax.random.normal(ks[0], (N, C), jnp.float32), 'src': jax.random.randint(ks[1], (E,), 0, N, jnp.int32), 'dst': jax.random.randint(ks[2], (E,), 0, N, jnp.int32), 'theta_w': jax.random.normal(ks[3], (C, C), jnp.float32) * s, 'phi_w': jax.random.normal(ks[4], (C, C), jnp.float32) * s, 'fc1_w': jax.random.normal(ks[5], (C, C), jnp.float32) * s, 'bn0_g': jnp.ones((C,), jnp.float32), 'bn0_b': jnp.zeros((C,), jnp.float32), 'bn1_g': jnp.ones((C,), jnp.float32), 'bn1_b': jnp.zeros((C,), jnp.float32)}
    _L1_gnn_all = _L1_gnn_setup()
    _L1_gnn_in = {k: v for k, v in _L1_gnn_all.items() if k in ('theta_w', 'phi_w', 'fc1_w', 'bn0_g', 'bn0_b', 'bn1_g', 'bn1_b')}
    del _L1_gnn_all

    def _L2_gnn_setup():
        import jax, jax.numpy as jnp
        import numpy as np
        N_NODES = 6250
        N_EDGES = 100000
        IN_DIM = 128
        HID_DIM = 128
        BN_EPS = 1e-05
        key = jax.random.key(seed)
        ks = jax.random.split(key, 7)
        x = jax.random.normal(ks[0], (N_NODES, IN_DIM), dtype=jnp.float32)
        edge_index = jax.random.randint(ks[1], (2, N_EDGES), 0, N_NODES, dtype=jnp.int32)
        edge_attr = jax.random.uniform(ks[2], (N_EDGES, 1), dtype=jnp.float32)
        W = jax.random.normal(ks[3], (IN_DIM, HID_DIM), dtype=jnp.float32) / np.sqrt(IN_DIM)
        b = jnp.zeros((HID_DIM,), dtype=jnp.float32)
        gamma = jnp.ones((HID_DIM,), dtype=jnp.float32)
        beta = jnp.zeros((HID_DIM,), dtype=jnp.float32)
        return {'x': x, 'edge_index': edge_index, 'edge_attr': edge_attr, 'W': W, 'b': b, 'gamma': gamma, 'beta': beta}
    _L2_gnn_all = _L2_gnn_setup()
    _L2_gnn_in = {k: v for k, v in _L2_gnn_all.items() if k in ('W', 'b', 'gamma', 'beta')}
    del _L2_gnn_all

    def _L3_gnn_setup():
        import jax, jax.numpy as jnp
        import numpy as np
        EPS = 0.0
        key = jax.random.key(seed)
        kx, ke, kw, k1, k2 = jax.random.split(key, 5)
        N, E, D, H = (12500, 75000, 128, 128)
        x = jax.random.normal(kx, (N, D), dtype=jnp.float32)
        edge_index = jax.random.randint(ke, (2, E), 0, N, dtype=jnp.int64)
        edge_weight = jax.random.uniform(kw, (E,), dtype=jnp.float32)
        W1 = jax.random.normal(k1, (D, H), dtype=jnp.float32) * (1.0 / np.sqrt(D))
        b1 = jnp.zeros((H,), dtype=jnp.float32)
        W2 = jax.random.normal(k2, (H, D), dtype=jnp.float32) * (1.0 / np.sqrt(H))
        b2 = jnp.zeros((D,), dtype=jnp.float32)
        return {'x': x, 'edge_index': edge_index, 'edge_weight': edge_weight, 'W1': W1, 'b1': b1, 'W2': W2, 'b2': b2}
    _L3_gnn_all = _L3_gnn_setup()
    _L3_gnn_in = {k: v for k, v in _L3_gnn_all.items() if k in ('W1', 'b1', 'W2', 'b2')}
    del _L3_gnn_all
    return {'x': x, 'src': src, 'dst': dst, 'edge_weight': edge_weight, 'edge_weight1': edge_weight1, 'L0_gnn_query_kernel': _L0_gnn_in['query_kernel'], 'L0_gnn_query_bias': _L0_gnn_in['query_bias'], 'L0_gnn_key_kernel': _L0_gnn_in['key_kernel'], 'L0_gnn_key_bias': _L0_gnn_in['key_bias'], 'L0_gnn_kernel': _L0_gnn_in['kernel'], 'L0_gnn_bias': _L0_gnn_in['bias'], 'L1_gnn_theta_w': _L1_gnn_in['theta_w'], 'L1_gnn_phi_w': _L1_gnn_in['phi_w'], 'L1_gnn_fc1_w': _L1_gnn_in['fc1_w'], 'L1_gnn_bn0_g': _L1_gnn_in['bn0_g'], 'L1_gnn_bn0_b': _L1_gnn_in['bn0_b'], 'L1_gnn_bn1_g': _L1_gnn_in['bn1_g'], 'L1_gnn_bn1_b': _L1_gnn_in['bn1_b'], 'L2_gnn_W': _L2_gnn_in['W'], 'L2_gnn_b': _L2_gnn_in['b'], 'L2_gnn_gamma': _L2_gnn_in['gamma'], 'L2_gnn_beta': _L2_gnn_in['beta'], 'L3_gnn_W1': _L3_gnn_in['W1'], 'L3_gnn_b1': _L3_gnn_in['b1'], 'L3_gnn_W2': _L3_gnn_in['W2'], 'L3_gnn_b2': _L3_gnn_in['b2']}

def reference(x, src, dst, edge_weight, edge_weight1, L0_gnn_query_kernel, L0_gnn_query_bias, L0_gnn_key_kernel, L0_gnn_key_bias, L0_gnn_kernel, L0_gnn_bias, L1_gnn_theta_w, L1_gnn_phi_w, L1_gnn_fc1_w, L1_gnn_bn0_g, L1_gnn_bn0_b, L1_gnn_bn1_g, L1_gnn_bn1_b, L2_gnn_W, L2_gnn_b, L2_gnn_gamma, L2_gnn_beta, L3_gnn_W1, L3_gnn_b1, L3_gnn_W2, L3_gnn_b2):
    import jax
    import jax.numpy as jnp

    def _L0_gnn_ref(x, edge_index, query_kernel, query_bias, key_kernel, key_bias, kernel, bias):
        import jax, jax.numpy as jnp
        import numpy as np
        N = 6250
        E = 100000
        F = 128
        UNITS = 128
        ATT_UNITS = 128
        HEADS = 8

        def segment_softmax(scores, seg, num_segments):
            smax = jax.ops.segment_max(scores, seg, num_segments=num_segments)
            sexp = jnp.exp(scores - smax[seg])
            ssum = jax.ops.segment_sum(sexp, seg, num_segments=num_segments)
            return sexp / ssum[seg]
        num_nodes = x.shape[0]
        loop = jnp.arange(num_nodes, dtype=edge_index.dtype)
        row = jnp.concatenate([edge_index[0], loop])
        col = jnp.concatenate([edge_index[1], loop])
        Q = jax.nn.relu(x @ query_kernel + query_bias)[row]
        K = jax.nn.relu(x @ key_kernel + key_bias)[col]
        V = (x @ kernel)[col]
        Qh = Q.reshape(-1, HEADS, ATT_UNITS // HEADS)
        Kh = K.reshape(-1, HEADS, ATT_UNITS // HEADS)
        att = jnp.sum(Qh * Kh, axis=-1)
        alpha = segment_softmax(att, row, num_nodes)
        Vh = V.reshape(-1, HEADS, UNITS // HEADS)
        msg = Vh * alpha[:, :, None]
        out = jax.ops.segment_sum(msg, row, num_segments=num_nodes)
        out = out.reshape(num_nodes, UNITS)
        out = out + bias
        return out

    def _L1_gnn_ref(h, src, dst, theta_w, phi_w, fc1_w, bn0_g, bn0_b, bn1_g, bn1_b):
        import jax, jax.numpy as jnp
        import numpy as np
        N, E, C = (12500, 200000, 128)
        EPS = 1e-05

        def _bn(x, g, b):
            mu = jnp.mean(x, axis=0)
            var = jnp.mean((x - mu) ** 2, axis=0)
            return g * (x - mu) * jax.lax.rsqrt(var + EPS) + b
        n = h.shape[0]
        x_src = h[src]
        x_dst = h[dst]
        e = (x_dst - x_src) @ theta_w.T + x_src @ phi_w.T
        e = jax.nn.relu(_bn(e, bn0_g, bn0_b))
        e = e @ fc1_w.T
        e = jax.nn.relu(_bn(e, bn1_g, bn1_b))
        agg = jax.ops.segment_sum(e, dst, num_segments=n)
        cnt = jax.ops.segment_sum(jnp.ones((e.shape[0],), e.dtype), dst, num_segments=n)
        x = agg / jnp.maximum(cnt, 1.0)[:, None]
        return jax.nn.relu(x + h)

    def _L2_gnn_ref(x, edge_index, edge_attr, W, b, gamma, beta):
        import jax, jax.numpy as jnp
        import numpy as np
        N_NODES = 6250
        N_EDGES = 100000
        IN_DIM = 128
        HID_DIM = 128
        BN_EPS = 1e-05
        n = x.shape[0]
        loop = jnp.arange(n, dtype=edge_index.dtype)
        src = jnp.concatenate([edge_index[0], loop])
        dst = jnp.concatenate([edge_index[1], loop])
        deg = jax.ops.segment_sum(jnp.ones_like(dst, dtype=x.dtype), dst, num_segments=n)
        dinv = jnp.where(deg > 0, jax.lax.rsqrt(deg), 0.0)
        norm = dinv[src] * dinv[dst]
        h = x @ W
        msg = h[src] * norm[:, None]
        agg = jax.ops.segment_sum(msg, dst, num_segments=n) + b
        y = jax.nn.relu(agg)
        mean = jnp.mean(y, axis=0)
        var = jnp.var(y, axis=0)
        return gamma * (y - mean) * jax.lax.rsqrt(var + BN_EPS) + beta

    def _L3_gnn_ref(x, edge_index, edge_weight, W1, b1, W2, b2):
        import jax, jax.numpy as jnp
        import numpy as np
        EPS = 0.0
        N = x.shape[0]
        src, dst = (edge_index[0], edge_index[1])
        msg = edge_weight[:, None] * x[src]
        agg = jax.ops.segment_sum(msg, dst, num_segments=N)
        out = (1.0 + EPS) * x + agg
        h = jax.nn.relu(out @ W1 + b1)
        return h @ W2 + b2
    edge_index = jnp.stack([src, dst])
    x = _layernorm(x + _L0_gnn_ref(x, edge_index, L0_gnn_query_kernel, L0_gnn_query_bias, L0_gnn_key_kernel, L0_gnn_key_bias, L0_gnn_kernel, L0_gnn_bias), axis=-1)
    x = _layernorm(x + _L1_gnn_ref(x, src, dst, L1_gnn_theta_w, L1_gnn_phi_w, L1_gnn_fc1_w, L1_gnn_bn0_g, L1_gnn_bn0_b, L1_gnn_bn1_g, L1_gnn_bn1_b), axis=-1)
    x = _layernorm(x + _L2_gnn_ref(x, edge_index, edge_weight1, L2_gnn_W, L2_gnn_b, L2_gnn_gamma, L2_gnn_beta), axis=-1)
    x = _layernorm(x + _L3_gnn_ref(x, edge_index, edge_weight, L3_gnn_W1, L3_gnn_b1, L3_gnn_W2, L3_gnn_b2), axis=-1)
    return x

_drawn_inputs = setup_inputs


def setup_inputs(seed=0):
    import zlib

    import numpy as np

    out = dict(_drawn_inputs(seed))
    spreads = {'L0_gnn_query_bias': (0.0, 0.1),
     'L0_gnn_key_bias': (0.0, 0.1),
     'L0_gnn_bias': (0.0, 0.1),
     'L1_gnn_bn0_g': (1.0, 0.577),
     'L1_gnn_bn0_b': (0.0, 0.715),
     'L1_gnn_bn1_g': (1.0, 0.2),
     'L1_gnn_bn1_b': (0.0, 0.1),
     'L2_gnn_b': (0.0, 0.1),
     'L2_gnn_gamma': (1.0, 0.2),
     'L2_gnn_beta': (0.0, 0.1),
     'L3_gnn_b1': (0.0, 0.362),
     'L3_gnn_b2': (0.0, 0.1)}
    factors = {}
    for name, (base, spread) in spreads.items():
        noise = np.random.default_rng([zlib.crc32(name.encode()), seed]).standard_normal(out[name].shape)
        drawn = base * np.exp(spread * noise) if base else spread * noise
        out[name] = jnp.asarray(drawn.astype(out[name].dtype))
    for name, factor in factors.items():
        out[name] = (out[name] * factor).astype(out[name].dtype)
    return out
```

```python
from contextlib import ExitStack

import concourse.bass as bass
from concourse import mybir

F32 = mybir.dt.float32
BF16 = mybir.dt.bfloat16
I32 = mybir.dt.int32
U32 = mybir.dt.uint32
ALU = mybir.AluOpType
ACT = mybir.ActivationFunctionType
AX = mybir.AxisListType.X

P = 128
D = 128
H = 8
HD = D // H
G = 4
GE = G * P
U = 4
EPS = 1e-5
FAR = 1.0e6


class Shapes:

    def __init__(self, nodes, edges):
        self.N, self.E = nodes, edges
        self.NB = -(-nodes // P)
        self.NB1 = (self.NB + 2) // 2 * 2
        self.PAD = self.NB * P
        self.ZROW = self.NB1 * P - 1
        self.SPARE = self.NB


class Sorted:

    def __init__(self, s, loops):
        self.T = -(-s.E // P)
        self.LT = s.NB if loops else 0
        self.TT = -(-(self.T + self.LT) // 8) * 8
        self.C = -(-self.TT // P)
        self.rows = self.TT * P
        ng = (s.E + self.LT * P) // GE + s.NB
        self.NGS = -(-ng // U) * U
        self.GMIN = (s.E + self.LT * P) // GE // U * U
        self.GC = -(-self.NGS // P)


class Chain:

    def __init__(self, eng, sem):
        self.eng, self.sem, self.n = eng, sem, 0

    def step(self, ins):
        self.n += 1
        ins.then_inc(self.sem, 1)
        self.eng.wait_ge(self.sem, self.n)

    def go(self, ins):
        self.n += 1
        ins.then_inc(self.sem, 1)


class Semaphores:

    def __init__(self, nc, ctx):
        self.nc, self.ctx, self.free = nc, ctx, []

    def take(self, name):
        return self.free.pop() if self.free else self.ctx.enter_context(self.nc.semaphore(name))

    def hand_back(self, taken):
        with self.nc.Block() as block:
            @block.gpsimd
            def _(pool):
                for s in taken:
                    pool.sem_clear(s)
        self.free += taken


def scope(nc, ctx, k):
    taken = []

    def sb(name, cols, dt=F32, parts=P):
        return ctx.enter_context(nc.sbuf_tensor(name, [parts, cols], dt))

    def ps(name, cols, dt=F32):
        return ctx.enter_context(nc.psum_tensor(name, [P, cols], dt))

    def sem(name, own=False):
        if own:
            return k["sems"].ctx.enter_context(nc.semaphore(name))
        taken.append(k["sems"].take(name))
        return taken[-1]
    ctx.callback(lambda: taken and k["sems"].hand_back(taken))
    return sb, ps, sem


def phase_constants(nc, s, x_in, k):
    with ExitStack() as ctx:
        sb, ps, sem = scope(nc, ctx, k)
        fi, pi = sb("fi", P, I32), sb("pi", 1, I32)
        ff = sb("ff", P)
        iota_done, const_step, x_cleared, x_loaded = sem("iota_done"), sem("const_step"), sem("x_cleared"), sem("x_loaded")
        full = s.N // P
        rest = s.N - full * P
        with nc.Block() as block:
            @block.gpsimd
            def _(pool):
                nc.gpsimd.iota(fi[:, :], pattern=[[1, P]], base=0, channel_multiplier=0).then_inc(iota_done, 1)
                nc.gpsimd.iota(pi[:, :], pattern=[[1, 1]], base=0, channel_multiplier=1).then_inc(iota_done, 1)

            @block.vector
            def _(dve):
                c = Chain(dve, const_step)
                nc.vector.memset(k["x"][:, full * D:], 0.0).then_inc(x_cleared, 1)
                c.go(nc.vector.memset(k["ones"][:, :], 1.0))
                c.go(nc.vector.memset(k["zero"][:, :], 0.0))
                dve.wait_ge(iota_done, 2)
                c.go(nc.vector.tensor_copy(ff[:, :], fi[:, :]))
                c.go(nc.vector.tensor_copy(k["iota_f"][:, :], fi[:, :]))
                c.step(nc.vector.tensor_copy(k["iota_p"][:, :], pi[:, :]))
                col = k["iota_p"][:, 0:1]
                c.go(nc.vector.tensor_scalar(k["ident"][:, :], ff[:, :], col, None, ALU.is_equal))
                c.go(nc.vector.tensor_scalar(k["ident_b"][:, :], ff[:, :], col, None, ALU.is_equal))
                c.go(nc.vector.memset(k["before"][:, 0:3 * P], 1.0))
                c.go(nc.vector.tensor_scalar(k["before"][:, 3 * P:], ff[:, :], col, None, ALU.is_lt))
                c.step(nc.vector.tensor_scalar(k["after"][:, :], ff[:, :], col, None, ALU.is_gt))

            @block.sync
            def _(sp):
                sp.wait_ge(x_cleared, 1)
                n = 0
                if full:
                    sp.dma_start(k["x"][:, 0:full * D].rearrange("p (b f) -> p b f", f=D),
                                 x_in[0:full * P, :].rearrange("(b p) f -> p b f", p=P)).then_inc(x_loaded, 16)
                    n += 16
                if rest:
                    sp.dma_start(k["x"][0:rest, full * D:(full + 1) * D], x_in[full * P:, :]).then_inc(x_loaded, 16)
                    n += 16
                sp.wait_ge(x_loaded, n)


def phase_sort_input(nc, s, z, k, a, key_in, other_in, weight_in, tag):
    with ExitStack() as ctx:
        sb, ps, sem = scope(nc, ctx, k)
        W = z.C * P
        ki, oi = sb("ki" + tag, W, I32), sb("oi" + tag, W, I32)
        kf, of = sb("kf" + tag, W), sb("of" + tag, W)
        li, lf, lm = sb("li" + tag, W, I32), sb("lf" + tag, W), sb("lm" + tag, W)
        wf = sb("wf" + tag, W) if weight_in is not None else None
        hi_i, lo_i = sb("hi_i" + tag, W, I32), sb("lo_i" + tag, W, I32)
        tps = [ps(f"tps{u}" + tag, 4 * P) for u in range(2)]
        cleared, loaded, stored = sem("cleared"), sem("loaded"), sem("stored")
        loop_iota, step = sem("loop_iota"), sem("in_step")
        rows_ready, turned, evacuated = sem("rows_ready"), sem("turned"), sem("evac")
        arrays = [(kf, 0), (of, 1)] + ([(wf, 2)] if wf is not None else [])
        lots = [(src, c, col, ci) for src, col in arrays for ci, c in enumerate(range(0, z.C, 4))]
        full_c, full_t = s.E // (P * P), s.E // P
        part = s.E - full_t * P

        def pieces(dst, src):
            if full_c:
                yield (dst[:, 0:full_c * P].rearrange("q (c l) -> q c l", l=P),
                       src[0:full_c * P * P].rearrange("(c q l) -> q c l", q=P, l=P))
            q = full_t - full_c * P
            if q:
                yield (dst[0:q, full_c * P:(full_c + 1) * P],
                       src[full_c * P * P:full_t * P].rearrange("(q l) -> q l", l=P))
            if part:
                yield (dst[q:q + 1, full_c * P:full_c * P + part],
                       src[full_t * P:s.E].rearrange("(q l) -> q l", q=1))

        pieces_n = len(list(pieces(ki, key_in))) * (2 if wf is None else 3)
        with nc.Block() as block:
            @block.sync
            def _(sp):
                sp.wait_ge(cleared, 2 if wf is None else 3)
                todo = [(ki, key_in), (oi, other_in)] + ([(wf, weight_in)] if wf is not None else [])
                for dst, src in todo:
                    for d, r in pieces(dst, src):
                        sp.dma_start(d, r).then_inc(loaded, 16)
                sp.wait_ge(rows_ready, 1)
                sp.dma_start(a["keyrow"][0:W * P].rearrange("(c q l) -> q c l", q=P, l=P),
                             kf[:, :].rearrange("q (c l) -> q c l", l=P)).then_inc(stored, 16)
                sp.dma_start(a["keyrow"][W * P:W * P + 8 * P].rearrange("(c l) -> c l", l=P), kf[0:8, 0:P]).then_inc(stored, 16)
                sp.wait_ge(stored, 32)

            @block.gpsimd
            def _(pool):
                nc.gpsimd.iota(li[:, :].rearrange("q (c l) -> q c l", l=P), pattern=[[P * P, z.C], [1, P]],
                               base=-z.T * P, channel_multiplier=P).then_inc(loop_iota, 1)

            @block.vector
            def _(dve):
                c = Chain(dve, step)
                nc.vector.memset(ki[:, :], s.PAD).then_inc(cleared, 1)
                nc.vector.memset(oi[:, :], 0).then_inc(cleared, 1)
                if wf is not None:
                    nc.vector.memset(wf[:, :], 0.0).then_inc(cleared, 1)
                dve.wait_ge(loaded, 16 * pieces_n)
                c.go(nc.vector.tensor_copy(kf[:, :], ki[:, :]))
                c.step(nc.vector.tensor_copy(of[:, :], oi[:, :]))
                if z.LT:
                    dve.wait_ge(loop_iota, 1)
                    c.step(nc.vector.tensor_copy(lf[:, :], li[:, :]))
                    c.step(nc.vector.tensor_scalar(lm[:, :], lf[:, :], 0.0, None, ALU.is_ge))
                    c.step(nc.vector.scalar_tensor_tensor(out=lm[:, :], in0=lf[:, :], scalar=float(s.PAD), in1=lm[:, :],
                                                          op0=ALU.is_lt, op1=ALU.mult))
                    for dst in (kf, of):
                        tmp = hi_i[:, :].bitcast(F32)
                        c.step(nc.vector.tensor_tensor(tmp, lf[:, :], dst[:, :], ALU.subtract))
                        c.step(nc.vector.tensor_tensor(tmp, tmp, lm[:, :], ALU.mult))
                        c.step(nc.vector.tensor_tensor(dst[:, :], dst[:, :], tmp, ALU.add))
                dve.sem_inc(rows_ready, 1)
                for n, (src, c0, col, _) in enumerate(lots):
                    w = min(4, z.C - c0) * P
                    dve.wait_ge(turned, n + 1)
                    dst = a["key"][:, c0 * P:c0 * P + w] if col == 0 else \
                        a["pay"][:, :].rearrange("p (t c) -> p t c", c=4)[:, c0 * P:c0 * P + w, col]
                    nc.vector.tensor_copy(dst, tps[n % 2][:, 0:w]).then_inc(evacuated, 1)
                dve.wait_ge(evacuated, len(lots))
                c.go(nc.vector.memset(a["key"][:, W:], 0.0))
                c.go(nc.vector.memset(a["hi"][:, W:], 0.0))
                c.go(nc.vector.memset(a["lo"][:, W:], 0.0))
                pay = a["pay"][:, :].rearrange("p (t c) -> p t c", c=4)
                c.step(nc.vector.tensor_scalar(pay[:, :, 0], a["key"][:, 0:W], float(s.PAD), FAR, ALU.is_ge, ALU.mult))
                c.go(nc.vector.tensor_tensor(pay[:, :, 0], pay[:, :, 0], a["key"][:, 0:W], ALU.add))
                c.go(nc.vector.memset(pay[:, :, 3], 0.0))
                if wf is None:
                    c.go(nc.vector.memset(pay[:, :, 2], 0.0))
                c.step(nc.vector.tensor_copy(lo_i[:, :], a["key"][:, 0:W]))
                c.go(nc.vector.tensor_single_scalar(hi_i[:, :], lo_i[:, :], 7, ALU.arith_shift_right))
                c.step(nc.vector.tensor_single_scalar(lo_i[:, :], lo_i[:, :], P - 1, ALU.bitwise_and))
                c.go(nc.vector.tensor_copy(a["hi"][:, 0:W], hi_i[:, :]))
                c.step(nc.vector.tensor_copy(a["lo"][:, 0:W], lo_i[:, :]))

            @block.tensor
            def _(pe):
                pe.wait_ge(rows_ready, 1)
                for n, (src, c0, col, _) in enumerate(lots):
                    if n >= 2:
                        pe.wait_ge(evacuated, n - 1)
                    for c in range(c0, min(c0 + 4, z.C)):
                        last = nc.tensor.transpose(tps[n % 2][:, (c - c0) * P:(c - c0 + 1) * P],
                                                   src[:, c * P:(c + 1) * P], k["ident"][:, :])
                    last.then_inc(turned, 1)


def phase_histogram(nc, s, z, k, a, tag):
    with ExitStack() as ctx:
        sb, ps, sem = scope(nc, ctx, k)
        lo1 = [sb(f"lo1_{u}" + tag, 4 * P, BF16) for u in range(2)]
        hi1 = [sb(f"hi1_{u}" + tag, 4 * s.NB1, BF16) for u in range(2)]
        hist = ps("hist" + tag, s.NB1)
        made = [sem(f"onehot_made{u}") for u in range(2)]
        used = [sem(f"onehot_used{u}") for u in range(2)]
        hist_done, hist_out = sem("hist_done"), sem("hist_out")
        n = z.TT // 8
        with nc.Block() as block:
            @block.vector
            def _(dve):
                for u in range(2):
                    dve.sem_inc(used[u], 1)
                with dve.Fori(1, n + 1) as i:
                    for u in range(2):
                        t0 = (i - 1) * 8 + u * 4
                        dve.wait_ge(used[u], i)
                        for j in range(4):
                            nc.vector.tensor_scalar(lo1[u][:, j * P:(j + 1) * P], k["iota_f"][:, :],
                                                    a["lo"][:, bass.ds(t0 + j, 1)], None, ALU.is_equal)
                        for j in range(4):
                            last = nc.vector.tensor_scalar(hi1[u][:, j * s.NB1:(j + 1) * s.NB1], k["iota_f"][:, 0:s.NB1],
                                                           a["hi"][:, bass.ds(t0 + j, 1)], None, ALU.is_equal)
                        last.then_inc(made[u], 1)
                dve.wait_ge(hist_done, 1)
                nc.vector.tensor_copy(a["counts"][:, :], hist[:, :]).then_inc(hist_out, 1)
                dve.wait_ge(hist_out, 1)

            @block.tensor
            def _(pe):
                nc.tensor.matmul(hist[:, :], k["zero"][:, :], k["zero"][:, 0:s.NB1], start=True, stop=False)
                with pe.Fori(1, n + 1) as i:
                    for u in range(2):
                        pe.wait_ge(made[u], i)
                        for j in range(4):
                            last = nc.tensor.matmul(hist[:, :], lo1[u][:, j * P:(j + 1) * P],
                                                    hi1[u][:, j * s.NB1:(j + 1) * s.NB1], start=False, stop=False)
                        last.then_inc(used[u], 1)
                nc.tensor.matmul(hist[:, :], k["zero"][:, :], k["zero"][:, 0:s.NB1], start=False, stop=True).then_inc(hist_done, 1)


def phase_offsets(nc, s, z, k, a, L, tag):
    with ExitStack() as ctx:
        sb, ps, sem = scope(nc, ctx, k)
        NB1 = s.NB1
        bc, inc, cstart = sb("bc" + tag, NB1), sb("inc" + tag, NB1), sb("cstart" + tag, NB1)
        gi, gc, gend, shift = sb("gi" + tag, NB1, I32), sb("gc" + tag, NB1), sb("gend" + tag, NB1), sb("shift" + tag, NB1)
        gid_i, gid = sb("gid_i" + tag, z.GC, I32), sb("gid" + tag, z.GC)
        m = sb("m" + tag, NB1)
        gb, go = sb("gb" + tag, z.GC), sb("go" + tag, z.GC)
        diag = sb("diag" + tag, 2 * z.GC * P)
        np_i = sb("np_i" + tag, 1, I32)
        p1 = ps("p1" + tag, 2 * NB1)
        pb, po = ps("pb" + tag, z.GC * P), ps("po" + tag, z.GC * P)
        step, sums, gid_done, diag_done, spread = (sem(x) for x in ("off_step", "sums", "gid_done", "diag_done", "spread"))
        with nc.Block() as block:
            @block.gpsimd
            def _(pool):
                nc.gpsimd.iota(gid_i[:, :], pattern=[[P, z.GC]], base=0, channel_multiplier=1).then_inc(gid_done, 1)

            @block.tensor
            def _(pe):
                nc.tensor.matmul(p1[:, 0:NB1], k["ones"][:, :], a["counts"][:, :], start=True, stop=True)
                nc.tensor.matmul(p1[:, NB1:2 * NB1], k["after"][:, :], a["counts"][:, :], start=True, stop=True).then_inc(sums, 1)
                pe.wait_ge(diag_done, 1)
                for dst, at in ((pb, 0), (po, z.GC)):
                    for c in range(z.GC):
                        last = nc.tensor.matmul(dst[:, c * P:(c + 1) * P], k["ones"][:, :],
                                                diag[:, (at + c) * P:(at + c + 1) * P], start=True, stop=True)
                last.then_inc(spread, 1)

            @block.vector
            def _(dve):
                c = Chain(dve, step)
                dve.wait_ge(sums, 1)
                c.step(nc.vector.tensor_copy(bc[:, :], p1[:, 0:NB1]))
                c.step(nc.vector.tensor_tensor_scan(inc[:, :], k["ones"][:, 0:NB1], bc[:, :], 0.0, ALU.mult, ALU.add))
                c.step(nc.vector.tensor_tensor(cstart[:, :], inc[:, :], bc[:, :], ALU.subtract))
                c.go(nc.vector.tensor_tensor(a["first"][:, :], cstart[:, :], p1[:, NB1:2 * NB1], ALU.add))
                c.step(nc.vector.tensor_scalar(inc[:, :], bc[:, :], float(GE - 1), None, ALU.add))
                c.step(nc.vector.tensor_copy(gi[:, :], inc[:, :]))
                c.step(nc.vector.tensor_single_scalar(gi[:, :], gi[:, :], 9, ALU.arith_shift_right))
                c.step(nc.vector.tensor_copy(gc[:, :], gi[:, :]))
                c.step(nc.vector.memset(gc[:, s.NB:], 0.0))
                c.step(nc.vector.tensor_tensor_scan(gend[:, :], k["ones"][:, 0:NB1], gc[:, :], 0.0, ALU.mult, ALU.add))
                c.step(nc.vector.tensor_scalar(m[:, 0:1], gend[:, NB1 - 1:NB1], float(U - 1), None, ALU.add))
                c.step(nc.vector.tensor_copy(np_i[:, :], m[:, 0:1]))
                c.step(nc.vector.tensor_single_scalar(L["rounds"][:, :], np_i[:, :], 2, ALU.arith_shift_right))
                c.step(nc.vector.tensor_tensor(shift[:, :], gend[:, :], gc[:, :], ALU.subtract))
                c.step(nc.vector.scalar_tensor_tensor(out=shift[:, :], in0=shift[:, :], scalar=-float(GE), in1=cstart[:, :],
                                                      op0=ALU.mult, op1=ALU.add))
                c.step(nc.vector.memset(shift[:, s.NB:], float(z.rows)))
                dve.wait_ge(gid_done, 1)
                c.step(nc.vector.tensor_copy(gid[:, :], gid_i[:, :]))
                for q in range(z.GC):
                    c.step(nc.vector.tensor_scalar(m[:, 0:s.NB], gend[:, 0:s.NB], gid[:, q:q + 1], None, ALU.is_le))
                    c.step(nc.vector.tensor_reduce(gb[:, q:q + 1], m[:, 0:s.NB], AX, ALU.add))
                    c.step(nc.vector.tensor_scalar(m[:, :], k["iota_f"][:, 0:NB1], gb[:, q:q + 1], None, ALU.is_equal))
                    c.step(nc.vector.tensor_tensor(m[:, :], m[:, :], shift[:, :], ALU.mult))
                    c.step(nc.vector.tensor_reduce(go[:, q:q + 1], m[:, :], AX, ALU.add))
                    c.step(nc.vector.scalar_tensor_tensor(out=go[:, q:q + 1], in0=gid[:, q:q + 1], scalar=float(GE),
                                                          in1=go[:, q:q + 1], op0=ALU.mult, op1=ALU.add))
                c.step(nc.vector.tensor_scalar(go[:, :], go[:, :], float(z.rows), None, ALU.min))
                for q in range(z.GC):
                    c.go(nc.vector.tensor_scalar(diag[:, q * P:(q + 1) * P], k["ident"][:, :], gb[:, q:q + 1], None, ALU.mult))
                    c.step(nc.vector.tensor_scalar(diag[:, (z.GC + q) * P:(z.GC + q + 1) * P], k["ident"][:, :],
                                                   go[:, q:q + 1], None, ALU.mult))
                dve.sem_inc(diag_done, 1)
                dve.wait_ge(spread, 1)
                c.go(nc.vector.tensor_copy(a["gblock"][:, :], pb[:, 0:z.NGS]))
                c.go(nc.vector.tensor_copy(a["gfirst"][:, :], po[0:1, 0:z.NGS]))
                c.step(nc.vector.tensor_copy(L["block"][:, :], pb[0:1, 0:z.NGS]))


def phase_positions(nc, s, z, k, a, tag):
    with ExitStack() as ctx:
        sb, ps, sem = scope(nc, ctx, k)
        NB1 = s.NB1
        lo1 = [sb(f"q_lo1_{u}" + tag, 4 * P, BF16) for u in range(2)]
        lo1T = [sb(f"q_lo1T_{u}" + tag, 4 * P) for u in range(2)]
        hi1 = [sb(f"q_hi1_{u}" + tag, 4 * NB1, BF16) for u in range(2)]
        krow = [sb(f"krow{u}" + tag, 4 * P) for u in range(2)]
        same = [sb(f"same{u}" + tag, 16 * P, BF16) for u in range(2)]
        rank = [sb(f"rank{u}" + tag, 4) for u in range(2)]
        sel, base = [sb(f"sel{u}" + tag, 4 * NB1) for u in range(2)], [sb(f"base{u}" + tag, 4) for u in range(2)]
        pos = [sb(f"pos{u}" + tag, 4, U32) for u in range(2)]
        rowp = [sb(f"rowp{u}" + tag, 16) for u in range(2)]
        snap = [sb(f"snap{u}" + tag, NB1) for u in range(2)]
        tail = sb("tail" + tag, GE * 4 // P)
        tail3 = tail[:, :].rearrange("p (j c) -> p j c", c=4)
        cnt = [ps(f"cnt{u}" + tag, NB1) for u in range(2)]
        tp = [ps(f"q_tp{u}" + tag, 4 * P, BF16) for u in range(2)]
        look = [ps(f"look{u}" + tag, 4 * NB1) for u in range(2)]
        names = ("krow_in", "oh_made", "oh_turned", "oh_copied", "looked", "counted", "summed", "pos_ready", "ranked")
        S = {n: [sem(f"{n}{u}") for u in range(2)] for n in names}
        S["scattered"] = [sem(f"scattered{u}" + tag, own=True) for u in range(2)]
        snapped, tail_set = sem("snapped"), sem("tail_set")
        scatter_go = sem("scatter_go")
        n = z.TT // 8
        with nc.Block() as block:
            @block.sync
            def _(sp):
                with sp.Fori(1, n + 2) as i:
                    for u in range(2):
                        sp.wait_ge(S["ranked"][u], i)
                        src = a["keyrow"][bass.ds((i - 1) * 8 * P + u * 4 * P, 4 * P)]
                        sp.dma_start(krow[u][:, :], src.rearrange("(o l) -> o l", o=1).broadcast_to([P, 4 * P])
                                     ).then_inc(S["krow_in"][u], 16)

            @block.vector
            def _(dve):
                def build(i, u):
                    t0 = (i - 1) * 8 + u * 4
                    dve.wait_ge(S["looked"][u], i)
                    for j in range(4):
                        nc.vector.tensor_scalar(lo1[u][:, j * P:(j + 1) * P], k["iota_f"][:, :],
                                                a["lo"][:, bass.ds(t0 + j, 1)], None, ALU.is_equal)
                    for j in range(4):
                        last = nc.vector.tensor_scalar(hi1[u][:, j * NB1:(j + 1) * NB1], k["iota_f"][:, 0:NB1],
                                                       a["hi"][:, bass.ds(t0 + j, 1)], None, ALU.is_equal)
                    last.then_inc(S["oh_made"][u], 1)
                    dve.wait_ge(S["krow_in"][u], i * 16)
                    for j in range(4):
                        last = nc.vector.scalar_tensor_tensor(
                            out=same[u][:, j * 4 * P:(j * 4 + j + 1) * P], in0=krow[u][:, 0:(j + 1) * P],
                            scalar=a["key"][:, bass.ds(t0 + j, 1)], in1=k["before"][:, (3 - j) * P:],
                            op0=ALU.is_equal, op1=ALU.mult, accum_out=rank[u][:, j:j + 1])
                    last.then_inc(S["ranked"][u], 1)

                def place(i, u):
                    t0 = (i - 1) * 8 + u * 4
                    dve.wait_ge(S["counted"][u], i)
                    dve.wait_ge(snapped, 2 * i - 1 + u)
                    nc.vector.tensor_tensor(snap[1 - u][:, :], snap[u][:, :], cnt[u][:, :], ALU.add).then_inc(snapped, 1)
                    dve.wait_ge(S["looked"][u], i + 1)
                    nc.vector.tensor_tensor(sel[u][:, :], look[u][:, :], hi1[u][:, :], ALU.mult).then_inc(S["summed"][u], 1)
                    dve.wait_ge(S["summed"][u], i * 3 - 2)
                    nc.vector.tensor_reduce(base[u][:, :], sel[u][:, :].rearrange("p (j b) -> p j b", j=4), AX, ALU.add
                                            ).then_inc(S["summed"][u], 1)
                    dve.wait_ge(S["summed"][u], i * 3 - 1)
                    dve.wait_ge(S["scattered"][u], (i - 1) * 64 + 16)
                    dve.wait_ge(S["ranked"][u], i + 1)
                    nc.vector.tensor_tensor(base[u][:, :], base[u][:, :], rank[u][:, :], ALU.add).then_inc(S["summed"][u], 1)
                    dve.wait_ge(S["summed"][u], i * 3)
                    nc.vector.tensor_copy(rowp[u][:, :], a["pay"][:, bass.ds(t0 * 4, 16)])
                    nc.vector.tensor_copy(pos[u][:, :], base[u][:, :]).then_inc(S["pos_ready"][u], 1)

                for u in range(2):
                    dve.sem_inc(S["ranked"][u], 1)
                    dve.sem_inc(S["looked"][u], 1)
                nc.vector.memset(tail[:, :], 0.0).then_inc(tail_set, 1)
                dve.wait_ge(tail_set, 1)
                nc.vector.memset(tail3[:, :, 0], FAR).then_inc(tail_set, 1)
                nc.vector.tensor_copy(snap[0][:, :], a["first"][:, :]).then_inc(snapped, 1)
                build(1, 0)
                build(1, 1)
                with dve.Fori(1, n + 1) as i:
                    for u in range(2):
                        place(i, u)
                        build(i + 1, u)

            @block.gpsimd
            def _(pool):
                pool.wait_ge(tail_set, 2)
                for u in range(2):
                    at = z.rows + u * GE // 2
                    nc.gpsimd.dma_start(a["rows"][at:at + GE // 2, :].rearrange("(p j) c -> p (j c)", p=P // 2),
                                        tail[0:P // 2, :]).then_inc(S["scattered"][u], 16)
                with pool.Fori(1, n + 1) as i:
                    for u in range(2):
                        pool.wait_ge(S["pos_ready"][u], i)
                        pool.sem_inc(scatter_go, 1)
                        for j in range(4):
                            nc.gpsimd.indirect_dma_start(a["rows"], bass.IndirectOffsetOnAxis(ap=pos[u][:, j:j + 1], axis=0),
                                                         rowp[u][:, j * 4:j * 4 + 4], None).then_inc(S["scattered"][u], 16)
                for u in range(2):
                    pool.wait_ge(S["scattered"][u], n * 64 + 16)

            @block.tensor
            def _(pe):
                def turn(i, u):
                    pe.wait_ge(S["oh_made"][u], i)
                    for j in range(4):
                        last = nc.tensor.transpose(tp[u][:, j * P:(j + 1) * P], lo1[u][:, j * P:(j + 1) * P], k["ident_b"][:, :])
                    last.then_inc(S["oh_turned"][u], 1)

                with pe.Fori(1, n + 1) as i:
                    for u in range(2):
                        turn(i, u)
                        for j in range(4):
                            last = nc.tensor.matmul(cnt[u][:, :], lo1[u][:, j * P:(j + 1) * P],
                                                    hi1[u][:, j * NB1:(j + 1) * NB1], start=(j == 0), stop=(j == 3))
                        last.then_inc(S["counted"][u], 1)
                        pe.wait_ge(S["oh_copied"][u], i)
                        pe.wait_ge(snapped, 2 * i - 1 + u)
                        for j in range(4):
                            last = nc.tensor.matmul(look[u][:, j * NB1:(j + 1) * NB1], lo1T[u][:, j * P:(j + 1) * P],
                                                    snap[u][:, :], start=True, stop=True)
                        last.then_inc(S["looked"][u], 1)

            @block.scalar
            def _(act):
                with act.Fori(1, n + 1) as i:
                    for u in range(2):
                        act.wait_ge(S["oh_turned"][u], i)
                        nc.scalar.copy(lo1T[u][:, :], tp[u][:, :]).then_inc(S["oh_copied"][u], 1)


def rounds_of(eng, L, z):
    return eng.value_load(L["rounds"][0:1, 0:1], min_val=1, max_val=z.NGS // U)


def phase_lists(nc, s, z, k, a, L, tag):
    with ExitStack() as ctx:
        sb, ps, sem = scope(nc, ctx, k)
        raw = sb("raw" + tag, z.NGS * 4 * G)
        base, vld, ofs = sb("lbase" + tag, z.NGS), sb("vld" + tag, z.NGS * G), sb("ofs" + tag, z.NGS * G)
        raw_clear, raw_in, step = sem("raw_clear"), sem("raw_in"), sem("list_step")
        r4 = raw[:, :].rearrange("p (g j c) -> p g j c", j=G, c=4)

        def pgj(t):
            return t[:, :].rearrange("p (g j) -> p g j", j=G)
        with nc.Block() as block:
            @block.sync
            def _(sp):
                sp.wait_ge(raw_clear, 1)
                n = rounds_of(sp, L, z)
                with sp.Fori(0, n * U) as g:
                    first = sp.value_load(a["gfirst"][0:1, bass.ds(g, 1)], min_val=0, max_val=z.rows)
                    sp.dma_start(raw[:, bass.ds(g * 16, 16)],
                                 a["rows"][bass.ds(first, GE), :].rearrange("(p j) c -> p (j c)", p=P)).then_inc(raw_in, 16)
                sp.wait_ge(raw_in, n * (16 * U))
                sp.sem_inc(raw_clear, 1)

            @block.vector
            def _(dve):
                c = Chain(dve, step)
                nc.vector.memset(raw[:, :], 0.0).then_inc(raw_clear, 1)
                c.step(nc.vector.tensor_scalar(base[:, :], a["gblock"][:, :], float(P), None, ALU.mult))
                dve.wait_ge(raw_clear, 2)
                c.step(nc.vector.tensor_tensor(pgj(L["place"]), r4[:, :, :, 0], base[:, :].unsqueeze(2).broadcast_to([P, z.NGS, G]),
                                               ALU.subtract))
                c.step(nc.vector.tensor_scalar(vld[:, :], L["place"][:, :], 0.0, None, ALU.is_ge))
                c.step(nc.vector.scalar_tensor_tensor(out=vld[:, :], in0=L["place"][:, :], scalar=float(P), in1=vld[:, :],
                                                      op0=ALU.is_lt, op1=ALU.mult))
                c.step(nc.vector.tensor_scalar(pgj(ofs), r4[:, :, :, 1], -float(s.ZROW), None, ALU.add))
                c.step(nc.vector.tensor_tensor(ofs[:, :], ofs[:, :], vld[:, :], ALU.mult))
                c.step(nc.vector.tensor_scalar(ofs[:, :], ofs[:, :], float(s.ZROW), None, ALU.add))
                c.step(nc.vector.tensor_copy(L["gather"][:, :], ofs[:, :]))
                if "weight" in L:
                    c.step(nc.vector.tensor_copy(pgj(L["weight"]), r4[:, :, :, 2]))
                if "segment" in L:
                    c.step(nc.vector.tensor_tensor(pgj(ofs), r4[:, :, :, 0], pgj(vld), ALU.mult))
                    c.step(nc.vector.tensor_tensor(ofs[:, :], ofs[:, :], vld[:, :], ALU.add))
                    c.step(nc.vector.tensor_scalar(L["segment"][:, :], ofs[:, :], -1.0, None, ALU.add))


def sort_edges(nc, s, z, k, L, key_in, other_in, weight_in, tag):
    with ExitStack() as ctx:
        def sb(name, cols, dt=F32, parts=P):
            return ctx.enter_context(nc.sbuf_tensor(name + tag, [parts, cols], dt))
        W = z.C * P
        a = dict(counts=L["counts"], first=sb("first", s.NB1), gblock=sb("gblock", z.NGS), gfirst=sb("gfirst", z.NGS, I32, 1),
                 rows=nc.dram_tensor("rows" + tag, [z.rows + GE, 4], F32).ap(),
                 keyrow=nc.dram_tensor("keyrow" + tag, [W * P + 8 * P], F32).ap())
        with ExitStack() as c2:
            for name, cols in (("key", W + 8), ("hi", W + 8), ("lo", W + 8), ("pay", W * 4)):
                a[name] = c2.enter_context(nc.sbuf_tensor(name + tag, [P, cols], F32))
            phase_sort_input(nc, s, z, k, a, key_in, other_in, weight_in, tag)
            phase_histogram(nc, s, z, k, a, tag)
            phase_offsets(nc, s, z, k, a, L, tag)
            phase_positions(nc, s, z, k, a, tag)
        phase_lists(nc, s, z, k, a, L, tag)


def phase_load(nc, k, loads, name):
    with ExitStack() as ctx:
        sb, ps, sem = scope(nc, ctx, k)
        loaded = sem("small_loaded")
        with nc.Block() as block:
            @block.sync
            def _(sp):
                for dst, src in loads:
                    sp.dma_start(dst, src).then_inc(loaded, 16)
                sp.wait_ge(loaded, 16 * len(loads))


def phase_dense(nc, s, k, src, weights, bias, outs, tag, blocks_out=True):
    F = weights.shape[1]
    with ExitStack() as ctx:
        sb, ps, sem = scope(nc, ctx, k)
        xb = [sb(f"d_xb{u}" + tag, D) for u in range(2)]
        xT = [sb(f"d_xT{u}" + tag, D) for u in range(2)]
        tps = [ps(f"d_tps{u}" + tag, P) for u in range(2)]
        ops = [ps(f"d_ops{u}" + tag, F) for u in range(2)]
        S = {n: [sem(f"d_{n}{u}") for u in range(2)] for n in ("copied", "turned", "xT_ready", "product", "evacuated")}
        n = s.NB1 // 2
        with nc.Block() as block:
            @block.vector
            def _(dve):
                for u in range(2):
                    dve.sem_inc(S["turned"][u], 1)
                    dve.sem_inc(S["product"][u], 1)
                with dve.Fori(1, n + 1) as i:
                    for u in range(2):
                        dve.wait_ge(S["turned"][u], i)
                        nc.vector.tensor_copy(xb[u][:, :], src[:, bass.ds(((i - 1) * 2 + u) * D, D)]).then_inc(S["copied"][u], 1)
                    for u in range(2):
                        dve.wait_ge(S["turned"][u], i + 1)
                        dve.wait_ge(S["product"][u], i)
                        nc.vector.tensor_copy(xT[u][:, :], tps[u][:, :]).then_inc(S["xT_ready"][u], 1)

            @block.tensor
            def _(pe):
                with pe.Fori(1, n + 1) as i:
                    for u in range(2):
                        pe.wait_ge(S["copied"][u], i)
                        nc.tensor.transpose(tps[u][:, :], xb[u][:, :], k["ident"][:, :]).then_inc(S["turned"][u], 1)
                    for u in range(2):
                        pe.wait_ge(S["xT_ready"][u], i)
                        pe.wait_ge(S["evacuated"][u], i)
                        last = nc.tensor.matmul(ops[u][:, :], xT[u][:, :], weights[:, :], start=True, stop=bias is None)
                        if bias is not None:
                            last = nc.tensor.matmul(ops[u][:, :], k["ones"][0:1, :], bias[0:1, :], start=False, stop=True)
                        last.then_inc(S["product"][u], 1)

            @block.scalar
            def _(act):
                for u in range(2):
                    act.sem_inc(S["evacuated"][u], 1)
                with act.Fori(1, n + 1) as i:
                    for u in range(2):
                        act.wait_ge(S["product"][u], i + 1)
                        for c0, c1, func, dest in outs:
                            last = nc.scalar.activation(dest((i - 1) * 2 + u), ops[u][:, c0:c1], func)
                        last.then_inc(S["evacuated"][u], 1)


def phase_split(nc, s, k, src, parts, tag):
    with ExitStack() as ctx:
        sb, ps, sem = scope(nc, ctx, k)
        step = sem("split_step")
        with nc.Block() as block:
            @block.vector
            def _(dve):
                c = Chain(dve, step)
                for n, part in enumerate(parts):
                    c.step(nc.vector.tensor_copy(part[:, :], src[:, :]))
                    if n < 2:
                        c.step(nc.vector.tensor_tensor(src[:, :], src[:, :], part[:, :], ALU.subtract))


def store_table(sp, table, tile, F, sem):
    sp.dma_start(table.rearrange("(b p) f -> p b f", p=P), tile[:, :].rearrange("p (b f) -> p b f", f=F)).then_inc(sem, 16)


def phase_store(nc, k, pairs):
    with ExitStack() as ctx:
        sb, ps, sem = scope(nc, ctx, k)
        stored = sem("table_stored")
        with nc.Block() as block:
            @block.sync
            def _(sp):
                for table, tile, F in pairs:
                    store_table(sp, table, tile, F, stored)
                sp.wait_ge(stored, 16 * len(pairs))


def over_blocks(row, s):
    return row.unsqueeze(1).broadcast_to([P, s.NB1, row.shape[1]])


def blocks(t, f=D):
    return t[:, :].rearrange("p (b f) -> p b f", f=f)


def phase_layernorm(nc, s, k, y, tag):
    with ExitStack() as ctx:
        sb, ps, sem = scope(nc, ctx, k)
        sq, m, sd, rs = sb("ln_sq" + tag, s.NB1 * D), sb("ln_m" + tag, s.NB1), sb("ln_sd" + tag, s.NB1), sb("ln_rs" + tag, s.NB1)
        step, centred, squared, var_ready, sd_ready = sem("ln_step"), sem("ln_centred"), sem("ln_squared"), sem("ln_var"), sem("ln_sd")
        with nc.Block() as block:
            @block.vector
            def _(dve):
                c = Chain(dve, step)
                c.step(nc.vector.tensor_reduce(m[:, :], blocks(y), AX, ALU.add))
                c.step(nc.vector.tensor_scalar(m[:, :], m[:, :], 1.0 / D, None, ALU.mult))
                nc.vector.tensor_tensor(blocks(y), blocks(y), m[:, :].unsqueeze(2).broadcast_to([P, s.NB1, D]),
                                        ALU.subtract).then_inc(centred, 1)
                dve.wait_ge(squared, 1)
                c.step(nc.vector.tensor_reduce(m[:, :], blocks(sq), AX, ALU.add))
                nc.vector.tensor_scalar(m[:, :], m[:, :], 1.0 / D, EPS, ALU.mult, ALU.add).then_inc(var_ready, 1)
                dve.wait_ge(sd_ready, 1)
                c.step(nc.vector.reciprocal(rs[:, :], sd[:, :]))
                c.step(nc.vector.tensor_tensor(blocks(k["x"]), blocks(y), rs[:, :].unsqueeze(2).broadcast_to([P, s.NB1, D]), ALU.mult))
                c.step(nc.vector.memset(k["x"][:, s.NB * D:], 0.0))

            @block.scalar
            def _(act):
                act.wait_ge(centred, 1)
                nc.scalar.activation(sq[:, :], y[:, :], ACT.Square).then_inc(squared, 1)
                act.wait_ge(var_ready, 1)
                nc.scalar.activation(sd[:, :], m[:, :], ACT.Sqrt).then_inc(sd_ready, 1)


def phase_scores(nc, s, z, k, L, Q, att, table, v_dram, att_dram):
    with ExitStack() as ctx:
        sb, ps, sem = scope(nc, ctx, k)
        R = range(U)
        kv = [sb(f"kv{u}", G * 2 * D) for u in R]
        vs = [sb(f"vs{u}", G * D) for u in R]
        oh = [sb(f"s_oh{u}", G * P, BF16) for u in R]
        ohT = [sb(f"s_ohT{u}", G * P, BF16) for u in R]
        idx = [sb(f"s_idx{u}", G, U32) for u in R]
        prod = [sb(f"prod{u}", G * D) for u in R]
        tps = [ps(f"s_tps{u}", G * P, BF16) for u in range(2)]
        qps = [ps(f"qps{u}", G * D) for u in R]
        landed = [sem(f"kv_landed{u}", own=True) for u in R]
        S = {n: [sem(f"s_{n}{u}") for u in R] for n in
             ("idx_set", "oh_made", "oh_turned", "oh_copied", "q_ready", "prod_made", "att_made", "v_copied", "v_free", "stored")}
        go, cleared, zeroed = sem("s_go"), sem("s_cleared"), sem("s_zeroed")
        with nc.Block() as block:
            @block.gpsimd
            def _(pool):
                n = rounds_of(pool, L, z)
                with pool.Fori(1, n + 1) as i:
                    for u in R:
                        pool.wait_ge(S["prod_made"][u], i)
                        pool.wait_ge(S["v_copied"][u], i)
                        pool.sem_inc(go, 1)
                        nc.gpsimd.tensor_copy(idx[u][:, :], L["gather"][:, bass.ds(((i - 1) * U + u) * G, G)]).then_inc(S["idx_set"][u], 1)
                        pool.wait_ge(S["idx_set"][u], i)
                        pool.sem_inc(go, 1)
                        for j in range(G):
                            nc.gpsimd.indirect_dma_start(kv[u][:, j * 2 * D:(j + 1) * 2 * D], None, table,
                                                         bass.IndirectOffsetOnAxis(ap=idx[u][:, j:j + 1], axis=0)).then_inc(landed[u], 16)

            @block.vector
            def _(dve):
                nc.vector.memset(att[:, :], 0.0).then_inc(cleared, 1)
                dve.wait_ge(cleared, 1)
                n = rounds_of(dve, L, z)
                for u in R:
                    dve.sem_inc(S["prod_made"][u], 1)
                    dve.sem_inc(S["oh_turned"][u], 1)
                    dve.sem_inc(S["att_made"][u], 1)
                dve.wait_ge(zeroed, 16)
                with dve.Fori(1, n + 1) as i:
                    for u in R:
                        g = (i - 1) * U + u
                        dve.wait_ge(S["oh_turned"][u], i)
                        for j in range(G):
                            last = nc.vector.tensor_scalar(oh[u][:, j * P:(j + 1) * P], k["iota_f"][:, :],
                                                           L["place"][:, bass.ds(g * G + j, 1)], None, ALU.is_equal)
                        last.then_inc(S["oh_made"][u], 1)
                    for u in R:
                        g = (i - 1) * U + u
                        dve.wait_ge(S["q_ready"][u], i)
                        dve.wait_ge(landed[u], i * 16 * G)
                        dve.wait_ge(S["att_made"][u], i)
                        kk = kv[u][:, :].rearrange("p (j c) -> p j c", j=G)[:, :, 0:D]
                        nc.vector.tensor_tensor(prod[u][:, :].rearrange("p (j c) -> p j c", j=G),
                                                qps[u][:, :].rearrange("p (j c) -> p j c", j=G), kk, ALU.mult
                                                ).then_inc(S["prod_made"][u], 1)
                        dve.wait_ge(S["prod_made"][u], i + 1)
                        nc.vector.tensor_reduce(att[:, bass.ds(g * G * H, G * H)],
                                                prod[u][:, :].rearrange("p (m d) -> p m d", d=HD), AX, ALU.add
                                                ).then_inc(S["att_made"][u], 1)

            @block.tensor
            def _(pe):
                n = rounds_of(pe, L, z)
                with pe.Fori(1, n + 1) as i:
                    for u in R:
                        pe.wait_ge(S["oh_made"][u], i)
                        if u >= 2:
                            pe.wait_ge(S["oh_copied"][u - 2], i)
                        for j in range(G):
                            last = nc.tensor.transpose(tps[u % 2][:, j * P:(j + 1) * P], oh[u][:, j * P:(j + 1) * P], k["ident_b"][:, :])
                        last.then_inc(S["oh_turned"][u], 1)
                    for u in R:
                        b = pe.value_load(L["block"][0:1, bass.ds((i - 1) * U + u, 1)], min_val=0, max_val=s.NB)
                        pe.wait_ge(S["oh_copied"][u], i)
                        pe.wait_ge(S["prod_made"][u], i)
                        for j in range(G):
                            for q in range(3):
                                last = nc.tensor.matmul(qps[u][:, j * D:(j + 1) * D], ohT[u][:, j * P:(j + 1) * P],
                                                        Q[q][:, bass.ds(b * D, D)], start=(q == 0), stop=(q == 2))
                        last.then_inc(S["q_ready"][u], 1)

            @block.scalar
            def _(act):
                n = rounds_of(act, L, z)
                for u in R:
                    act.sem_inc(S["v_copied"][u], 1)
                with act.Fori(1, n + 1) as i:
                    for u in R:
                        act.wait_ge(S["oh_turned"][u], i + 1)
                        nc.scalar.copy(ohT[u][:, :], tps[u % 2][:, :]).then_inc(S["oh_copied"][u], 1)
                    for u in R:
                        act.wait_ge(landed[u], i * 16 * G)
                        act.wait_ge(S["v_free"][u], i)
                        nc.scalar.copy(vs[u][:, :].rearrange("p (j c) -> p j c", j=G),
                                       kv[u][:, :].rearrange("p (j c) -> p j c", j=G)[:, :, D:]).then_inc(S["v_copied"][u], 1)

            @block.sync
            def _(sp):
                sp.wait_ge(cleared, 1)
                sp.dma_start(att_dram[z.GMIN * P:, :].rearrange("(g p) c -> p g c", p=P),
                             att[:, z.GMIN * G * H:].rearrange("p (g c) -> p g c", c=G * H)).then_inc(zeroed, 16)
                sp.wait_ge(zeroed, 16)
                n = rounds_of(sp, L, z)
                for u in R:
                    sp.sem_inc(S["v_free"][u], 1)
                with sp.Fori(1, n + 1) as i:
                    for u in R:
                        g = (i - 1) * U + u
                        sp.wait_ge(S["v_copied"][u], i + 1)
                        sp.dma_start(v_dram[bass.ds(g * P, P), :], vs[u][:, :]).then_inc(S["stored"][u], 16)
                        sp.wait_ge(S["att_made"][u], i + 1)
                        sp.dma_start(att_dram[bass.ds(g * P, P), :], att[:, bass.ds(g * G * H, G * H)]).then_inc(S["stored"][u], 16)
                    for u in R:
                        sp.wait_ge(S["stored"][u], i * 32)
                        sp.sem_inc(S["v_free"][u], 1)


def phase_softmax(nc, s, z, k, L, att, seg_dram, att_dram, ex_dram):
    S_ = z.NGS * G
    with ExitStack() as ctx:
        sb, ps, sem = scope(nc, ctx, k)
        seg, prv, nxt = sb("seg", S_), sb("prv", S_), sb("nxt", S_)
        same = [prv, nxt]
        run = [sb("run_f", S_), sb("run_b", S_)]
        ends, whole = sb("ends", 2 * H), sb("whole", 2 * H)
        endT, wholeT, carT = sb("endT", P, F32, 2 * H), sb("wholeT", P, F32, 2 * H), sb("carT", P + 2, F32, 2 * H)
        car, least = sb("car", 2 * H), sb("least", 2)
        lead = sb("lead", 8, F32, 1)
        tp = ps("car_tp", 4 * P)
        seg_out, in_, step, pe1, out_, ready, pe2 = (sem(x) for x in ("seg_out", "sm_in", "sm_step", "sm_pe", "sm_out", "sm_ready", "sm_pe2"))
        row_done = sem("sm_row_done")
        a3 = att[:, :].rearrange("p (m h) -> p m h", h=H)
        n_all = P * S_
        with nc.Block() as block:
            @block.sync
            def _(sp):
                sp.dma_start(seg_dram[8:8 + n_all].rearrange("(g p j) -> p g j", p=P, j=G),
                             L["segment"][:, :].rearrange("p (g j) -> p g j", j=G)).then_inc(seg_out, 16)
                sp.wait_ge(ready, 1)
                sp.dma_start(seg_dram[0:8].rearrange("(o c) -> o c", o=1), lead[:, :]).then_inc(seg_out, 16)
                sp.dma_start(seg_dram[8 + n_all:16 + n_all].rearrange("(o c) -> o c", o=1), lead[:, :]).then_inc(seg_out, 16)
                sp.wait_ge(seg_out, 48)
                for t, at in ((seg, 8), (prv, 7), (nxt, 9)):
                    sp.dma_start(t[:, :], seg_dram[at:at + n_all].rearrange("(p m) -> p m", p=P)).then_inc(in_, 16)
                sp.dma_start(att[:, :], att_dram.rearrange("(p m) c -> p (m c)", p=P)).then_inc(in_, 16)
                sp.wait_ge(out_, H)
                sp.dma_start(ex_dram.rearrange("(p m) c -> p (m c)", p=P), att[:, :]).then_inc(seg_out, 16)
                sp.wait_ge(seg_out, 64)
                sp.dma_start(att[:, :].rearrange("p (g c) -> p g c", c=G * H),
                             ex_dram.rearrange("(g p) c -> p g c", p=P)).then_inc(seg_out, 16)
                sp.wait_ge(seg_out, 80)

            @block.vector
            def _(dve):
                c = Chain(dve, step)
                nc.vector.memset(lead[:, :], -2.0).then_inc(ready, 1)
                c.go(nc.vector.memset(carT[:, :], 0.0))
                dve.wait_ge(in_, 64)
                for t in same:
                    c.step(nc.vector.tensor_tensor(t[:, :], t[:, :], seg[:, :], ALU.is_equal))

                def scan(d, h, init):
                    sl = slice(None) if d == 0 else slice(None, None, -1)
                    return nc.vector.tensor_tensor_scan(run[d][:, sl], same[d][:, sl], a3[:, sl, h], init, ALU.mult, ALU.max)
                for d in range(2):
                    c.step(nc.vector.tensor_reduce(least[:, d:d + 1], same[d][:, :], AX, ALU.min))
                    c.step(nc.vector.tensor_copy(whole[:, d * H:(d + 1) * H], least[:, d:d + 1].broadcast_to([P, H])))
                    for h in range(H):
                        c.step(scan(d, h, 0.0))
                        end = run[d][:, S_ - 1:S_] if d == 0 else run[d][:, 0:1]
                        c.step(nc.vector.tensor_copy(ends[:, d * H + h:d * H + h + 1], end))
                dve.sem_inc(pe1, 1)
                dve.wait_ge(pe2, 1)
                for d in range(2):
                    c.step(nc.vector.tensor_copy(endT[0:H, :], tp[0:H, d * P:(d + 1) * P]))
                    c.step(nc.vector.tensor_copy(wholeT[0:H, :], tp[0:H, (2 + d) * P:(3 + d) * P]))
                    if d == 0:
                        c.step(nc.vector.tensor_tensor_scan(carT[0:H, 1:P + 1], wholeT[0:H, :], endT[0:H, :], 0.0, ALU.mult, ALU.max))
                    else:
                        c.step(nc.vector.tensor_tensor_scan(carT[0:H, P:0:-1], wholeT[0:H, ::-1], endT[0:H, ::-1], 0.0, ALU.mult, ALU.max))
                        c.step(nc.vector.memset(carT[0:H, P + 1:P + 2], 0.0))
                    dve.sem_inc(pe1, 1)
                    dve.wait_ge(pe2, 2 + d)
                    c.step(nc.vector.tensor_copy(car[:, d * H:(d + 1) * H], tp[:, 0:H]))
                    if d == 0:
                        pass
                for h in range(H):
                    for d in range(2):
                        c.step(scan(d, h, car[:, d * H + h:d * H + h + 1]))
                    c.step(nc.vector.tensor_tensor(run[0][:, :], run[0][:, :], run[1][:, :], ALU.max))
                    c.n += 1
                    nc.vector.tensor_tensor(a3[:, :, h], a3[:, :, h], run[0][:, :], ALU.subtract).then_inc(step, 1)
                    dve.wait_ge(step, c.n)
                    dve.sem_inc(row_done, 1)

            @block.tensor
            def _(pe):
                pe.wait_ge(pe1, 1)
                for d in range(2):
                    nc.tensor.transpose(tp[0:H, d * P:(d + 1) * P], ends[:, d * H:(d + 1) * H], k["ident"][:, :])
                    last = nc.tensor.transpose(tp[0:H, (2 + d) * P:(3 + d) * P], whole[:, d * H:(d + 1) * H], k["ident"][:, :])
                last.then_inc(pe2, 1)
                for d in range(2):
                    pe.wait_ge(pe1, 2 + d)
                    nc.tensor.transpose(tp[:, 0:H], carT[0:H, 0:P] if d == 0 else carT[0:H, 2:P + 2],
                                        k["ident"][0:H, 0:H]).then_inc(pe2, 1)

            @block.scalar
            def _(act):
                for h in range(H):
                    act.wait_ge(row_done, h + 1)
                    nc.scalar.activation(a3[:, :, h], a3[:, :, h], ACT.Exp).then_inc(out_, 1)


def phase_messages(nc, s, z, k, L, ex, acc, v_dram):
    M = D + H
    with ExitStack() as ctx:
        sb, ps, sem = scope(nc, ctx, k)
        R = range(U)
        vin = [sb(f"m_v{u}", G * D) for u in R]
        oh = [sb(f"m_oh{u}", G * P) for u in R]
        msg = [sb(f"msg{u}", G * M) for u in R]
        sps = [ps(f"m_ps{u}", M) for u in R]
        S = {n: [sem(f"m_{n}{u}") for u in R] for n in ("v_in", "oh_made", "msg_made", "ex_made", "summed", "added")}
        cleared, chain = sem("m_cleared"), sem("m_chain")
        with nc.Block() as block:
            @block.sync
            def _(sp):
                n = rounds_of(sp, L, z)
                with sp.Fori(1, n + 1) as i:
                    for u in R:
                        sp.wait_ge(S["msg_made"][u], i)
                        sp.dma_start(vin[u][:, :], v_dram[bass.ds(((i - 1) * U + u) * P, P), :]).then_inc(S["v_in"][u], 16)

            @block.vector
            def _(dve):
                nc.vector.memset(acc[:, :], 0.0).then_inc(cleared, 1)
                dve.wait_ge(cleared, 1)
                nc.vector.memset(acc[:, :].rearrange("p (b c) -> p b c", c=M)[:, s.NB:, D:], 1.0).then_inc(chain, 1)
                n = rounds_of(dve, L, z)
                for u in R:
                    dve.sem_inc(S["msg_made"][u], 1)
                    dve.sem_inc(S["summed"][u], 1)
                with dve.Fori(1, n + 1) as i:
                    for u in R:
                        g = (i - 1) * U + u
                        dve.wait_ge(S["summed"][u], i)
                        for j in range(G):
                            last = nc.vector.tensor_scalar(oh[u][:, j * P:(j + 1) * P], k["iota_f"][:, :],
                                                           L["place"][:, bass.ds(g * G + j, 1)], None, ALU.is_equal)
                        last.then_inc(S["oh_made"][u], 1)
                        dve.wait_ge(S["v_in"][u], i * 16)
                        nc.vector.tensor_tensor(
                            msg[u][:, :].rearrange("p (j c) -> p j c", j=G)[:, :, 0:D].rearrange("p j (h d) -> p j h d", h=H),
                            vin[u][:, :].rearrange("p (j h d) -> p j h d", j=G, h=H),
                            ex[:, bass.ds(g * G * H, G * H)].rearrange("p (j h) -> p j h", j=G).unsqueeze(3).broadcast_to([P, G, H, HD]),
                            ALU.mult).then_inc(S["msg_made"][u], 1)
                    for u in R:
                        b = dve.value_load(L["block"][0:1, bass.ds((i - 1) * U + u, 1)], min_val=0, max_val=s.NB)
                        dve.wait_ge(S["summed"][u], i + 1)
                        dve.wait_ge(chain, (i - 1) * U + u + 1)
                        nc.vector.tensor_tensor(acc[:, bass.ds(b * M, M)], acc[:, bass.ds(b * M, M)], sps[u][:, :], ALU.add
                                                ).then_inc(chain, 1)

            @block.scalar
            def _(act):
                n = rounds_of(act, L, z)
                with act.Fori(1, n + 1) as i:
                    for u in R:
                        act.wait_ge(S["summed"][u], i)
                        nc.scalar.copy(msg[u][:, :].rearrange("p (j c) -> p j c", j=G)[:, :, D:],
                                       ex[:, bass.ds(((i - 1) * U + u) * G * H, G * H)].rearrange("p (j h) -> p j h", j=G)
                                       ).then_inc(S["ex_made"][u], 1)

            @block.tensor
            def _(pe):
                n = rounds_of(pe, L, z)
                with pe.Fori(1, n + 1) as i:
                    for u in R:
                        pe.wait_ge(S["msg_made"][u], i + 1)
                        pe.wait_ge(S["ex_made"][u], i)
                        for j in range(G):
                            last = nc.tensor.matmul(sps[u][:, :], oh[u][:, j * P:(j + 1) * P], msg[u][:, j * M:(j + 1) * M],
                                                    start=(j == 0), stop=(j == G - 1))
                        last.then_inc(S["summed"][u], 1)


def phase_attention_out(nc, s, k, acc, bias):
    M = D + H
    with ExitStack() as ctx:
        sb, ps, sem = scope(nc, ctx, k)
        den, y = sb("den", s.NB1 * H), sb("y0", s.NB1 * D)
        step = sem("ao_step")
        a3 = acc[:, :].rearrange("p (b c) -> p b c", c=M)
        with nc.Block() as block:
            @block.vector
            def _(dve):
                c = Chain(dve, step)
                c.step(nc.vector.reciprocal(den[:, :].rearrange("p (b h) -> p b h", h=H), a3[:, :, D:]))
                for h in range(H):
                    c.go(nc.vector.tensor_tensor(blocks(y)[:, :, h * HD:(h + 1) * HD], a3[:, :, h * HD:(h + 1) * HD],
                                                 den[:, :].rearrange("p (b h) -> p b h", h=H)[:, :, h:h + 1].broadcast_to([P, s.NB1, HD]),
                                                 ALU.mult))
                dve.wait_ge(step, c.n)
                c.step(nc.vector.tensor_tensor(blocks(y), blocks(y), over_blocks(bias[:, :], s), ALU.add))
                c.step(nc.vector.tensor_tensor(y[:, :], y[:, :], k["x"][:, :], ALU.add))
        phase_layernorm(nc, s, k, y, "0")


def phase_gather_sum(nc, s, z, k, L, table, acc, weighted, tag):
    with ExitStack() as ctx:
        sb, ps, sem = scope(nc, ctx, k)
        R = range(U)
        row = [sb(f"g_row{u}" + tag, G * D) for u in R]
        oh = [sb(f"g_oh{u}" + tag, G * P) for u in R]
        idx = [sb(f"g_idx{u}" + tag, G, U32) for u in R]
        sps = [ps(f"g_ps{u}" + tag, D) for u in R]
        landed = [sem(f"row_landed{u}" + tag, own=True) for u in R]
        S = {n: [sem(f"g_{n}{u}") for u in R] for n in ("idx_set", "oh_made", "summed", "added")}
        cleared, chain, go = sem("g_cleared"), sem("g_chain"), sem("g_go")
        with nc.Block() as block:
            @block.gpsimd
            def _(pool):
                n = rounds_of(pool, L, z)
                with pool.Fori(1, n + 1) as i:
                    for u in R:
                        pool.wait_ge(S["summed"][u], i)
                        pool.sem_inc(go, 1)
                        nc.gpsimd.tensor_copy(idx[u][:, :], L["gather"][:, bass.ds(((i - 1) * U + u) * G, G)]).then_inc(S["idx_set"][u], 1)
                        pool.wait_ge(S["idx_set"][u], i)
                        pool.sem_inc(go, 1)
                        for j in range(G):
                            nc.gpsimd.indirect_dma_start(row[u][:, j * D:(j + 1) * D], None, table,
                                                         bass.IndirectOffsetOnAxis(ap=idx[u][:, j:j + 1], axis=0)).then_inc(landed[u], 16)

            @block.vector
            def _(dve):
                nc.vector.memset(acc[:, :], 0.0).then_inc(chain, 1)
                n = rounds_of(dve, L, z)
                for u in R:
                    dve.sem_inc(S["summed"][u], 1)
                with dve.Fori(1, n + 1) as i:
                    for u in R:
                        g = (i - 1) * U + u
                        dve.wait_ge(S["summed"][u], i)
                        for j in range(G):
                            place = L["place"][:, bass.ds(g * G + j, 1)]
                            if weighted:
                                last = nc.vector.tensor_scalar(oh[u][:, j * P:(j + 1) * P], k["iota_f"][:, :], place,
                                                               L["weight"][:, bass.ds(g * G + j, 1)], ALU.is_equal, ALU.mult)
                            else:
                                last = nc.vector.tensor_scalar(oh[u][:, j * P:(j + 1) * P], k["iota_f"][:, :], place, None, ALU.is_equal)
                        last.then_inc(S["oh_made"][u], 1)
                    for u in R:
                        b = dve.value_load(L["block"][0:1, bass.ds((i - 1) * U + u, 1)], min_val=0, max_val=s.NB)
                        dve.wait_ge(S["summed"][u], i + 1)
                        dve.wait_ge(chain, (i - 1) * U + u + 1)
                        nc.vector.tensor_tensor(acc[:, bass.ds(b * D, D)], acc[:, bass.ds(b * D, D)], sps[u][:, :], ALU.add
                                                ).then_inc(chain, 1)

            @block.tensor
            def _(pe):
                n = rounds_of(pe, L, z)
                with pe.Fori(1, n + 1) as i:
                    for u in R:
                        pe.wait_ge(S["oh_made"][u], i)
                        pe.wait_ge(landed[u], i * 16 * G)
                        for j in range(G):
                            last = nc.tensor.matmul(sps[u][:, :], oh[u][:, j * P:(j + 1) * P], row[u][:, j * D:(j + 1) * D],
                                                    start=(j == 0), stop=(j == G - 1))
                        last.then_inc(S["summed"][u], 1)


def phase_edge_sums(nc, s, z, k, L, Pn, table, e_dram, stats):
    with ExitStack() as ctx:
        sb, ps, sem = scope(nc, ctx, k)
        R = range(U)
        row = [sb(f"e_row{u}", G * D) for u in R]
        oh = [sb(f"e_oh{u}", G * P, BF16) for u in R]
        ohT = [sb(f"e_ohT{u}", G * P, BF16) for u in R]
        idx = [sb(f"e_idx{u}", G, U32) for u in R]
        es = [sb(f"e_s{u}", GE) for u in R]
        tps = [ps(f"e_tps{u}", G * P, BF16) for u in range(2)]
        eps = [ps(f"e_ps{u}", GE) for u in R]
        landed = [sem(f"r_landed{u}", own=True) for u in R]
        S = {n: [sem(f"e_{n}{u}") for u in R] for n in
             ("idx_set", "oh_made", "oh_turned", "oh_copied", "e_made", "e_copied", "e_free", "stored", "stat")}
        go, cleared = sem("e_go"), sem("e_cleared")
        with nc.Block() as block:
            @block.gpsimd
            def _(pool):
                n = rounds_of(pool, L, z)
                with pool.Fori(1, n + 1) as i:
                    for u in R:
                        pool.wait_ge(S["e_made"][u], i)
                        pool.sem_inc(go, 1)
                        nc.gpsimd.tensor_copy(idx[u][:, :], L["gather"][:, bass.ds(((i - 1) * U + u) * G, G)]).then_inc(S["idx_set"][u], 1)
                        pool.wait_ge(S["idx_set"][u], i)
                        pool.sem_inc(go, 1)
                        for j in range(G):
                            nc.gpsimd.indirect_dma_start(row[u][:, j * D:(j + 1) * D], None, table,
                                                         bass.IndirectOffsetOnAxis(ap=idx[u][:, j:j + 1], axis=0)).then_inc(landed[u], 16)

            @block.vector
            def _(dve):
                nc.vector.memset(stats[:, :], 0.0).then_inc(cleared, 1)
                dve.wait_ge(cleared, 1)
                n = rounds_of(dve, L, z)
                for u in R:
                    dve.sem_inc(S["oh_turned"][u], 1)
                    dve.sem_inc(S["stat"][u], 1)
                with dve.Fori(1, n + 1) as i:
                    for u in R:
                        g = (i - 1) * U + u
                        dve.wait_ge(S["oh_turned"][u], i)
                        for j in range(G):
                            last = nc.vector.tensor_scalar(oh[u][:, j * P:(j + 1) * P], k["iota_f"][:, :],
                                                           L["place"][:, bass.ds(g * G + j, 1)], None, ALU.is_equal)
                        last.then_inc(S["oh_made"][u], 1)
                    for u in R:
                        dve.wait_ge(S["e_copied"][u], i)
                        nc.vector.bn_stats(stats[:, bass.ds(((i - 1) * U + u) * 6, 6)], es[u][:, :]).then_inc(S["stat"][u], 1)

            @block.tensor
            def _(pe):
                n = rounds_of(pe, L, z)
                for u in R:
                    pe.sem_inc(S["e_made"][u], 1)
                with pe.Fori(1, n + 1) as i:
                    for u in R:
                        pe.wait_ge(S["oh_made"][u], i)
                        if u >= 2:
                            pe.wait_ge(S["oh_copied"][u - 2], i)
                        for j in range(G):
                            last = nc.tensor.transpose(tps[u % 2][:, j * P:(j + 1) * P], oh[u][:, j * P:(j + 1) * P], k["ident_b"][:, :])
                        last.then_inc(S["oh_turned"][u], 1)
                    for u in R:
                        b = pe.value_load(L["block"][0:1, bass.ds((i - 1) * U + u, 1)], min_val=0, max_val=s.NB)
                        pe.wait_ge(S["oh_copied"][u], i)
                        pe.wait_ge(landed[u], i * 16 * G)
                        pe.wait_ge(S["e_free"][u], i)
                        for j in range(G):
                            nc.tensor.matmul(eps[u][:, j * P:(j + 1) * P], row[u][:, j * D:(j + 1) * D], k["ident"][:, :],
                                             start=True, stop=False)
                            for q in range(3):
                                last = nc.tensor.matmul(eps[u][:, j * P:(j + 1) * P], Pn[q][:, bass.ds(b * D, D)],
                                                        ohT[u][:, j * P:(j + 1) * P], start=False, stop=(q == 2))
                        last.then_inc(S["e_made"][u], 1)

            @block.scalar
            def _(act):
                n = rounds_of(act, L, z)
                for u in R:
                    act.sem_inc(S["e_free"][u], 1)
                with act.Fori(1, n + 1) as i:
                    for u in R:
                        act.wait_ge(S["oh_turned"][u], i + 1)
                        nc.scalar.copy(ohT[u][:, :], tps[u % 2][:, :]).then_inc(S["oh_copied"][u], 1)
                    for u in R:
                        act.wait_ge(S["e_made"][u], i + 1)
                        act.wait_ge(S["stat"][u], i)
                        act.wait_ge(S["e_free"][u], i)
                        nc.scalar.copy(es[u][:, :], eps[u][:, :]).then_inc(S["e_copied"][u], 1)

            @block.sync
            def _(sp):
                n = rounds_of(sp, L, z)
                with sp.Fori(1, n + 1) as i:
                    for u in R:
                        sp.wait_ge(S["e_copied"][u], i)
                        sp.dma_start(e_dram[bass.ds(((i - 1) * U + u) * P, P), :], es[u][:, :]).then_inc(S["stored"][u], 16)
                    for u in R:
                        sp.wait_ge(S["stored"][u], i * 16)
                        sp.sem_inc(S["e_free"][u], 1)


def phase_stats(nc, s, z, k, L, stats, g, b, pad_col, sc, sh, tag):
    with ExitStack() as ctx:
        sb, ps, sem = scope(nc, ctx, k)
        NG2 = z.NGS * 2
        t1, t2 = sb("st1" + tag, NG2), sb("st2" + tag, NG2)
        m, q, v, nf, pd, sd = (sb(f"st_{x}" + tag, 1) for x in ("m", "q", "v", "n", "p", "sd"))
        nps = ps("st_np" + tag, 1)
        step, ready, sd_ready, r_in, r_out = sem("st_step"), sem("st_ready"), sem("st_sd"), sem("st_rin"), sem("st_rout")
        st3 = stats[:, :].rearrange("p (m c) -> p m c", c=3)
        with nc.Block() as block:
            @block.vector
            def _(dve):
                c = Chain(dve, step)
                c.step(nc.vector.tensor_tensor(t1[:, :], st3[:, :, 0], st3[:, :, 1], ALU.mult))
                c.step(nc.vector.tensor_reduce(m[:, :], t1[:, :], AX, ALU.add))
                c.step(nc.vector.tensor_tensor(t2[:, :], t1[:, :], st3[:, :, 1], ALU.mult))
                c.step(nc.vector.tensor_tensor(t2[:, :], t2[:, :], st3[:, :, 2], ALU.add))
                c.step(nc.vector.tensor_reduce(q[:, :], t2[:, :], AX, ALU.add))
                if pad_col is not None:
                    c.step(nc.vector.tensor_reduce(nf[:, :], st3[:, :, 0], AX, ALU.add))
                    c.step(nc.vector.tensor_scalar(nf[:, :], nf[:, :], -float(s.E), None, ALU.add))
                    c.step(nc.vector.tensor_tensor(pd[:, :], nf[:, :], pad_col, ALU.mult))
                    c.step(nc.vector.tensor_tensor(m[:, :], m[:, :], pd[:, :], ALU.subtract))
                    c.step(nc.vector.tensor_tensor(pd[:, :], pd[:, :], pad_col, ALU.mult))
                    c.step(nc.vector.tensor_tensor(q[:, :], q[:, :], pd[:, :], ALU.subtract))
                c.step(nc.vector.tensor_scalar(m[:, :], m[:, :], 1.0 / s.E, None, ALU.mult))
                c.step(nc.vector.tensor_scalar(q[:, :], q[:, :], 1.0 / s.E, None, ALU.mult))
                c.step(nc.vector.tensor_tensor(v[:, :], m[:, :], m[:, :], ALU.mult))
                c.step(nc.vector.tensor_tensor(v[:, :], q[:, :], v[:, :], ALU.subtract))
                c.step(nc.vector.tensor_scalar(v[:, :], v[:, :], 0.0, EPS, ALU.max, ALU.add))
                dve.sem_inc(ready, 1)
                dve.wait_ge(sd_ready, 1)
                c.step(nc.vector.reciprocal(v[:, :], sd[:, :]))
                c.step(nc.vector.tensor_tensor(sc, v[:, :], g, ALU.mult))
                c.step(nc.vector.tensor_tensor(m[:, :], m[:, :], sc, ALU.mult))
                c.step(nc.vector.tensor_tensor(sh, b, m[:, :], ALU.subtract))

            @block.scalar
            def _(act):
                act.wait_ge(ready, 1)
                nc.scalar.activation(sd[:, :], v[:, :], ACT.Sqrt).then_inc(sd_ready, 1)


def phase_fc_stats(nc, s, z, k, L, fcT, sc, sh, e_dram, stats, empty):
    with ExitStack() as ctx:
        sb, ps, sem = scope(nc, ctx, k)
        R = range(U)
        ein = [sb(f"f_e{u}", GE) for u in R]
        act_t = [sb(f"f_a{u}", GE) for u in R]
        zps = [ps(f"f_z{u}", GE) for u in R]
        r0 = sb("f_r0", 1)
        eps_ = ps("f_empty", 1)
        S = {n: [sem(f"f_{n}{u}") for u in R] for n in ("e_in", "a_made", "z_made", "stat")}
        cleared, r0_made, empty_made, empty_out = sem("f_cleared"), sem("f_r0_made"), sem("f_empty_made"), sem("f_empty_out")
        with nc.Block() as block:
            @block.sync
            def _(sp):
                n = rounds_of(sp, L, z)
                for u in R:
                    sp.sem_inc(S["a_made"][u], 1)
                with sp.Fori(1, n + 1) as i:
                    for u in R:
                        sp.wait_ge(S["a_made"][u], i)
                        sp.dma_start(ein[u][:, :], e_dram[bass.ds(((i - 1) * U + u) * P, P), :]).then_inc(S["e_in"][u], 16)

            @block.scalar
            def _(act):
                nc.scalar.activation(r0[:, :], sh, ACT.Relu).then_inc(r0_made, 1)
                n = rounds_of(act, L, z)
                for u in R:
                    act.sem_inc(S["z_made"][u], 1)
                with act.Fori(1, n + 1) as i:
                    for u in R:
                        act.wait_ge(S["e_in"][u], i * 16)
                        act.wait_ge(S["z_made"][u], i)
                        nc.scalar.activation(act_t[u][:, :], ein[u][:, :], ACT.Relu, bias=sh, scale=sc).then_inc(S["a_made"][u], 1)

            @block.tensor
            def _(pe):
                pe.wait_ge(r0_made, 1)
                nc.tensor.matmul(eps_[:, :], fcT[:, :], r0[:, :], start=True, stop=True).then_inc(empty_made, 1)
                n = rounds_of(pe, L, z)
                with pe.Fori(1, n + 1) as i:
                    for u in R:
                        pe.wait_ge(S["a_made"][u], i + 1)
                        pe.wait_ge(S["stat"][u], i)
                        nc.tensor.matmul(zps[u][:, :], fcT[:, :], act_t[u][:, :], start=True, stop=True).then_inc(S["z_made"][u], 1)

            @block.vector
            def _(dve):
                nc.vector.memset(stats[:, :], 0.0).then_inc(cleared, 1)
                dve.wait_ge(cleared, 1)
                dve.wait_ge(empty_made, 1)
                nc.vector.tensor_copy(empty[:, :], eps_[:, :]).then_inc(empty_out, 1)
                n = rounds_of(dve, L, z)
                for u in R:
                    dve.sem_inc(S["stat"][u], 1)
                with dve.Fori(1, n + 1) as i:
                    for u in R:
                        dve.wait_ge(S["z_made"][u], i + 1)
                        nc.vector.bn_stats(stats[:, bass.ds(((i - 1) * U + u) * 6, 6)], zps[u][:, :]).then_inc(S["stat"][u], 1)


def phase_fc_weights(nc, s, k, fc, sc, sh, fcs, shrow):
    with ExitStack() as ctx:
        sb, ps, sem = scope(nc, ctx, k)
        t, dg = sb("w_t", D), sb("w_dg", D)
        p1, p2 = ps("w_p1", D), ps("w_p2", D)
        step, made, done = sem("w_step"), sem("w_made"), sem("w_done")
        with nc.Block() as block:
            @block.vector
            def _(dve):
                c = Chain(dve, step)
                nc.vector.tensor_scalar(t[:, :], fc[:, :], sc, None, ALU.mult).then_inc(made, 1)
                nc.vector.tensor_scalar(dg[:, :], k["ident"][:, :], sh, None, ALU.mult).then_inc(made, 1)
                dve.wait_ge(done, 2)
                c.go(nc.vector.tensor_copy(fcs[:, :], p1[:, :]))
                for j in range(G):
                    c.go(nc.vector.tensor_copy(shrow[:, j * D:(j + 1) * D], p2[:, :]))
                dve.wait_ge(step, c.n)

            @block.tensor
            def _(pe):
                pe.wait_ge(made, 2)
                nc.tensor.transpose(p1[:, :], t[:, :], k["ident"][:, :]).then_inc(done, 1)
                nc.tensor.matmul(p2[:, :], k["ones"][:, :], dg[:, :], start=True, stop=True).then_inc(done, 1)


def phase_edge_out(nc, s, z, k, L, fcs, shrow, sc, sh, e_dram, acc):
    with ExitStack() as ctx:
        sb, ps, sem = scope(nc, ctx, k)
        R = range(U)
        ein = [sb(f"o_e{u}", GE) for u in R]
        act_t = [sb(f"o_a{u}", GE) for u in R]
        zs = [sb(f"o_z{u}", G * D) for u in R]
        zr = [sb(f"o_r{u}", G * D) for u in R]
        oh = [sb(f"o_oh{u}", G * P) for u in R]
        zps = [ps(f"o_zps{u}", G * D) for u in R]
        sps = [ps(f"o_sps{u}", D) for u in R]
        S = {n: [sem(f"o_{n}{u}") for u in R] for n in ("e_in", "a_made", "z_made", "z_shifted", "z_relu", "oh_made", "summed")}
        chain = sem("o_chain")
        with nc.Block() as block:
            @block.sync
            def _(sp):
                n = rounds_of(sp, L, z)
                for u in R:
                    sp.sem_inc(S["a_made"][u], 1)
                with sp.Fori(1, n + 1) as i:
                    for u in R:
                        sp.wait_ge(S["a_made"][u], i)
                        sp.dma_start(ein[u][:, :], e_dram[bass.ds(((i - 1) * U + u) * P, P), :]).then_inc(S["e_in"][u], 16)

            @block.scalar
            def _(act):
                n = rounds_of(act, L, z)
                for u in R:
                    act.sem_inc(S["z_made"][u], 1)
                with act.Fori(1, n + 1) as i:
                    for u in R:
                        act.wait_ge(S["e_in"][u], i * 16)
                        act.wait_ge(S["z_made"][u], i)
                        nc.scalar.activation(act_t[u][:, :], ein[u][:, :], ACT.Relu, bias=sh, scale=sc).then_inc(S["a_made"][u], 1)
                    for u in R:
                        act.wait_ge(S["z_shifted"][u], i + 1)
                        act.wait_ge(S["summed"][u], i)
                        nc.scalar.activation(zr[u][:, :], zs[u][:, :], ACT.Relu).then_inc(S["z_relu"][u], 1)

            @block.tensor
            def _(pe):
                n = rounds_of(pe, L, z)
                with pe.Fori(1, n + 1) as i:
                    for u in R:
                        pe.wait_ge(S["a_made"][u], i + 1)
                        pe.wait_ge(S["z_shifted"][u], i)
                        for j in range(G):
                            last = nc.tensor.matmul(zps[u][:, j * D:(j + 1) * D], act_t[u][:, j * P:(j + 1) * P], fcs[:, :],
                                                    start=True, stop=True)
                        last.then_inc(S["z_made"][u], 1)
                    for u in R:
                        pe.wait_ge(S["oh_made"][u], i)
                        pe.wait_ge(S["z_relu"][u], i + 1)
                        for j in range(G):
                            last = nc.tensor.matmul(sps[u][:, :], oh[u][:, j * P:(j + 1) * P], zr[u][:, j * D:(j + 1) * D],
                                                    start=(j == 0), stop=(j == G - 1))
                        last.then_inc(S["summed"][u], 1)

            @block.vector
            def _(dve):
                nc.vector.memset(acc[:, :], 0.0).then_inc(chain, 1)
                n = rounds_of(dve, L, z)
                for u in R:
                    dve.sem_inc(S["summed"][u], 1)
                    dve.sem_inc(S["z_shifted"][u], 1)
                    dve.sem_inc(S["z_relu"][u], 1)
                with dve.Fori(1, n + 1) as i:
                    for u in R:
                        g = (i - 1) * U + u
                        dve.wait_ge(S["summed"][u], i)
                        for j in range(G):
                            last = nc.vector.tensor_scalar(oh[u][:, j * P:(j + 1) * P], k["iota_f"][:, :],
                                                           L["place"][:, bass.ds(g * G + j, 1)], None, ALU.is_equal)
                        last.then_inc(S["oh_made"][u], 1)
                    for u in R:
                        dve.wait_ge(S["z_made"][u], i + 1)
                        dve.wait_ge(S["z_relu"][u], i)
                        nc.vector.tensor_tensor(zs[u][:, :], zps[u][:, :], shrow[:, :], ALU.add).then_inc(S["z_shifted"][u], 1)
                    for u in R:
                        b = dve.value_load(L["block"][0:1, bass.ds((i - 1) * U + u, 1)], min_val=0, max_val=s.NB)
                        dve.wait_ge(S["summed"][u], i + 1)
                        dve.wait_ge(chain, (i - 1) * U + u + 1)
                        nc.vector.tensor_tensor(acc[:, bass.ds(b * D, D)], acc[:, bass.ds(b * D, D)], sps[u][:, :], ALU.add
                                                ).then_inc(chain, 1)


def phase_edge_mean(nc, s, k, acc, counts):
    with ExitStack() as ctx:
        sb, ps, sem = scope(nc, ctx, k)
        rc = sb("em_rc", s.NB1)
        step = sem("em_step")
        with nc.Block() as block:
            @block.vector
            def _(dve):
                c = Chain(dve, step)
                c.step(nc.vector.tensor_scalar(rc[:, :], counts[:, :], 1.0, None, ALU.max))
                c.step(nc.vector.reciprocal(rc[:, :], rc[:, :]))
                c.step(nc.vector.tensor_tensor(blocks(acc), blocks(acc), rc[:, :].unsqueeze(2).broadcast_to([P, s.NB1, D]), ALU.mult))
                c.step(nc.vector.tensor_tensor(acc[:, :], acc[:, :], k["x"][:, :], ALU.add))
                c.step(nc.vector.scalar_tensor_tensor(out=acc[:, :], in0=acc[:, :], scalar=0.0, in1=k["x"][:, :],
                                                      op0=ALU.max, op1=ALU.add))
        phase_layernorm(nc, s, k, acc, "1")


def phase_degrees(nc, s, k, counts, dinv, h):
    with ExitStack() as ctx:
        sb, ps, sem = scope(nc, ctx, k)
        dg, sq = sb("dg_d", s.NB1), sb("dg_s", s.NB1)
        step, ready, rooted = sem("dg_step"), sem("dg_ready"), sem("dg_rooted")
        with nc.Block() as block:
            @block.vector
            def _(dve):
                c = Chain(dve, step)
                nc.vector.tensor_scalar(dg[:, :], counts[:, :], 1.0, None, ALU.add).then_inc(ready, 1)
                dve.wait_ge(rooted, 1)
                c.step(nc.vector.reciprocal(dinv[:, :], sq[:, :]))
                c.step(nc.vector.tensor_tensor(blocks(h), blocks(h), dinv[:, :].unsqueeze(2).broadcast_to([P, s.NB1, D]), ALU.mult))

            @block.scalar
            def _(act):
                act.wait_ge(ready, 1)
                nc.scalar.activation(sq[:, :], dg[:, :], ACT.Sqrt).then_inc(rooted, 1)


def phase_conv_out(nc, s, k, acc, h, dinv, bias, gamma, beta):
    with ExitStack() as ctx:
        sb, ps, sem = scope(nc, ctx, k)
        mask_i, mask = sb("co_mi", s.NB1, I32), sb("co_m", s.NB1)
        part, row = sb("co_part", D), sb("co_row", D)
        tot = [ps(f"co_tot{n}", D) for n in range(2)]
        step, ready, totals, node_id, ready2, rooted = (sem(x) for x in ("co_step", "co_ready", "co_tot", "co_id", "co_ready2", "co_root"))
        sd = sb("co_sd", D)
        with nc.Block() as block:
            @block.gpsimd
            def _(pool):
                nc.gpsimd.iota(mask_i[:, :], pattern=[[P, s.NB1]], base=0, channel_multiplier=1).then_inc(node_id, 1)

            @block.tensor
            def _(pe):
                for n in range(2):
                    pe.wait_ge(ready, n + 1)
                    nc.tensor.matmul(tot[n][:, :], k["ones"][:, :], part[:, :], start=True, stop=True).then_inc(totals, 1)

            @block.scalar
            def _(act):
                act.wait_ge(ready2, 1)
                nc.scalar.activation(sd[:, :], row[:, :], ACT.Sqrt).then_inc(rooted, 1)

            @block.vector
            def _(dve):
                c = Chain(dve, step)
                by_feature = acc[:, :].rearrange("p (b f) -> p f b", f=D)
                sq_feature = h[:, :].rearrange("p (b f) -> p f b", f=D)
                c.step(nc.vector.tensor_tensor(acc[:, :], acc[:, :], h[:, :], ALU.add))
                c.step(nc.vector.tensor_tensor(blocks(acc), blocks(acc), dinv[:, :].unsqueeze(2).broadcast_to([P, s.NB1, D]), ALU.mult))
                c.step(nc.vector.tensor_tensor(blocks(acc), blocks(acc), over_blocks(bias[:, :], s), ALU.add))
                dve.wait_ge(node_id, 1)
                c.step(nc.vector.tensor_copy(mask[:, :], mask_i[:, :]))
                c.step(nc.vector.tensor_scalar(mask[:, :], mask[:, :], float(s.N), None, ALU.is_lt))
                m3 = mask[:, :].unsqueeze(2).broadcast_to([P, s.NB1, D])
                c.step(nc.vector.scalar_tensor_tensor(out=blocks(acc), in0=blocks(acc), scalar=0.0, in1=m3, op0=ALU.max, op1=ALU.mult))
                c.step(nc.vector.tensor_reduce(part[:, :], by_feature, AX, ALU.add))
                dve.sem_inc(ready, 1)
                dve.wait_ge(totals, 1)
                c.step(nc.vector.tensor_scalar(row[:, :], tot[0][:, :], 1.0 / s.N, None, ALU.mult))
                c.step(nc.vector.tensor_tensor(blocks(acc), blocks(acc), over_blocks(row[:, :], s), ALU.subtract))
                c.step(nc.vector.tensor_tensor(blocks(acc), blocks(acc), m3, ALU.mult))
                c.step(nc.vector.tensor_tensor(h[:, :], acc[:, :], acc[:, :], ALU.mult))
                c.step(nc.vector.tensor_reduce(part[:, :], sq_feature, AX, ALU.add))
                dve.sem_inc(ready, 1)
                dve.wait_ge(totals, 2)
                c.step(nc.vector.tensor_scalar(row[:, :], tot[1][:, :], 1.0 / s.N, EPS, ALU.mult, ALU.add))
                dve.sem_inc(ready2, 1)
                dve.wait_ge(rooted, 1)
                c.step(nc.vector.reciprocal(row[:, :], sd[:, :]))
                c.step(nc.vector.tensor_tensor(row[:, :], row[:, :], gamma[:, :], ALU.mult))
                c.step(nc.vector.tensor_tensor(blocks(acc), blocks(acc), over_blocks(row[:, :], s), ALU.mult))
                c.step(nc.vector.tensor_tensor(blocks(acc), blocks(acc), over_blocks(beta[:, :], s), ALU.add))
                c.step(nc.vector.tensor_tensor(acc[:, :], acc[:, :], k["x"][:, :], ALU.add))
        phase_layernorm(nc, s, k, acc, "2")


def phase_add_x(nc, s, k, y):
    with ExitStack() as ctx:
        sb, ps, sem = scope(nc, ctx, k)
        added = sem("x_added")
        with nc.Block() as block:
            @block.vector
            def _(dve):
                nc.vector.tensor_tensor(y[:, :], y[:, :], k["x"][:, :], ALU.add).then_inc(added, 1)
                dve.wait_ge(added, 1)


def phase_turn(nc, k, pairs, tag):
    with ExitStack() as ctx:
        sb, ps, sem = scope(nc, ctx, k)
        tp = ps("t_tp" + tag, len(pairs) * P)
        diff = [sb(f"t_diff{n}" + tag, P) for n in range(len(pairs))]
        made, turned, out = sem("t_made"), sem("t_turned"), sem("t_out")
        with nc.Block() as block:
            @block.vector
            def _(dve):
                for n, (dst, src, minus) in enumerate(pairs):
                    if minus is None:
                        nc.vector.tensor_copy(diff[n][:, :], src[:, :]).then_inc(made, 1)
                    else:
                        nc.vector.tensor_tensor(diff[n][:, :], src[:, :], minus[:, :], ALU.subtract).then_inc(made, 1)
                dve.wait_ge(turned, 1)
                for n, (dst, src, minus) in enumerate(pairs):
                    nc.vector.tensor_copy(dst, tp[:, n * P:(n + 1) * P]).then_inc(out, 1)
                dve.wait_ge(out, len(pairs))

            @block.tensor
            def _(pe):
                pe.wait_ge(made, len(pairs))
                for n in range(len(pairs)):
                    last = nc.tensor.transpose(tp[:, n * P:(n + 1) * P], diff[n][:, :], k["ident"][:, :])
                last.then_inc(turned, 1)


def gnn_kernel(nc, x, src, dst, edge_weight, q_w, q_b, k_w, k_b, v_w, att_bias, theta, phi, fc1, g0, b0, g1, b1,
               conv_w, conv_b, gamma, beta, w1, bias1, w2, bias2, out):
    s = Shapes(x.shape[0], src.shape[0])
    zs, zd = Sorted(s, True), Sorted(s, False)
    NF = s.NB1 * D

    def dram(name, shape):
        return nc.dram_tensor(name, shape, F32).ap()

    def spread(vec, n=P):
        return vec.rearrange("(o f) -> o f", o=1).broadcast_to([n, vec.shape[0]])

    def column(vec):
        return vec.rearrange("(f o) -> f o", o=1)

    with ExitStack() as top:
        def tile(ctx, name, cols, dt=F32, parts=P):
            return ctx.enter_context(nc.sbuf_tensor(name, [parts, cols], dt))
        k = dict(sems=Semaphores(nc, top))
        for name, cols, dt in (("x", NF, F32), ("ones", P, F32), ("zero", P, F32), ("iota_f", P, BF16), ("iota_p", 1, F32),
                               ("ident", P, F32), ("ident_b", P, BF16), ("before", 4 * P, F32), ("after", P, F32)):
            k[name] = tile(top, name, cols, dt)
        phase_constants(nc, s, x, k)

        with ExitStack() as c0:
            L = dict(rounds=tile(c0, "rounds_s", 1, I32), block=tile(c0, "block_s", zs.NGS, I32, 1),
                     counts=tile(c0, "counts_s", s.NB1), place=tile(c0, "place_s", zs.NGS * G),
                     gather=tile(c0, "gather_s", zs.NGS * G, U32), segment=tile(c0, "segment_s", zs.NGS * G))
            sort_edges(nc, s, zs, k, L, src, dst, None, "_s")
            kv_table, v_dram = dram("kv_table", [s.NB1 * P, 2 * D]), dram("v_edges", [zs.NGS * P, G * D])
            att_dram, ex_dram = dram("att_edges", [zs.NGS * P, G * H]), dram("ex_edges", [zs.NGS * P, G * H])
            seg_dram = dram("segments", [zs.NGS * GE + 16])
            abias = tile(c0, "abias", D)
            att = None
            with ExitStack() as c1:
                Q = [tile(c1, f"q_part{n}", NF, BF16) for n in range(3)]
                with ExitStack() as c2:
                    qf, kvf = tile(c2, "q_full", NF), tile(c2, "kv_full", 2 * NF)
                    w, brow = tile(c2, "qkv_w", 3 * D), tile(c2, "qkv_b", 3 * D, F32, 1)
                    phase_load(nc, k, [(w[:, 0:D], q_w), (w[:, D:2 * D], k_w), (w[:, 2 * D:], v_w), (abias[:, :], spread(att_bias)),
                                       (brow[:, 0:D], spread(q_b, 1)), (brow[:, D:2 * D], spread(k_b, 1))], "w0")
                    phase_zero(nc, k, brow[:, 2 * D:])
                    phase_dense(nc, s, k, k["x"], w[:, :], brow,
                                [(0, D, ACT.Relu, lambda b: qf[:, bass.ds(b * D, D)]),
                                 (D, 2 * D, ACT.Relu, lambda b: kvf[:, bass.ds(b * 2 * D, D)]),
                                 (2 * D, 3 * D, ACT.Copy, lambda b: kvf[:, bass.ds(b * 2 * D + D, D)])], "_qkv")
                    phase_store(nc, k, [(kv_table, kvf, 2 * D)])
                    phase_split(nc, s, k, qf, Q, "_q")
                with ExitStack() as c2:
                    att_a = tile(c2, "att_scores", zs.NGS * G * H)
                    phase_scores(nc, s, zs, k, L, Q, att_a, kv_table, v_dram, att_dram)
            att = tile(c0, "att", zs.NGS * G * H)
            phase_softmax(nc, s, zs, k, L, att, seg_dram, att_dram, ex_dram)
            with ExitStack() as c1:
                acc = tile(c1, "acc0", s.NB1 * (D + H))
                phase_messages(nc, s, zs, k, L, att, acc, v_dram)
                phase_attention_out(nc, s, k, acc, abias)

        L = dict(rounds=tile(top, "rounds_d", 1, I32), block=tile(top, "block_d", zd.NGS, I32, 1),
                 counts=tile(top, "counts_d", s.NB1), place=tile(top, "place_d", zd.NGS * G),
                 gather=tile(top, "gather_d", zd.NGS * G, U32), weight=tile(top, "weight_d", zd.NGS * G))
        sort_edges(nc, s, zd, k, L, dst, src, edge_weight, "_d")
        acc = tile(top, "acc", NF)

        with ExitStack() as c0:
            r_table, e_dram = dram("r_table", [s.NB1 * P, D]), dram("e_edges", [zd.NGS * P, GE])
            stats, fc, fcT, fcs = tile(c0, "stats", zd.NGS * 6), tile(c0, "fc", D), tile(c0, "fcT", D), tile(c0, "fcs", D)
            shrow, cols, empty = tile(c0, "shrow", G * D), tile(c0, "bn_cols", 8), tile(c0, "empty", 1)
            Pn = [tile(c0, f"p_part{n}", NF, BF16) for n in range(3)]
            with ExitStack() as c1:
                th, ph, w = tile(c1, "theta", D), tile(c1, "phi", D), tile(c1, "pr_w", 2 * D)
                pf, rf = tile(c1, "p_full", NF), tile(c1, "r_full", NF)
                phase_load(nc, k, [(th[:, :], theta), (ph[:, :], phi), (fc[:, :], fc1), (cols[:, 0:1], column(g0)),
                                   (cols[:, 1:2], column(b0)), (cols[:, 2:3], column(g1)), (cols[:, 3:4], column(b1))], "w1")
                phase_turn(nc, k, [(w[:, 0:D], th, None), (w[:, D:], ph, th), (fcT[:, :], fc, None)], "_w1")
                phase_dense(nc, s, k, k["x"], w[:, :], None,
                            [(0, D, ACT.Copy, lambda b: pf[:, bass.ds(b * D, D)]),
                             (D, 2 * D, ACT.Copy, lambda b: rf[:, bass.ds(b * D, D)])], "_pr")
                phase_store(nc, k, [(r_table, rf, D)])
                phase_split(nc, s, k, pf, Pn, "_p")
            phase_edge_sums(nc, s, zd, k, L, Pn, r_table, e_dram, stats)
            phase_stats(nc, s, zd, k, L, stats, cols[:, 0:1], cols[:, 1:2], None, cols[:, 4:5], cols[:, 5:6], "a")
            phase_fc_stats(nc, s, zd, k, L, fcT, cols[:, 4:5], cols[:, 5:6], e_dram, stats, empty)
            phase_stats(nc, s, zd, k, L, stats, cols[:, 2:3], cols[:, 3:4], empty[:, :], cols[:, 6:7], cols[:, 7:8], "b")
            phase_fc_weights(nc, s, k, fc, cols[:, 6:7], cols[:, 7:8], fcs, shrow)
            phase_edge_out(nc, s, zd, k, L, fcs, shrow, cols[:, 4:5], cols[:, 5:6], e_dram, acc)
            phase_edge_mean(nc, s, k, acc, L["counts"])

        with ExitStack() as c0:
            g_table = dram("g_table", [s.NB1 * P, D])
            h, w, dinv = tile(c0, "h", NF), tile(c0, "conv_w", D), tile(c0, "dinv", s.NB1)
            rows3 = [tile(c0, f"conv_row{n}", D) for n in range(3)]
            phase_load(nc, k, [(w[:, :], conv_w)] + [(t[:, :], spread(v)) for t, v in zip(rows3, (conv_b, gamma, beta))], "w2")
            phase_dense(nc, s, k, k["x"], w[:, :], None, [(0, D, ACT.Copy, lambda b: h[:, bass.ds(b * D, D)])], "_h")
            phase_degrees(nc, s, k, L["counts"], dinv, h)
            phase_store(nc, k, [(g_table, h, D)])
            phase_gather_sum(nc, s, zd, k, L, g_table, acc, False, "_g")
            phase_conv_out(nc, s, k, acc, h, dinv, *rows3)

        with ExitStack() as c0:
            x_table = dram("x_table", [s.NB1 * P, D])
            w, brow, y = tile(c0, "mlp_w", 2 * D), tile(c0, "mlp_b", 2 * D, F32, 1), tile(c0, "mlp_y", NF)
            phase_load(nc, k, [(w[:, 0:D], w1), (w[:, D:], w2), (brow[:, 0:D], spread(bias1, 1)), (brow[:, D:], spread(bias2, 1))], "w3")
            phase_store(nc, k, [(x_table, k["x"], D)])
            phase_gather_sum(nc, s, zd, k, L, x_table, acc, True, "_x")
            phase_add_x(nc, s, k, acc)
            phase_dense(nc, s, k, acc, w[:, 0:D], brow[:, 0:D], [(0, D, ACT.Relu, lambda b: y[:, bass.ds(b * D, D)])], "_m1")
            phase_dense(nc, s, k, y, w[:, D:], brow[:, D:], [(0, D, ACT.Copy, lambda b: acc[:, bass.ds(b * D, D)])], "_m2")
            phase_add_x(nc, s, k, acc)
            phase_layernorm(nc, s, k, acc, "3")
            phase_result(nc, s, k, out)


def phase_zero(nc, k, ap):
    with ExitStack() as ctx:
        sb, ps, sem = scope(nc, ctx, k)
        done = sem("zero_done")
        with nc.Block() as block:
            @block.vector
            def _(dve):
                nc.vector.memset(ap, 0.0).then_inc(done, 1)
                dve.wait_ge(done, 1)


def phase_result(nc, s, k, out):
    with ExitStack() as ctx:
        sb, ps, sem = scope(nc, ctx, k)
        stored = sem("result_stored")
        full = s.N // P
        with nc.Block() as block:
            @block.sync
            def _(sp):
                n = 0
                if full:
                    sp.dma_start(out[0:full * P, :].rearrange("(b p) f -> p b f", p=P),
                                 k["x"][:, 0:full * D].rearrange("p (b f) -> p b f", f=D)).then_inc(stored, 16)
                    n += 16
                if s.N > full * P:
                    sp.dma_start(out[full * P:, :], k["x"][0:s.N - full * P, full * D:(full + 1) * D]).then_inc(stored, 16)
                    n += 16
                sp.wait_ge(stored, n)


_INS = ["x", "src", "dst", "edge_weight", "L0_gnn_query_kernel", "L0_gnn_query_bias", "L0_gnn_key_kernel", "L0_gnn_key_bias",
        "L0_gnn_kernel", "L0_gnn_bias", "L1_gnn_theta_w", "L1_gnn_phi_w", "L1_gnn_fc1_w", "L1_gnn_bn0_g", "L1_gnn_bn0_b",
        "L1_gnn_bn1_g", "L1_gnn_bn1_b", "L2_gnn_W", "L2_gnn_b", "L2_gnn_gamma", "L2_gnn_beta",
        "L3_gnn_W1", "L3_gnn_b1", "L3_gnn_W2", "L3_gnn_b2"]


def kernel(**inputs):
    import numpy as _np
    import concourse.bacc as _bacc
    from concourse.bass_utils import run_bass_kernel_spmd as _run

    nc = _bacc.Bacc("TRN2", target_bir_lowering=False, num_devices=1)
    arrays, args = {}, []
    for name in _INS:
        a = _np.ascontiguousarray(inputs[name])
        arrays[f"in_{name}_dram"] = a
        args.append(nc.dram_tensor(f"in_{name}_dram", a.shape, mybir.dt.from_np(a.dtype), kind="ExternalInput").ap())
    args.append(nc.dram_tensor("out_dram", inputs["x"].shape, F32, kind="ExternalOutput").ap())
    gnn_kernel(nc, *args)
    r = _run(nc, [arrays], core_ids=[0])
    return r.results[0]["out_dram"]
```

```python
from contextlib import ExitStack

import concourse.bass as bass
from concourse import mybir

F32 = mybir.dt.float32
BF16 = mybir.dt.bfloat16
I32 = mybir.dt.int32
U32 = mybir.dt.uint32
ALU = mybir.AluOpType
ACT = mybir.ActivationFunctionType
AX = mybir.AxisListType.X

P = 128
D = 128
H = 8
HD = D // H
G = 4
GE = G * P
U = 4
RUN = 8
EPS = 1e-5
FAR = 1.0e6


class Shapes:

    def __init__(self, nodes, edges):
        self.N, self.E = nodes, edges
        self.NB = -(-nodes // P)
        self.NB1 = (self.NB + 2) // 2 * 2
        self.PAD = self.NB * P
        self.ZROW = self.NB1 * P - 1
        self.SPARE = self.NB


class Sorted:

    def __init__(self, s, loops):
        self.T = -(-s.E // P)
        self.LT = s.NB if loops else 0
        self.TT = -(-(self.T + s.NB) // 16) * 16
        self.C = -(-self.TT // P)
        self.rows = self.TT * P
        ng = (s.E + self.LT * P) // GE + s.NB
        self.NGS = -(-ng // U) * U
        self.GMIN = (s.E + self.LT * P) // GE // U * U
        self.GC = -(-self.NGS // P)


class Chain:

    def __init__(self, eng, sem):
        self.eng, self.sem, self.n = eng, sem, 0

    def step(self, ins):
        self.n += 1
        ins.then_inc(self.sem, 1)
        self.eng.wait_ge(self.sem, self.n)

    def go(self, ins):
        self.n += 1
        ins.then_inc(self.sem, 1)


class Semaphores:

    def __init__(self, nc, ctx):
        self.nc, self.ctx, self.free = nc, ctx, []

    def take(self, name):
        return self.free.pop() if self.free else self.ctx.enter_context(self.nc.semaphore(name))

    def hand_back(self, taken):
        with self.nc.Block() as block:
            @block.gpsimd
            def _(pool):
                for s in taken:
                    pool.sem_clear(s)
        self.free += taken


def scope(nc, ctx, k):
    taken = []

    def sb(name, cols, dt=F32, parts=P):
        return ctx.enter_context(nc.sbuf_tensor(name, [parts, cols], dt))

    def ps(name, cols, dt=F32):
        return ctx.enter_context(nc.psum_tensor(name, [P, cols], dt))

    def sem(name, own=False):
        if own:
            return k["sems"].ctx.enter_context(nc.semaphore(name))
        taken.append(k["sems"].take(name))
        return taken[-1]
    ctx.push(lambda et, ev, tb: None if et else (k["sems"].hand_back(taken) if taken else None))
    return sb, ps, sem


def phase_constants(nc, s, x_in, k):
    with ExitStack() as ctx:
        sb, ps, sem = scope(nc, ctx, k)
        fi, pi = sb("fi", P, I32), sb("pi", 1, I32)
        ff, fw = sb("ff", P), sb("fw", 8 * P, I32)
        iota_done, const_step, x_cleared, x_loaded = sem("iota_done"), sem("const_step"), sem("x_cleared"), sem("x_loaded")
        full = s.N // P
        rest = s.N - full * P
        with nc.Block() as block:
            @block.gpsimd
            def _(pool):
                nc.gpsimd.iota(fi[:, :], pattern=[[1, P]], base=0, channel_multiplier=0).then_inc(iota_done, 1)
                nc.gpsimd.iota(pi[:, :], pattern=[[1, 1]], base=0, channel_multiplier=1).then_inc(iota_done, 1)
                nc.gpsimd.iota(fw[:, :], pattern=[[1, P], [0, 8]], base=0, channel_multiplier=0).then_inc(iota_done, 1)

            @block.vector
            def _(dve):
                c = Chain(dve, const_step)
                nc.vector.memset(k["x"][:, full * D:], 0.0).then_inc(x_cleared, 1)
                c.go(nc.vector.memset(k["ones"][:, :], 1.0))
                c.go(nc.vector.memset(k["zero"][:, :], 0.0))
                dve.wait_ge(iota_done, 3)
                c.go(nc.vector.tensor_copy(k["iota_8"][:, :], fw[:, :]))
                c.go(nc.vector.tensor_copy(ff[:, :], fi[:, :]))
                c.go(nc.vector.tensor_copy(k["iota_f"][:, :], fi[:, :]))
                c.step(nc.vector.tensor_copy(k["iota_p"][:, :], pi[:, :]))
                col = k["iota_p"][:, 0:1]
                c.go(nc.vector.tensor_scalar(k["ident"][:, :], ff[:, :], col, None, ALU.is_equal))
                c.go(nc.vector.tensor_scalar(k["ident_b"][:, :], ff[:, :], col, None, ALU.is_equal))
                c.go(nc.vector.memset(k["before"][:, 0:3 * P], 1.0))
                c.go(nc.vector.tensor_scalar(k["before"][:, 3 * P:], ff[:, :], col, None, ALU.is_lt))
                c.step(nc.vector.tensor_scalar(k["after"][:, :], ff[:, :], col, None, ALU.is_gt))

            @block.sync
            def _(sp):
                sp.wait_ge(x_cleared, 1)
                n = 0
                if full:
                    sp.dma_start(k["x"][:, 0:full * D].rearrange("p (b f) -> p b f", f=D),
                                 x_in[0:full * P, :].rearrange("(b p) f -> p b f", p=P)).then_inc(x_loaded, 16)
                    n += 16
                if rest:
                    sp.dma_start(k["x"][0:rest, full * D:(full + 1) * D], x_in[full * P:, :]).then_inc(x_loaded, 16)
                    n += 16
                sp.wait_ge(x_loaded, n)


def phase_sort_input(nc, s, z, k, a, key_in, other_in, weight_in, tag):
    with ExitStack() as ctx:
        sb, ps, sem = scope(nc, ctx, k)
        W = z.C * P
        ki, oi = sb("ki" + tag, W, I32), sb("oi" + tag, W, I32)
        kf, of = sb("kf" + tag, W), sb("of" + tag, W)
        if z.LT:
            li, lf, lm = sb("li" + tag, W, I32), sb("lf" + tag, W), sb("lm" + tag, W)
        else:
            rows, nxt = sb("rowform" + tag, 4 * W), sb("nxt" + tag, W)
            tail, bad = sb("tail_in" + tag, GE * 4 // P), sb("bad" + tag, 1)
            bps = ps("bad_ps" + tag, 1)
        last16 = sb("last16" + tag, P, F32, 16)
        tail_ready, nxt_in, bad_made, bad_sum = sem("tail_ready"), sem("nxt_in"), sem("bad_made"), sem("bad_sum")
        wf = sb("wf" + tag, W) if weight_in is not None else None
        hi_i, lo_i = oi, ki
        tps = [ps(f"tps{u}" + tag, 4 * P) for u in range(2)]
        cleared, loaded, stored = sem("cleared"), sem("loaded"), sem("stored")
        loop_iota, step = sem("loop_iota"), sem("in_step")
        rows_ready, turned, evacuated = sem("rows_ready"), sem("turned"), sem("evac")
        arrays = [(kf, 0), (of, 1)] + ([(wf, 2)] if wf is not None else [])
        lots = [(src, c, col, ci) for src, col in arrays for ci, c in enumerate(range(0, z.C, 4))]
        full_c, full_t = s.E // (P * P), s.E // P
        part = s.E - full_t * P

        def pieces(dst, src):
            if full_c:
                yield (dst[:, 0:full_c * P].rearrange("q (c l) -> q c l", l=P),
                       src[0:full_c * P * P].rearrange("(c q l) -> q c l", q=P, l=P))
            q = full_t - full_c * P
            if q:
                yield (dst[0:q, full_c * P:(full_c + 1) * P],
                       src[full_c * P * P:full_t * P].rearrange("(q l) -> q l", l=P))
            if part:
                yield (dst[q:q + 1, full_c * P:full_c * P + part],
                       src[full_t * P:s.E].rearrange("(q l) -> q l", q=1))

        pieces_n = len(list(pieces(ki, key_in))) * (2 if wf is None else 3)
        with nc.Block() as block:
            @block.sync
            def _(sp):
                sp.wait_ge(cleared, 2 if wf is None else 3)
                todo = [(ki, key_in), (oi, other_in)] + ([(wf, weight_in)] if wf is not None else [])
                for dst, src in todo:
                    for d, r in pieces(dst, src):
                        sp.dma_start(d, r).then_inc(loaded, 16)
                sp.wait_ge(rows_ready, 1)
                sp.dma_start(a["keyrow"][0:W * P].rearrange("(c q l) -> q c l", q=P, l=P),
                             kf[:, :].rearrange("q (c l) -> q c l", l=P)).then_inc(stored, 16)
                sp.wait_ge(tail_ready, 1)
                sp.dma_start(a["keyrow"][W * P:W * P + 16 * P].rearrange("(c l) -> c l", l=P), last16[:, :]).then_inc(stored, 16)
                sp.wait_ge(stored, 32)
                if not z.LT:
                    sp.dma_start(nxt[:, :].rearrange("q (c l) -> q c l", l=P),
                                 a["keyrow"][1:W * P + 1].rearrange("(c q l) -> q c l", q=P, l=P)).then_inc(nxt_in, 16)
                    sp.wait_ge(tail_ready, 3)
                    sp.dma_start(a["rows"][0:W * P, :].rearrange("(c q l) f -> q c (l f)", q=P, l=P),
                                 rows[:, :].rearrange("q (c x) -> q c x", x=4 * P)).then_inc(stored, 16)
                    sp.dma_start(a["rows"][W * P:W * P + GE, :].rearrange("(p j) c -> p (j c)", p=P), tail[:, :]).then_inc(stored, 16)
                    sp.wait_ge(stored, 64)

            @block.gpsimd
            def _(pool):
                if not z.LT:
                    return
                nc.gpsimd.iota(li[:, :].rearrange("q (c l) -> q c l", l=P), pattern=[[P * P, z.C], [1, P]],
                               base=-z.T * P, channel_multiplier=P).then_inc(loop_iota, 1)

            @block.vector
            def _(dve):
                c = Chain(dve, step)
                nc.vector.memset(ki[:, :], s.PAD).then_inc(cleared, 1)
                nc.vector.memset(oi[:, :], 0).then_inc(cleared, 1)
                if wf is not None:
                    nc.vector.memset(wf[:, :], 0.0).then_inc(cleared, 1)
                dve.wait_ge(loaded, 16 * pieces_n)
                c.go(nc.vector.tensor_copy(kf[:, :], ki[:, :]))
                c.step(nc.vector.tensor_copy(of[:, :], oi[:, :]))
                if z.LT:
                    dve.wait_ge(loop_iota, 1)
                    c.step(nc.vector.tensor_copy(lf[:, :], li[:, :]))
                    c.step(nc.vector.tensor_scalar(lm[:, :], lf[:, :], 0.0, None, ALU.is_ge))
                    c.step(nc.vector.scalar_tensor_tensor(out=lm[:, :], in0=lf[:, :], scalar=float(s.PAD), in1=lm[:, :],
                                                          op0=ALU.is_lt, op1=ALU.mult))
                    for dst in (kf, of):
                        tmp = hi_i[:, :].bitcast(F32)
                        c.step(nc.vector.tensor_tensor(tmp, lf[:, :], dst[:, :], ALU.subtract))
                        c.step(nc.vector.tensor_tensor(tmp, tmp, lm[:, :], ALU.mult))
                        c.step(nc.vector.tensor_tensor(dst[:, :], dst[:, :], tmp, ALU.add))
                dve.sem_inc(rows_ready, 1)
                nc.vector.memset(last16[:, :], float(s.PAD)).then_inc(tail_ready, 1)
                if not z.LT:
                    r4 = rows[:, :].rearrange("q (t c) -> q t c", c=4)
                    c.step(nc.vector.tensor_scalar(r4[:, :, 0], kf[:, :], float(s.PAD), FAR, ALU.is_ge, ALU.mult))
                    c.go(nc.vector.tensor_tensor(r4[:, :, 0], r4[:, :, 0], kf[:, :], ALU.add))
                    c.go(nc.vector.tensor_copy(r4[:, :, 1], of[:, :]))
                    c.go(nc.vector.tensor_copy(r4[:, :, 2], wf[:, :]))
                    c.step(nc.vector.memset(r4[:, :, 3], 0.0))
                    dve.sem_inc(tail_ready, 1)
                    nc.vector.memset(tail[:, :], FAR).then_inc(tail_ready, 1)
                for n, (src, c0, col, _) in enumerate(lots):
                    w = min(4, z.C - c0) * P
                    dve.wait_ge(turned, n + 1)
                    dst = a["key"][:, c0 * P:c0 * P + w] if col == 0 else \
                        a["pay"][:, :].rearrange("p (t c) -> p t c", c=4)[:, c0 * P:c0 * P + w, col]
                    nc.vector.tensor_copy(dst, tps[n % 2][:, 0:w]).then_inc(evacuated, 1)
                dve.wait_ge(evacuated, len(lots))
                c.go(nc.vector.memset(a["key"][:, W:], 0.0))
                c.go(nc.vector.memset(a["hi"][:, W:], 0.0))
                c.go(nc.vector.memset(a["lo"][:, W:], 0.0))
                pay = a["pay"][:, :].rearrange("p (t c) -> p t c", c=4)
                c.step(nc.vector.tensor_scalar(pay[:, :, 0], a["key"][:, 0:W], float(s.PAD), FAR, ALU.is_ge, ALU.mult))
                c.go(nc.vector.tensor_tensor(pay[:, :, 0], pay[:, :, 0], a["key"][:, 0:W], ALU.add))
                c.go(nc.vector.memset(pay[:, :, 3], 0.0))
                if wf is None:
                    c.go(nc.vector.memset(pay[:, :, 2], 0.0))
                if not z.LT:
                    dve.wait_ge(nxt_in, 16)
                    c.step(nc.vector.tensor_tensor(nxt[:, :], nxt[:, :], kf[:, :], ALU.is_lt))
                    nc.vector.tensor_reduce(bad[:, :], nxt[:, :], AX, ALU.add).then_inc(bad_made, 1)
                    dve.wait_ge(bad_sum, 1)
                    c.step(nc.vector.tensor_copy(a["disorder"][:, :], bps[0:1, :]))
                c.step(nc.vector.tensor_copy(lo_i[:, :], a["key"][:, 0:W]))
                c.go(nc.vector.tensor_single_scalar(hi_i[:, :], lo_i[:, :], 7, ALU.arith_shift_right))
                c.step(nc.vector.tensor_single_scalar(lo_i[:, :], lo_i[:, :], P - 1, ALU.bitwise_and))
                c.go(nc.vector.tensor_copy(a["hi"][:, 0:W], hi_i[:, :]))
                c.step(nc.vector.tensor_copy(a["lo"][:, 0:W], lo_i[:, :]))

            @block.tensor
            def _(pe):
                pe.wait_ge(rows_ready, 1)
                for n, (src, c0, col, _) in enumerate(lots):
                    if n >= 2:
                        pe.wait_ge(evacuated, n - 1)
                    for c in range(c0, min(c0 + 4, z.C)):
                        last = nc.tensor.transpose(tps[n % 2][:, (c - c0) * P:(c - c0 + 1) * P],
                                                   src[:, c * P:(c + 1) * P], k["ident"][:, :])
                    last.then_inc(turned, 1)
                if not z.LT:
                    pe.wait_ge(bad_made, 1)
                    nc.tensor.matmul(bps[:, :], k["ones"][:, :], bad[:, :], start=True, stop=True).then_inc(bad_sum, 1)


def one_hot(nc, k, out, n, values, t0):
    return nc.vector.tensor_tensor(out[:, :].rearrange("p (v t) -> p v t", t=8),
                                   k["iota_8"][:, 0:8 * n].rearrange("p (v t) -> p v t", t=8),
                                   values[:, bass.ds(t0, 8)].unsqueeze(1).broadcast_to([P, n, 8]), ALU.is_equal)


def of_tile(t, j):
    return t[:, :].rearrange("p (v t) -> p v t", t=8)[:, :, j]


class Histogram:

    def __init__(self, nc, s, k, a, sb, ps, sem, tag):
        self.nc, self.s, self.k, self.a = nc, s, k, a
        self.lo1 = [sb(f"lo1_{u}" + tag, 8 * P, BF16) for u in range(2)]
        self.hi1 = [sb(f"hi1_{u}" + tag, 8 * s.NB1, BF16) for u in range(2)]
        self.hist = ps("hist" + tag, s.NB1)
        self.made = [sem(f"onehot_made{u}") for u in range(2)]
        self.used = [sem(f"onehot_used{u}") for u in range(2)]
        self.done, self.out = sem("hist_done"), sem("hist_out")

    def vector_start(self, dve):
        for u in range(2):
            dve.sem_inc(self.used[u], 1)

    def vector_half(self, dve, i, u):
        t0 = (i - 1) * 16 + u * 8
        dve.wait_ge(self.used[u], i)
        one_hot(self.nc, self.k, self.lo1[u], P, self.a["lo"], t0)
        one_hot(self.nc, self.k, self.hi1[u], self.s.NB1, self.a["hi"], t0).then_inc(self.made[u], 1)

    def vector_end(self, dve):
        dve.wait_ge(self.done, 1)
        self.nc.vector.tensor_copy(self.a["counts"][:, :], self.hist[:, :]).then_inc(self.out, 1)
        dve.wait_ge(self.out, 1)

    def tensor_start(self):
        zero = self.k["zero"]
        self.nc.tensor.matmul(self.hist[:, :], zero[:, :], zero[:, 0:self.s.NB1], start=True, stop=False)

    def tensor_half(self, pe, i, u):
        pe.wait_ge(self.made[u], i)
        for j in range(8):
            last = self.nc.tensor.matmul(self.hist[:, :], of_tile(self.lo1[u], j), of_tile(self.hi1[u], j), start=False, stop=False)
        last.then_inc(self.used[u], 1)

    def tensor_end(self):
        zero = self.k["zero"]
        self.nc.tensor.matmul(self.hist[:, :], zero[:, :], zero[:, 0:self.s.NB1], start=False, stop=True).then_inc(self.done, 1)


def phase_histogram(nc, s, z, k, a, tag):
    with ExitStack() as ctx:
        h = Histogram(nc, s, k, a, *scope(nc, ctx, k), tag)
        n = z.TT // 16
        with nc.Block() as block:
            @block.vector
            def _(dve):
                h.vector_start(dve)
                with dve.Fori(1, n + 1) as i:
                    for u in range(2):
                        h.vector_half(dve, i, u)
                h.vector_end(dve)

            @block.tensor
            def _(pe):
                h.tensor_start()
                with pe.Fori(1, n + 1) as i:
                    for u in range(2):
                        h.tensor_half(pe, i, u)
                h.tensor_end()


def phase_offsets(nc, s, z, k, a, L, tag):
    with ExitStack() as ctx:
        sb, ps, sem = scope(nc, ctx, k)
        NB1 = s.NB1
        bc, inc, cstart = sb("bc" + tag, NB1), sb("inc" + tag, NB1), sb("cstart" + tag, NB1)
        gi, gc, gend, shift = sb("gi" + tag, NB1, I32), sb("gc" + tag, NB1), sb("gend" + tag, NB1), sb("shift" + tag, NB1)
        gid_i, gid = sb("gid_i" + tag, z.GC, I32), sb("gid" + tag, z.GC)
        m, run, run_i = sb("m" + tag, NB1), sb("run" + tag, NB1), sb("run_i" + tag, NB1, I32)
        gb = sb("gb" + tag, z.GC)
        diag = sb("diag" + tag, z.GC * P)
        np_i = sb("np_i" + tag, 1, I32)
        far = sb("far" + tag, z.NGS * 4 * G) if z.LT else None
        far_set, far_out = sem("far_set"), sem("far_out")
        p1 = ps("p1" + tag, 2 * NB1)
        pb = ps("pb" + tag, z.GC * P)
        step, sums, gid_done, diag_done, spread = (sem(x) for x in ("off_step", "sums", "gid_done", "diag_done", "spread"))
        with nc.Block() as block:
            @block.gpsimd
            def _(pool):
                nc.gpsimd.iota(gid_i[:, :], pattern=[[P, z.GC]], base=0, channel_multiplier=1).then_inc(gid_done, 1)

            @block.sync
            def _(sp):
                if z.LT:
                    sp.wait_ge(far_set, 1)
                    sp.dma_start(a["rows"][0:z.NGS * GE, :].rearrange("(p m) c -> p (m c)", p=P), far[:, :]).then_inc(far_out, 16)
                    sp.wait_ge(far_out, 16)

            @block.tensor
            def _(pe):
                nc.tensor.matmul(p1[:, 0:NB1], k["ones"][:, :], a["counts"][:, :], start=True, stop=True)
                nc.tensor.matmul(p1[:, NB1:2 * NB1], k["after"][:, :], a["counts"][:, :], start=True, stop=True).then_inc(sums, 1)
                pe.wait_ge(diag_done, 1)
                for c in range(z.GC):
                    last = nc.tensor.matmul(pb[:, c * P:(c + 1) * P], k["ones"][:, :], diag[:, c * P:(c + 1) * P],
                                            start=True, stop=True)
                last.then_inc(spread, 1)

            @block.vector
            def _(dve):
                c = Chain(dve, step)
                if z.LT:
                    nc.vector.memset(far[:, :], FAR).then_inc(far_set, 1)
                dve.wait_ge(sums, 1)
                c.step(nc.vector.tensor_copy(bc[:, :], p1[:, 0:NB1]))
                c.step(nc.vector.tensor_tensor_scan(inc[:, :], k["ones"][:, 0:NB1], bc[:, :], 0.0, ALU.mult, ALU.add))
                c.step(nc.vector.tensor_tensor(cstart[:, :], inc[:, :], bc[:, :], ALU.subtract))
                c.step(nc.vector.tensor_scalar(inc[:, :], bc[:, :], float(GE - 1), None, ALU.add))
                c.step(nc.vector.tensor_copy(gi[:, :], inc[:, :]))
                c.step(nc.vector.tensor_single_scalar(gi[:, :], gi[:, :], GE.bit_length() - 1, ALU.arith_shift_right))
                c.step(nc.vector.tensor_copy(gc[:, :], gi[:, :]))
                c.step(nc.vector.memset(gc[:, s.NB:], 0.0))
                c.step(nc.vector.tensor_tensor_scan(gend[:, :], k["ones"][:, 0:NB1], gc[:, :], 0.0, ALU.mult, ALU.add))
                c.step(nc.vector.tensor_scalar(m[:, 0:1], gend[:, NB1 - 1:NB1], float(U - 1), None, ALU.add))
                c.step(nc.vector.tensor_copy(np_i[:, :], m[:, 0:1]))
                c.step(nc.vector.tensor_single_scalar(L["rounds"][:, :], np_i[:, :], U.bit_length() - 1, ALU.arith_shift_right))
                c.step(nc.vector.tensor_tensor(shift[:, :], gend[:, :], gc[:, :], ALU.subtract))
                if z.LT:
                    c.step(nc.vector.tensor_scalar(cstart[:, :], shift[:, :], float(GE), None, ALU.mult))
                c.step(nc.vector.tensor_tensor(a["first"][:, :], cstart[:, :], p1[:, NB1:2 * NB1], ALU.add))
                if not z.LT:
                    c.step(nc.vector.tensor_copy(gi[:, :], gc[:, :]))
                    c.go(nc.vector.tensor_single_scalar(run_i[:, :], gi[:, :], RUN.bit_length() - 1, ALU.arith_shift_right))
                    c.step(nc.vector.tensor_single_scalar(gi[:, :], gi[:, :], RUN - 1, ALU.bitwise_and))
                    c.go(nc.vector.tensor_copy(run[:, :], run_i[:, :]))
                    c.step(nc.vector.tensor_copy(m[:, :], gi[:, :]))
                    for row, value in enumerate((cstart, shift, run, m)):
                        c.step(nc.vector.tensor_copy(a["block_rows"][:, row * NB1:(row + 1) * NB1], value[0:1, :]))
                    c.step(nc.vector.tensor_tensor(run[:, :], run[:, :], m[:, :], ALU.add))
                    c.go(nc.vector.tensor_reduce(m[:, 0:1], run[:, 0:s.NB // 2], AX, ALU.add))
                    c.step(nc.vector.tensor_reduce(m[:, 1:2], run[:, s.NB // 2:], AX, ALU.add))
                    c.step(nc.vector.tensor_copy(a["block_rows"][:, 4 * NB1:], m[0:1, 0:2]))
                dve.wait_ge(gid_done, 1)
                c.step(nc.vector.tensor_copy(gid[:, :], gid_i[:, :]))
                for q in range(z.GC):
                    c.step(nc.vector.tensor_scalar(m[:, 0:s.NB], gend[:, 0:s.NB], gid[:, q:q + 1], None, ALU.is_le))
                    c.step(nc.vector.tensor_reduce(gb[:, q:q + 1], m[:, 0:s.NB], AX, ALU.add))
                for q in range(z.GC):
                    c.step(nc.vector.tensor_scalar(diag[:, q * P:(q + 1) * P], k["ident"][:, :], gb[:, q:q + 1], None, ALU.mult))
                dve.sem_inc(diag_done, 1)
                dve.wait_ge(spread, 1)
                c.go(nc.vector.tensor_copy(a["gblock"][:, :], pb[:, 0:z.NGS]))
                c.step(nc.vector.tensor_copy(L["block"][:, :], pb[0:1, 0:z.NGS]))


def phase_positions(nc, s, z, k, a, tag, counted=None):
    with ExitStack() as ctx:
        sb, ps, sem = scope(nc, ctx, k)
        tally = Histogram(nc, s, k, counted, sb, ps, sem, tag + "c") if counted else None
        NB1 = s.NB1
        lo1 = [sb(f"q_lo1_{u}" + tag, 8 * P, BF16) for u in range(2)]
        hi1 = [sb(f"q_hi1_{u}" + tag, 8 * NB1, BF16) for u in range(2)]
        lo1T = [sb(f"q_lo1T_{h}" + tag, 4 * P) for h in range(2)]
        krow = [sb(f"krow{h}" + tag, 4 * P) for h in range(4)]
        same = [sb(f"same{h}" + tag, 16 * P, BF16) for h in range(4)]
        rank = [sb(f"rank{h}" + tag, 4) for h in range(4)]
        sel, base = [sb(f"sel{h}" + tag, 4 * NB1) for h in range(2)], [sb(f"base{h}" + tag, 4) for h in range(2)]
        pos = [sb(f"pos{h}" + tag, 4, U32) for h in range(4)]
        rowp = [sb(f"rowp{h}" + tag, 16) for h in range(4)]
        snap = [sb(f"snap{h}" + tag, NB1) for h in range(2)]
        tail = sb("tail" + tag, 4)
        cnt = [ps(f"cnt{h}" + tag, NB1) for h in range(2)]
        tp = [ps(f"q_tp{h}" + tag, 4 * P, BF16) for h in range(2)]
        look = [ps(f"look{h}" + tag, 4 * NB1) for h in range(2)]
        lots = range(4)
        S = {n: [sem(f"{n}{h}") for h in lots] for n in ("krow_in", "oh_turned", "oh_copied", "looked", "counted", "summed", "pos_ready", "ranked")}
        made = [sem(f"q_made{u}") for u in range(2)]
        scattered = [sem(f"scattered{h}" + tag, own=True) for h in lots]
        snapped, tail_set, scatter_go = sem("snapped"), sem("tail_set"), sem("scatter_go")
        n = z.TT // 16

        def if_needed(eng):
            if z.LT:
                return ExitStack()
            return eng.If(eng.value_load(a["disorder"][0:1, 0:1], min_val=0, max_val=z.rows) > 0)

        with nc.Block() as block:
            @block.sync
            def _(sp):
                with if_needed(sp), sp.Fori(1, n + 2) as i:
                    for h in lots:
                        sp.wait_ge(S["ranked"][h], i)
                        src = a["keyrow"][bass.ds((i - 1) * 16 * P + h * 4 * P, 4 * P)]
                        sp.dma_start(krow[h][:, :], src.rearrange("(o l) -> o l", o=1).broadcast_to([P, 4 * P])).then_inc(S["krow_in"][h], 16)

            @block.vector
            def _(dve):
                def build(i, u):
                    t0 = (i - 1) * 16 + u * 8
                    for h in (2 * u, 2 * u + 1):
                        dve.wait_ge(S["looked"][h], i)
                    one_hot(nc, k, lo1[u], P, a["lo"], t0)
                    one_hot(nc, k, hi1[u], NB1, a["hi"], t0).then_inc(made[u], 1)
                    for h in (2 * u, 2 * u + 1):
                        dve.wait_ge(S["krow_in"][h], i * 16)
                        for j in range(4):
                            t = t0 + (h % 2) * 4 + j
                            last = nc.vector.scalar_tensor_tensor(
                                out=same[h][:, j * 4 * P:(j * 4 + j + 1) * P], in0=krow[h][:, 0:(j + 1) * P],
                                scalar=a["key"][:, bass.ds(t, 1)], in1=k["before"][:, (3 - j) * P:],
                                op0=ALU.is_equal, op1=ALU.mult, accum_out=rank[h][:, j:j + 1])
                        last.then_inc(S["ranked"][h], 1)

                def select(i, h):
                    dve.wait_ge(S["counted"][h], i)
                    dve.wait_ge(snapped, 4 * (i - 1) + h + 1)
                    nc.vector.tensor_tensor(snap[(h + 1) % 2][:, :], snap[h % 2][:, :], cnt[h % 2][:, :], ALU.add).then_inc(snapped, 1)
                    dve.wait_ge(S["looked"][h], i + 1)
                    v = h % 2
                    nc.vector.tensor_tensor(sel[v][:, :].rearrange("p (j b) -> p j b", j=4), look[v][:, :].rearrange("p (j b) -> p j b", j=4),
                                            hi1[h // 2][:, :].rearrange("p (b t) -> p t b", t=8)[:, v * 4:v * 4 + 4, :], ALU.mult
                                            ).then_inc(S["summed"][h], 1)

                def total(i, h):
                    v = h % 2
                    dve.wait_ge(S["summed"][h], i * 3 - 2)
                    nc.vector.tensor_reduce(base[v][:, :], sel[v][:, :].rearrange("p (j b) -> p j b", j=4), AX, ALU.add
                                            ).then_inc(S["summed"][h], 1)

                def add_rank(i, h):
                    v = h % 2
                    dve.wait_ge(S["summed"][h], i * 3 - 1)
                    dve.wait_ge(S["ranked"][h], i + 1)
                    nc.vector.tensor_tensor(base[v][:, :], base[v][:, :], rank[h][:, :], ALU.add).then_inc(S["summed"][h], 1)

                def hand_out(i, h):
                    t0 = (i - 1) * 16 + h * 4
                    dve.wait_ge(S["summed"][h], i * 3)
                    dve.wait_ge(scattered[h], (i - 1) * 64 + 16)
                    nc.vector.tensor_copy(rowp[h][:, :], a["pay"][:, bass.ds(t0 * 4, 16)])
                    nc.vector.tensor_copy(pos[h][:, :], base[h % 2][:, :]).then_inc(S["pos_ready"][h], 1)

                with if_needed(dve):
                    for h in lots:
                        dve.sem_inc(S["ranked"][h], 1)
                        dve.sem_inc(S["looked"][h], 1)
                    nc.vector.memset(tail[:, :], FAR).then_inc(tail_set, 1)
                    nc.vector.tensor_copy(snap[0][:, :], a["first"][:, :]).then_inc(snapped, 1)
                    build(1, 0)
                    build(1, 1)
                    if counted:
                        tally.vector_start(dve)
                    with dve.Fori(1, n + 1) as i:
                        for u in range(2):
                            h0, h1 = 2 * u, 2 * u + 1
                            select(i, h0)
                            if counted:
                                tally.vector_half(dve, i, u)
                            total(i, h0)
                            select(i, h1)
                            add_rank(i, h0)
                            total(i, h1)
                            hand_out(i, h0)
                            add_rank(i, h1)
                            hand_out(i, h1)
                            build(i + 1, u)
                    if counted:
                        tally.vector_end(dve)

            @block.gpsimd
            def _(pool):
                with if_needed(pool):
                    pool.wait_ge(tail_set, 1)
                    for h in lots:
                        at = a["rows"].shape[0] - (h + 1) * P
                        nc.gpsimd.dma_start(a["rows"][at:at + P, :], tail[:, :]).then_inc(scattered[h], 16)
                    with pool.Fori(1, n + 1) as i:
                        for h in lots:
                            pool.wait_ge(S["pos_ready"][h], i)
                            pool.sem_inc(scatter_go, 1)
                            for j in range(4):
                                nc.gpsimd.indirect_dma_start(a["rows"], bass.IndirectOffsetOnAxis(ap=pos[h][:, j:j + 1], axis=0),
                                                             rowp[h][:, j * 4:j * 4 + 4], None).then_inc(scattered[h], 16)
                    for h in lots:
                        pool.wait_ge(scattered[h], n * 64 + 16)
                    pool.sem_inc(scatter_go, 1)

            @block.tensor
            def _(pe):
                with if_needed(pe):
                    if counted:
                        tally.tensor_start()
                    with pe.Fori(1, n + 1) as i:
                        for h in lots:
                            u, v = h // 2, h % 2
                            pe.wait_ge(made[u], i)
                            for j in range(4):
                                last = nc.tensor.transpose(tp[v][:, j * P:(j + 1) * P], of_tile(lo1[u], v * 4 + j), k["ident_b"][:, :])
                            last.then_inc(S["oh_turned"][h], 1)
                            for j in range(4):
                                last = nc.tensor.matmul(cnt[v][:, :], of_tile(lo1[u], v * 4 + j), of_tile(hi1[u], v * 4 + j),
                                                        start=(j == 0), stop=(j == 3))
                            last.then_inc(S["counted"][h], 1)
                            pe.wait_ge(S["oh_copied"][h], i)
                            pe.wait_ge(snapped, 4 * (i - 1) + h + 1)
                            for j in range(4):
                                last = nc.tensor.matmul(look[v][:, j * NB1:(j + 1) * NB1], lo1T[v][:, j * P:(j + 1) * P],
                                                        snap[v][:, :], start=True, stop=True)
                            last.then_inc(S["looked"][h], 1)
                            if counted and v == 1:
                                tally.tensor_half(pe, i, u)
                    if counted:
                        tally.tensor_end()

            @block.scalar
            def _(act):
                with if_needed(act), act.Fori(1, n + 1) as i:
                    for h in lots:
                        act.wait_ge(S["oh_turned"][h], i)
                        nc.scalar.copy(lo1T[h % 2][:, :], tp[h % 2][:, :]).then_inc(S["oh_copied"][h], 1)


def rounds_of(eng, L, z):
    return eng.value_load(L["rounds"][0:1, 0:1], min_val=max(1, z.GMIN // U), max_val=z.NGS // U)


def phase_lists(nc, s, z, k, a, L, tag):
    with ExitStack() as ctx:
        sb, ps, sem = scope(nc, ctx, k)
        raw = sb("raw" + tag, z.NGS * 4 * G)
        base, vld, ofs = sb("lbase" + tag, z.NGS), sb("vld" + tag, z.NGS * G), sb("ofs" + tag, z.NGS * G)
        raw_clear, raw_in, raw_in2, step = sem("raw_clear"), sem("raw_in"), sem("raw_in2"), sem("list_step")
        r4 = raw[:, :].rearrange("p (g j c) -> p g j c", j=G, c=4)

        def pgj(t):
            return t[:, :].rearrange("p (g j) -> p g j", j=G)
        with nc.Block() as block:
            def load_blocks(eng, first, end, landed):
                def entry(row, b):
                    return eng.value_load(a["block_rows"][0:1, bass.ds(b + row * s.NB1, 1)], min_val=0, max_val=z.rows)
                def load(group, row, n):
                    group = group.with_bounds(min_val=0, max_val=z.NGS - n)
                    row = row.with_bounds(min_val=0, max_val=z.rows)
                    eng.dma_start(raw[:, bass.ds(group * 4 * G, n * 4 * G)].rearrange("p (c x) -> p c x", c=n),
                                  a["rows"][bass.ds(row, n * GE), :].rearrange("(c p j) x -> p c (j x)", p=P, j=G)).then_inc(landed, 16)
                eng.sem_inc(landed, 16)
                with eng.Fori(first, end) as b:
                    row0, group0, runs, singles = (entry(row, b) for row in range(4))
                    with eng.If(runs > 0), eng.Fori(0, runs) as r:
                        load(group0 + r * RUN, row0 + r * (RUN * GE), RUN)
                    with eng.If(singles > 0), eng.Fori(0, singles) as g:
                        load(group0 + runs * RUN + g, row0 + (runs * RUN + g) * GE, 1)
                n = entry(4, 0 if first == 0 else 1)
                eng.wait_ge(landed, n * 16 + 16)
                eng.sem_inc(raw_clear, 1)

            @block.sync
            def _(sp):
                sp.wait_ge(raw_clear, 1)
                if z.LT:
                    sp.dma_start(raw[:, :].rearrange("p (g x) -> p g x", x=4 * G),
                                 a["rows"][0:z.NGS * GE, :].rearrange("(g p j) c -> p g (j c)", p=P, j=G)).then_inc(raw_in, 16)
                    sp.wait_ge(raw_in, 16)
                    sp.sem_inc(raw_clear, 2)
                else:
                    load_blocks(sp, 0, s.NB // 2, raw_in)

            @block.scalar
            def _(act):
                if not z.LT:
                    act.wait_ge(raw_clear, 1)
                    load_blocks(act, s.NB // 2, s.NB, raw_in2)

            @block.vector
            def _(dve):
                c = Chain(dve, step)
                nc.vector.memset(raw[:, :], 0.0).then_inc(raw_clear, 1)
                c.step(nc.vector.tensor_scalar(base[:, :], a["gblock"][:, :], float(P), None, ALU.mult))
                dve.wait_ge(raw_clear, 3)
                c.step(nc.vector.tensor_tensor(pgj(L["place"]), r4[:, :, :, 0], base[:, :].unsqueeze(2).broadcast_to([P, z.NGS, G]),
                                               ALU.subtract))
                c.step(nc.vector.tensor_scalar(vld[:, :], L["place"][:, :], 0.0, None, ALU.is_ge))
                c.step(nc.vector.scalar_tensor_tensor(out=vld[:, :], in0=L["place"][:, :], scalar=float(P), in1=vld[:, :],
                                                      op0=ALU.is_lt, op1=ALU.mult))
                c.step(nc.vector.tensor_scalar(pgj(ofs), r4[:, :, :, 1], -float(s.ZROW), None, ALU.add))
                c.step(nc.vector.tensor_tensor(ofs[:, :], ofs[:, :], vld[:, :], ALU.mult))
                c.step(nc.vector.tensor_scalar(ofs[:, :], ofs[:, :], float(s.ZROW), None, ALU.add))
                c.step(nc.vector.tensor_copy(L["gather"][:, 0:z.NGS * G], ofs[:, :]))
                c.step(nc.vector.memset(L["gather"][:, z.NGS * G:], 0))
                if "weight" in L:
                    c.step(nc.vector.tensor_copy(pgj(L["weight"]), r4[:, :, :, 2]))
                if "segment" in L:
                    c.step(nc.vector.tensor_tensor(pgj(ofs), r4[:, :, :, 0], pgj(vld), ALU.mult))
                    c.step(nc.vector.tensor_tensor(ofs[:, :], ofs[:, :], vld[:, :], ALU.add))
                    c.step(nc.vector.tensor_scalar(L["segment"][:, :], ofs[:, :], -1.0, None, ALU.add))


def sort_state(nc, s, z, ctx, L, tag):
    def sb(name, cols, dt=F32, parts=P):
        return ctx.enter_context(nc.sbuf_tensor(name + tag, [parts, cols], dt))
    W = z.C * P
    return dict(counts=L["counts"], first=sb("first", s.NB1), gblock=sb("gblock", z.NGS), block_rows=sb("block_rows", 4 * s.NB1 + 2, I32, 1),
                rows=nc.dram_tensor("rows" + tag, [max(z.NGS * GE, W * P) + 16 * P + GE, 4], F32).ap(),
                disorder=sb("disorder", 1, I32, 1),
                keyrow=nc.dram_tensor("keyrow" + tag, [W * P + 16 * P], F32).ap())


def sort_arrays(nc, z, ctx, a, tag):
    W = z.C * P
    for name, cols, dt in (("key", W + 16, F32), ("hi", W + 16, BF16), ("lo", W + 16, BF16), ("pay", W * 4, F32)):
        a[name] = ctx.enter_context(nc.sbuf_tensor(name + tag, [P, cols], dt))


def phase_load(nc, k, loads, name):
    with ExitStack() as ctx:
        sb, ps, sem = scope(nc, ctx, k)
        loaded = sem("small_loaded")
        with nc.Block() as block:
            @block.sync
            def _(sp):
                for dst, src in loads:
                    sp.dma_start(dst, src).then_inc(loaded, 16)
                sp.wait_ge(loaded, 16 * len(loads))


def phase_dense(nc, s, k, src, weights, bias, outs, tag):
    F = weights.shape[1]
    with ExitStack() as ctx:
        sb, ps, sem = scope(nc, ctx, k)
        xb = [sb(f"d_xb{u}" + tag, D) for u in range(2)]
        xT = [sb(f"d_xT{u}" + tag, D) for u in range(2)]
        tps = [ps(f"d_tps{u}" + tag, P) for u in range(2)]
        ops = [ps(f"d_ops{u}" + tag, F) for u in range(2)]
        S = {n: [sem(f"d_{n}{u}") for u in range(2)] for n in ("copied", "turned", "xT_ready", "product", "evacuated")}
        n = s.NB1 // 2
        with nc.Block() as block:
            @block.vector
            def _(dve):
                for u in range(2):
                    dve.sem_inc(S["turned"][u], 1)
                    dve.sem_inc(S["product"][u], 1)
                with dve.Fori(1, n + 1) as i:
                    for u in range(2):
                        dve.wait_ge(S["turned"][u], i)
                        nc.vector.tensor_copy(xb[u][:, :], src[:, bass.ds(((i - 1) * 2 + u) * D, D)]).then_inc(S["copied"][u], 1)
                    for u in range(2):
                        dve.wait_ge(S["turned"][u], i + 1)
                        dve.wait_ge(S["product"][u], i)
                        nc.vector.tensor_copy(xT[u][:, :], tps[u][:, :]).then_inc(S["xT_ready"][u], 1)

            @block.tensor
            def _(pe):
                with pe.Fori(1, n + 1) as i:
                    for u in range(2):
                        pe.wait_ge(S["copied"][u], i)
                        nc.tensor.transpose(tps[u][:, :], xb[u][:, :], k["ident"][:, :]).then_inc(S["turned"][u], 1)
                    for u in range(2):
                        pe.wait_ge(S["xT_ready"][u], i)
                        pe.wait_ge(S["evacuated"][u], i)
                        last = nc.tensor.matmul(ops[u][:, :], xT[u][:, :], weights[:, :], start=True, stop=bias is None)
                        if bias is not None:
                            last = nc.tensor.matmul(ops[u][:, :], k["ones"][0:1, :], bias[0:1, :], start=False, stop=True)
                        last.then_inc(S["product"][u], 1)

            @block.scalar
            def _(act):
                for u in range(2):
                    act.sem_inc(S["evacuated"][u], 1)
                with act.Fori(1, n + 1) as i:
                    for u in range(2):
                        act.wait_ge(S["product"][u], i + 1)
                        for c0, c1, func, dest in outs:
                            last = nc.scalar.activation(dest((i - 1) * 2 + u), ops[u][:, c0:c1], func)
                        last.then_inc(S["evacuated"][u], 1)


def phase_split_and_store(nc, k, src, parts, pairs):
    with ExitStack() as ctx:
        sb, ps, sem = scope(nc, ctx, k)
        step, stored = sem("split_step"), sem("tables_stored")
        with nc.Block() as block:
            @block.sync
            def _(sp):
                store_tables(sp, pairs, stored)

            @block.vector
            def _(dve):
                c = Chain(dve, step)
                for n, part in enumerate(parts):
                    c.step(nc.vector.tensor_copy(part[:, :], src[:, :]))
                    if n < 2:
                        c.step(nc.vector.tensor_tensor(src[:, :], src[:, :], part[:, :], ALU.subtract))


def store_tables(sp, pairs, stored):
    for table, tile, F in pairs:
        sp.dma_start(table.rearrange("(b p) f -> p b f", p=P), tile[:, :].rearrange("p (b f) -> p b f", f=F)).then_inc(stored, 16)
    sp.wait_ge(stored, 16 * len(pairs))


def phase_store(nc, k, pairs):
    with ExitStack() as ctx:
        sb, ps, sem = scope(nc, ctx, k)
        stored = sem("table_stored")
        with nc.Block() as block:
            @block.sync
            def _(sp):
                store_tables(sp, pairs, stored)


def over_blocks(row, s):
    return row.unsqueeze(1).broadcast_to([P, s.NB1, row.shape[1]])


def blocks(t, f=D):
    return t[:, :].rearrange("p (b f) -> p b f", f=f)


def phase_layernorm(nc, s, k, y, tag):
    with ExitStack() as ctx:
        sb, ps, sem = scope(nc, ctx, k)
        sq, m, sd, rs = sb("ln_sq" + tag, s.NB1 * D), sb("ln_m" + tag, s.NB1), sb("ln_sd" + tag, s.NB1), sb("ln_rs" + tag, s.NB1)
        step, centred, squared, var_ready, sd_ready = sem("ln_step"), sem("ln_centred"), sem("ln_squared"), sem("ln_var"), sem("ln_sd")
        with nc.Block() as block:
            @block.vector
            def _(dve):
                c = Chain(dve, step)
                c.step(nc.vector.tensor_reduce(m[:, :], blocks(y), AX, ALU.add))
                c.step(nc.vector.tensor_scalar(m[:, :], m[:, :], 1.0 / D, None, ALU.mult))
                nc.vector.tensor_tensor(blocks(y), blocks(y), m[:, :].unsqueeze(2).broadcast_to([P, s.NB1, D]),
                                        ALU.subtract).then_inc(centred, 1)
                dve.wait_ge(squared, 1)
                c.step(nc.vector.tensor_reduce(m[:, :], blocks(sq), AX, ALU.add))
                nc.vector.tensor_scalar(m[:, :], m[:, :], 1.0 / D, EPS, ALU.mult, ALU.add).then_inc(var_ready, 1)
                dve.wait_ge(sd_ready, 1)
                c.step(nc.vector.reciprocal(rs[:, :], sd[:, :]))
                c.step(nc.vector.tensor_tensor(blocks(k["x"]), blocks(y), rs[:, :].unsqueeze(2).broadcast_to([P, s.NB1, D]), ALU.mult))
                c.step(nc.vector.memset(k["x"][:, s.NB * D:], 0.0))

            @block.scalar
            def _(act):
                act.wait_ge(centred, 1)
                nc.scalar.activation(sq[:, :], y[:, :], ACT.Square).then_inc(squared, 1)
                act.wait_ge(var_ready, 1)
                nc.scalar.activation(sd[:, :], m[:, :], ACT.Sqrt).then_inc(sd_ready, 1)


def set_index(nc, L, idx, i, u):
    return nc.vector.tensor_copy(idx[u][:, :], L["gather"][:, bass.ds(((i - 1) * U + u) * G, G)])


def phase_scores(nc, s, z, k, L, Q, att, table, v_dram, att_dram):
    with ExitStack() as ctx:
        sb, ps, sem = scope(nc, ctx, k)
        R = range(U)
        kv = [sb(f"kv{u}", G * 2 * D) for u in R]
        vs = [sb(f"vs{u}", G * D) for u in R]
        oh = [sb(f"s_oh{u}", G * P, BF16) for u in R]
        ohT = [sb(f"s_ohT{u}", G * P, BF16) for u in R]
        idx = [sb(f"s_idx{u}", G, U32) for u in R]
        prod = [sb(f"prod{u}", G * D) for u in R]
        tps = [ps(f"s_tps{u}", G * P, BF16) for u in range(2)]
        qps = [ps(f"qps{u}", G * D) for u in R]
        landed = [sem(f"kv_landed{u}", own=True) for u in R]
        S = {n: [sem(f"s_{n}{u}") for u in R] for n in
             ("idx_set", "oh_made", "oh_turned", "oh_copied", "q_ready", "prod_made", "att_made", "v_copied", "v_free", "stored")}
        go, cleared, zeroed = sem("s_go"), sem("s_cleared"), sem("s_zeroed")
        with nc.Block() as block:
            @block.gpsimd
            def _(pool):
                n = rounds_of(pool, L, z)
                with pool.Fori(1, n + 1) as i:
                    for u in R:
                        pool.wait_ge(S["prod_made"][u], i)
                        pool.wait_ge(S["v_copied"][u], i)
                        pool.wait_ge(S["idx_set"][u], i)
                        pool.sem_inc(go, 1)
                        for j in range(G):
                            nc.gpsimd.indirect_dma_start(kv[u][:, j * 2 * D:(j + 1) * 2 * D], None, table,
                                                         bass.IndirectOffsetOnAxis(ap=idx[u][:, j:j + 1], axis=0)).then_inc(landed[u], 16)

            @block.vector
            def _(dve):
                nc.vector.memset(att[:, :], 0.0).then_inc(cleared, 1)
                dve.wait_ge(cleared, 1)
                n = rounds_of(dve, L, z)
                for u in R:
                    dve.sem_inc(S["prod_made"][u], 1)
                    dve.sem_inc(S["oh_turned"][u], 1)
                    dve.sem_inc(S["att_made"][u], 1)
                    set_index(nc, L, idx, 1, u).then_inc(S["idx_set"][u], 1)
                dve.wait_ge(zeroed, 16)
                with dve.Fori(1, n + 1) as i:
                    for u in R:
                        g = (i - 1) * U + u
                        dve.wait_ge(S["oh_turned"][u], i)
                        for j in range(G):
                            last = nc.vector.tensor_scalar(oh[u][:, j * P:(j + 1) * P], k["iota_f"][:, :],
                                                           L["place"][:, bass.ds(g * G + j, 1)], None, ALU.is_equal)
                        last.then_inc(S["oh_made"][u], 1)
                    for u in R:
                        g = (i - 1) * U + u
                        dve.wait_ge(S["q_ready"][u], i)
                        dve.wait_ge(landed[u], i * 16 * G)
                        set_index(nc, L, idx, i + 1, u).then_inc(S["idx_set"][u], 1)
                        dve.wait_ge(S["att_made"][u], i)
                        kk = kv[u][:, :].rearrange("p (j c) -> p j c", j=G)[:, :, 0:D]
                        nc.vector.tensor_tensor(prod[u][:, :].rearrange("p (j c) -> p j c", j=G),
                                                qps[u][:, :].rearrange("p (j c) -> p j c", j=G), kk, ALU.mult
                                                ).then_inc(S["prod_made"][u], 1)
                        dve.wait_ge(S["prod_made"][u], i + 1)
                        nc.vector.tensor_reduce(att[:, bass.ds(g * G * H, G * H)],
                                                prod[u][:, :].rearrange("p (m d) -> p m d", d=HD), AX, ALU.add
                                                ).then_inc(S["att_made"][u], 1)

            @block.tensor
            def _(pe):
                n = rounds_of(pe, L, z)
                with pe.Fori(1, n + 1) as i:
                    for u in R:
                        pe.wait_ge(S["oh_made"][u], i)
                        if u >= 2:
                            pe.wait_ge(S["oh_copied"][u - 2], i)
                        for j in range(G):
                            last = nc.tensor.transpose(tps[u % 2][:, j * P:(j + 1) * P], oh[u][:, j * P:(j + 1) * P], k["ident_b"][:, :])
                        last.then_inc(S["oh_turned"][u], 1)
                    for u in R:
                        b = pe.value_load(L["block"][0:1, bass.ds((i - 1) * U + u, 1)], min_val=0, max_val=s.NB)
                        pe.wait_ge(S["oh_copied"][u], i)
                        pe.wait_ge(S["prod_made"][u], i)
                        for j in range(G):
                            for q in range(3):
                                last = nc.tensor.matmul(qps[u][:, j * D:(j + 1) * D], ohT[u][:, j * P:(j + 1) * P],
                                                        Q[q][:, bass.ds(b * D, D)], start=(q == 0), stop=(q == 2))
                        last.then_inc(S["q_ready"][u], 1)

            @block.scalar
            def _(act):
                n = rounds_of(act, L, z)
                for u in R:
                    act.sem_inc(S["v_copied"][u], 1)
                with act.Fori(1, n + 1) as i:
                    for u in R:
                        act.wait_ge(S["oh_turned"][u], i + 1)
                        nc.scalar.copy(ohT[u][:, :], tps[u % 2][:, :]).then_inc(S["oh_copied"][u], 1)
                    for u in R:
                        act.wait_ge(landed[u], i * 16 * G)
                        act.wait_ge(S["v_free"][u], i)
                        nc.scalar.copy(vs[u][:, :].rearrange("p (j c) -> p j c", j=G),
                                       kv[u][:, :].rearrange("p (j c) -> p j c", j=G)[:, :, D:]).then_inc(S["v_copied"][u], 1)

            @block.sync
            def _(sp):
                sp.wait_ge(cleared, 1)
                sp.dma_start(att_dram[z.GMIN * P:, :].rearrange("(g p) c -> p g c", p=P),
                             att[:, z.GMIN * G * H:].rearrange("p (g c) -> p g c", c=G * H)).then_inc(zeroed, 16)
                sp.wait_ge(zeroed, 16)
                n = rounds_of(sp, L, z)
                for u in R:
                    sp.sem_inc(S["v_free"][u], 1)
                with sp.Fori(1, n + 1) as i:
                    for u in R:
                        g = (i - 1) * U + u
                        sp.wait_ge(S["v_copied"][u], i + 1)
                        sp.dma_start(v_dram[bass.ds(g * P, P), :], vs[u][:, :]).then_inc(S["stored"][u], 16)
                        sp.wait_ge(S["att_made"][u], i + 1)
                        sp.dma_start(att_dram[bass.ds(g * P, P), :], att[:, bass.ds(g * G * H, G * H)]).then_inc(S["stored"][u], 16)
                    for u in R:
                        sp.wait_ge(S["stored"][u], i * 32)
                        sp.sem_inc(S["v_free"][u], 1)


def phase_softmax(nc, s, z, k, L, att, seg_dram, att_dram, ex_dram):
    S_ = z.NGS * G
    with ExitStack() as ctx:
        sb, ps, sem = scope(nc, ctx, k)
        seg, prv, nxt = sb("seg", S_), sb("prv", S_), sb("nxt", S_)
        same = [prv, nxt]
        run = [sb("run_f", S_), sb("run_b", S_)]
        ends, whole = sb("ends", 2 * H), sb("whole", 2 * H)
        endT, wholeT, carT = sb("endT", P, F32, 2 * H), sb("wholeT", P, F32, 2 * H), sb("carT", P + 2, F32, 2 * H)
        car, least = sb("car", 2 * H), sb("least", 2)
        lead = sb("lead", 8, F32, 1)
        tp = ps("car_tp", 4 * P)
        seg_out, in_, step, pe1, out_, ready, pe2 = (sem(x) for x in ("seg_out", "sm_in", "sm_step", "sm_pe", "sm_out", "sm_ready", "sm_pe2"))
        row_done = sem("sm_row_done")
        a3 = att[:, :].rearrange("p (m h) -> p m h", h=H)
        n_all = P * S_
        with nc.Block() as block:
            @block.sync
            def _(sp):
                sp.dma_start(seg_dram[8:8 + n_all].rearrange("(g p j) -> p g j", p=P, j=G),
                             L["segment"][:, :].rearrange("p (g j) -> p g j", j=G)).then_inc(seg_out, 16)
                sp.wait_ge(ready, 1)
                sp.dma_start(seg_dram[0:8].rearrange("(o c) -> o c", o=1), lead[:, :]).then_inc(seg_out, 16)
                sp.dma_start(seg_dram[8 + n_all:16 + n_all].rearrange("(o c) -> o c", o=1), lead[:, :]).then_inc(seg_out, 16)
                sp.wait_ge(seg_out, 48)
                for t, at in ((seg, 8), (prv, 7), (nxt, 9)):
                    sp.dma_start(t[:, :], seg_dram[at:at + n_all].rearrange("(p m) -> p m", p=P)).then_inc(in_, 16)
                sp.dma_start(att[:, :], att_dram.rearrange("(p m) c -> p (m c)", p=P)).then_inc(in_, 16)
                sp.wait_ge(out_, H)
                sp.dma_start(ex_dram.rearrange("(p m) c -> p (m c)", p=P), att[:, :]).then_inc(seg_out, 16)
                sp.wait_ge(seg_out, 64)
                sp.dma_start(att[:, :].rearrange("p (g c) -> p g c", c=G * H),
                             ex_dram.rearrange("(g p) c -> p g c", p=P)).then_inc(seg_out, 16)
                sp.wait_ge(seg_out, 80)

            @block.vector
            def _(dve):
                c = Chain(dve, step)
                nc.vector.memset(lead[:, :], -2.0).then_inc(ready, 1)
                c.go(nc.vector.memset(carT[:, :], 0.0))
                dve.wait_ge(in_, 64)
                for t in same:
                    c.step(nc.vector.tensor_tensor(t[:, :], t[:, :], seg[:, :], ALU.is_equal))

                def scan(d, h, init):
                    sl = slice(None) if d == 0 else slice(None, None, -1)
                    return nc.vector.tensor_tensor_scan(run[d][:, sl], same[d][:, sl], a3[:, sl, h], init, ALU.mult, ALU.max)
                for d in range(2):
                    c.step(nc.vector.tensor_reduce(least[:, d:d + 1], same[d][:, :], AX, ALU.min))
                    c.step(nc.vector.tensor_copy(whole[:, d * H:(d + 1) * H], least[:, d:d + 1].broadcast_to([P, H])))
                    for h in range(H):
                        c.step(scan(d, h, 0.0))
                        end = run[d][:, S_ - 1:S_] if d == 0 else run[d][:, 0:1]
                        c.step(nc.vector.tensor_copy(ends[:, d * H + h:d * H + h + 1], end))
                dve.sem_inc(pe1, 1)
                dve.wait_ge(pe2, 1)
                for d in range(2):
                    c.step(nc.vector.tensor_copy(endT[0:H, :], tp[0:H, d * P:(d + 1) * P]))
                    c.step(nc.vector.tensor_copy(wholeT[0:H, :], tp[0:H, (2 + d) * P:(3 + d) * P]))
                    if d == 0:
                        c.step(nc.vector.tensor_tensor_scan(carT[0:H, 1:P + 1], wholeT[0:H, :], endT[0:H, :], 0.0, ALU.mult, ALU.max))
                    else:
                        c.step(nc.vector.tensor_tensor_scan(carT[0:H, P:0:-1], wholeT[0:H, ::-1], endT[0:H, ::-1], 0.0, ALU.mult, ALU.max))
                        c.step(nc.vector.memset(carT[0:H, P + 1:P + 2], 0.0))
                    dve.sem_inc(pe1, 1)
                    dve.wait_ge(pe2, 2 + d)
                    c.step(nc.vector.tensor_copy(car[:, d * H:(d + 1) * H], tp[:, 0:H]))
                for h in range(H):
                    for d in range(2):
                        c.step(scan(d, h, car[:, d * H + h:d * H + h + 1]))
                    c.step(nc.vector.tensor_tensor(run[0][:, :], run[0][:, :], run[1][:, :], ALU.max))
                    c.step(nc.vector.tensor_tensor(a3[:, :, h], a3[:, :, h], run[0][:, :], ALU.subtract))
                    dve.sem_inc(row_done, 1)

            @block.tensor
            def _(pe):
                pe.wait_ge(pe1, 1)
                for d in range(2):
                    nc.tensor.transpose(tp[0:H, d * P:(d + 1) * P], ends[:, d * H:(d + 1) * H], k["ident"][:, :])
                    last = nc.tensor.transpose(tp[0:H, (2 + d) * P:(3 + d) * P], whole[:, d * H:(d + 1) * H], k["ident"][:, :])
                last.then_inc(pe2, 1)
                for d in range(2):
                    pe.wait_ge(pe1, 2 + d)
                    nc.tensor.transpose(tp[:, 0:H], carT[0:H, 0:P] if d == 0 else carT[0:H, 2:P + 2],
                                        k["ident"][0:H, 0:H]).then_inc(pe2, 1)

            @block.scalar
            def _(act):
                for h in range(H):
                    act.wait_ge(row_done, h + 1)
                    nc.scalar.activation(a3[:, :, h], a3[:, :, h], ACT.Exp).then_inc(out_, 1)


def phase_messages(nc, s, z, k, L, ex, acc, v_dram):
    M = D + H
    with ExitStack() as ctx:
        sb, ps, sem = scope(nc, ctx, k)
        R = range(U)
        vin = [sb(f"m_v{u}", G * D) for u in R]
        oh = [sb(f"m_oh{u}", G * P) for u in R]
        msg = [sb(f"msg{u}", G * M) for u in R]
        sps = [ps(f"m_ps{u}", M) for u in R]
        sums = [sb(f"m_sum{u}", M) for u in R]
        S = {n: [sem(f"m_{n}{u}") for u in R] for n in ("v_in", "oh_made", "msg_made", "ex_made", "summed", "copied")}
        cleared, chain, add_go = sem("m_cleared"), sem("m_chain"), sem("m_add_go")
        with nc.Block() as block:
            @block.sync
            def _(sp):
                n = rounds_of(sp, L, z)
                with sp.Fori(1, n + 1) as i:
                    for u in R:
                        sp.wait_ge(S["msg_made"][u], i)
                        sp.dma_start(vin[u][:, :], v_dram[bass.ds(((i - 1) * U + u) * P, P), :]).then_inc(S["v_in"][u], 16)

            @block.vector
            def _(dve):
                nc.vector.memset(acc[:, :], 0.0).then_inc(cleared, 1)
                dve.wait_ge(cleared, 1)
                nc.vector.memset(acc[:, :].rearrange("p (b c) -> p b c", c=M)[:, s.NB:, D:], 1.0).then_inc(chain, 1)
                n = rounds_of(dve, L, z)
                for u in R:
                    dve.sem_inc(S["msg_made"][u], 1)
                    dve.sem_inc(S["summed"][u], 1)
                with dve.Fori(1, n + 1) as i:
                    for u in R:
                        g = (i - 1) * U + u
                        dve.wait_ge(S["summed"][u], i)
                        for j in range(G):
                            last = nc.vector.tensor_scalar(oh[u][:, j * P:(j + 1) * P], k["iota_f"][:, :],
                                                           L["place"][:, bass.ds(g * G + j, 1)], None, ALU.is_equal)
                        last.then_inc(S["oh_made"][u], 1)
                        dve.wait_ge(S["v_in"][u], i * 16)
                        nc.vector.tensor_tensor(
                            msg[u][:, :].rearrange("p (j c) -> p j c", j=G)[:, :, 0:D].rearrange("p j (h d) -> p j h d", h=H),
                            vin[u][:, :].rearrange("p (j h d) -> p j h d", j=G, h=H),
                            ex[:, bass.ds(g * G * H, G * H)].rearrange("p (j h) -> p j h", j=G).unsqueeze(3).broadcast_to([P, G, H, HD]),
                            ALU.mult).then_inc(S["msg_made"][u], 1)

            @block.gpsimd
            def _(pool):
                n = rounds_of(pool, L, z)
                pool.sem_inc(chain, U)
                for u in R:
                    pool.sem_inc(S["copied"][u], 1)
                with pool.Fori(1, n + 1) as i:
                    blocks = [pool.value_load(L["block"][0:1, bass.ds((i - 1) * U + u, 1)], min_val=0, max_val=s.NB) for u in R]
                    for u, b in zip(R, blocks):
                        pool.wait_ge(S["copied"][u], i + 1)
                        pool.wait_ge(chain, i * U + u + 1)
                        pool.sem_inc(add_go, 1)
                        nc.gpsimd.tensor_tensor(acc[:, bass.ds(b * M, M)], acc[:, bass.ds(b * M, M)], sums[u][:, :], ALU.add
                                                ).then_inc(chain, 1)

            @block.scalar
            def _(act):
                n = rounds_of(act, L, z)
                with act.Fori(1, n + 1) as i:
                    for u in R:
                        act.wait_ge(S["summed"][u], i)
                        nc.scalar.copy(msg[u][:, :].rearrange("p (j c) -> p j c", j=G)[:, :, D:],
                                       ex[:, bass.ds(((i - 1) * U + u) * G * H, G * H)].rearrange("p (j h) -> p j h", j=G)
                                       ).then_inc(S["ex_made"][u], 1)
                    for u in R:
                        act.wait_ge(S["summed"][u], i + 1)
                        act.wait_ge(chain, (i - 1) * U + u + 2)
                        nc.scalar.copy(sums[u][:, :], sps[u][:, :]).then_inc(S["copied"][u], 1)

            @block.tensor
            def _(pe):
                n = rounds_of(pe, L, z)
                with pe.Fori(1, n + 1) as i:
                    for u in R:
                        pe.wait_ge(S["copied"][u], i)
                        pe.wait_ge(S["msg_made"][u], i + 1)
                        pe.wait_ge(S["ex_made"][u], i)
                        for j in range(G):
                            last = nc.tensor.matmul(sps[u][:, :], oh[u][:, j * P:(j + 1) * P], msg[u][:, j * M:(j + 1) * M],
                                                    start=(j == 0), stop=(j == G - 1))
                        last.then_inc(S["summed"][u], 1)


def phase_attention_out(nc, s, k, acc, bias):
    M = D + H
    with ExitStack() as ctx:
        sb, ps, sem = scope(nc, ctx, k)
        den, y = sb("den", s.NB1 * H), sb("y0", s.NB1 * D)
        step = sem("ao_step")
        a3 = acc[:, :].rearrange("p (b c) -> p b c", c=M)
        with nc.Block() as block:
            @block.vector
            def _(dve):
                c = Chain(dve, step)
                c.step(nc.vector.reciprocal(den[:, :].rearrange("p (b h) -> p b h", h=H), a3[:, :, D:]))
                for h in range(H):
                    c.go(nc.vector.tensor_tensor(blocks(y)[:, :, h * HD:(h + 1) * HD], a3[:, :, h * HD:(h + 1) * HD],
                                                 den[:, :].rearrange("p (b h) -> p b h", h=H)[:, :, h:h + 1].broadcast_to([P, s.NB1, HD]),
                                                 ALU.mult))
                dve.wait_ge(step, c.n)
                c.step(nc.vector.tensor_tensor(blocks(y), blocks(y), over_blocks(bias[:, :], s), ALU.add))
                c.step(nc.vector.tensor_tensor(y[:, :], y[:, :], k["x"][:, :], ALU.add))
        phase_layernorm(nc, s, k, y, "0")


def phase_gather_sum(nc, s, z, k, L, table, acc, weighted, tag):
    with ExitStack() as ctx:
        sb, ps, sem = scope(nc, ctx, k)
        R = range(U)
        row = [sb(f"g_row{u}" + tag, G * D) for u in R]
        oh = [sb(f"g_oh{u}" + tag, G * P) for u in R]
        idx = [sb(f"g_idx{u}" + tag, G, U32) for u in R]
        sps = [ps(f"g_ps{u}" + tag, D) for u in R]
        landed = [sem(f"row_landed{u}" + tag, own=True) for u in R]
        S = {n: [sem(f"g_{n}{u}") for u in R] for n in ("idx_set", "oh_made", "summed")}
        chain, go = sem("g_chain"), sem("g_go")
        with nc.Block() as block:
            @block.gpsimd
            def _(pool):
                n = rounds_of(pool, L, z)
                with pool.Fori(1, n + 1) as i:
                    for u in R:
                        pool.wait_ge(S["idx_set"][u], i)
                        pool.sem_inc(go, 1)
                        for j in range(G):
                            nc.gpsimd.indirect_dma_start(row[u][:, j * D:(j + 1) * D], None, table,
                                                         bass.IndirectOffsetOnAxis(ap=idx[u][:, j:j + 1], axis=0)).then_inc(landed[u], 16)

            @block.vector
            def _(dve):
                nc.vector.memset(acc[:, :], 0.0).then_inc(chain, 1)
                n = rounds_of(dve, L, z)
                for u in R:
                    dve.sem_inc(S["summed"][u], 1)
                    set_index(nc, L, idx, 1, u).then_inc(S["idx_set"][u], 1)
                with dve.Fori(1, n + 1) as i:
                    for u in R:
                        g = (i - 1) * U + u
                        dve.wait_ge(S["summed"][u], i)
                        for j in range(G):
                            place = L["place"][:, bass.ds(g * G + j, 1)]
                            if weighted:
                                last = nc.vector.tensor_scalar(oh[u][:, j * P:(j + 1) * P], k["iota_f"][:, :], place,
                                                               L["weight"][:, bass.ds(g * G + j, 1)], ALU.is_equal, ALU.mult)
                            else:
                                last = nc.vector.tensor_scalar(oh[u][:, j * P:(j + 1) * P], k["iota_f"][:, :], place, None, ALU.is_equal)
                        last.then_inc(S["oh_made"][u], 1)
                    for u in R:
                        b = dve.value_load(L["block"][0:1, bass.ds((i - 1) * U + u, 1)], min_val=0, max_val=s.NB)
                        dve.wait_ge(S["summed"][u], i + 1)
                        set_index(nc, L, idx, i + 1, u).then_inc(S["idx_set"][u], 1)
                        dve.wait_ge(chain, (i - 1) * U + u + 1)
                        nc.vector.tensor_tensor(acc[:, bass.ds(b * D, D)], acc[:, bass.ds(b * D, D)], sps[u][:, :], ALU.add
                                                ).then_inc(chain, 1)

            @block.tensor
            def _(pe):
                n = rounds_of(pe, L, z)
                with pe.Fori(1, n + 1) as i:
                    for u in R:
                        pe.wait_ge(S["oh_made"][u], i)
                        pe.wait_ge(landed[u], i * 16 * G)
                        for j in range(G):
                            last = nc.tensor.matmul(sps[u][:, :], oh[u][:, j * P:(j + 1) * P], row[u][:, j * D:(j + 1) * D],
                                                    start=(j == 0), stop=(j == G - 1))
                        last.then_inc(S["summed"][u], 1)


def phase_edge_sums(nc, s, z, k, L, Pn, table, e_dram, stats):
    with ExitStack() as ctx:
        sb, ps, sem = scope(nc, ctx, k)
        R = range(U)
        row = [sb(f"e_row{u}", G * D) for u in R]
        oh = [sb(f"e_oh{u}", G * P, BF16) for u in R]
        ohT = [sb(f"e_ohT{u}", G * P, BF16) for u in R]
        idx = [sb(f"e_idx{u}", G, U32) for u in R]
        es = [sb(f"e_s{u}", GE) for u in R]
        tps = [ps(f"e_tps{u}", G * P, BF16) for u in range(2)]
        eps = [ps(f"e_ps{u}", GE) for u in R]
        landed = [sem(f"r_landed{u}", own=True) for u in R]
        S = {n: [sem(f"e_{n}{u}") for u in R] for n in
             ("idx_set", "oh_made", "oh_turned", "oh_copied", "e_made", "e_copied", "e_free", "stored", "stat")}
        go, cleared = sem("e_go"), sem("e_cleared")
        with nc.Block() as block:
            @block.gpsimd
            def _(pool):
                n = rounds_of(pool, L, z)
                with pool.Fori(1, n + 1) as i:
                    for u in R:
                        pool.wait_ge(S["idx_set"][u], i)
                        pool.sem_inc(go, 1)
                        for j in range(G):
                            nc.gpsimd.indirect_dma_start(row[u][:, j * D:(j + 1) * D], None, table,
                                                         bass.IndirectOffsetOnAxis(ap=idx[u][:, j:j + 1], axis=0)).then_inc(landed[u], 16)

            @block.vector
            def _(dve):
                nc.vector.memset(stats[:, :], 0.0).then_inc(cleared, 1)
                dve.wait_ge(cleared, 1)
                n = rounds_of(dve, L, z)
                for u in R:
                    dve.sem_inc(S["oh_turned"][u], 1)
                    dve.sem_inc(S["stat"][u], 1)
                    set_index(nc, L, idx, 1, u).then_inc(S["idx_set"][u], 1)
                with dve.Fori(1, n + 1) as i:
                    for u in R:
                        g = (i - 1) * U + u
                        dve.wait_ge(S["oh_turned"][u], i)
                        for j in range(G):
                            last = nc.vector.tensor_scalar(oh[u][:, j * P:(j + 1) * P], k["iota_f"][:, :],
                                                           L["place"][:, bass.ds(g * G + j, 1)], None, ALU.is_equal)
                        last.then_inc(S["oh_made"][u], 1)
                    for u in R:
                        dve.wait_ge(S["e_copied"][u], i)
                        set_index(nc, L, idx, i + 1, u).then_inc(S["idx_set"][u], 1)
                        nc.vector.bn_stats(stats[:, bass.ds(((i - 1) * U + u) * 6, 6)], es[u][:, :]).then_inc(S["stat"][u], 1)

            @block.tensor
            def _(pe):
                n = rounds_of(pe, L, z)
                for u in R:
                    pe.sem_inc(S["e_made"][u], 1)
                with pe.Fori(1, n + 1) as i:
                    for u in R:
                        pe.wait_ge(S["oh_made"][u], i)
                        if u >= 2:
                            pe.wait_ge(S["oh_copied"][u - 2], i)
                        for j in range(G):
                            last = nc.tensor.transpose(tps[u % 2][:, j * P:(j + 1) * P], oh[u][:, j * P:(j + 1) * P], k["ident_b"][:, :])
                        last.then_inc(S["oh_turned"][u], 1)
                    for u in R:
                        b = pe.value_load(L["block"][0:1, bass.ds((i - 1) * U + u, 1)], min_val=0, max_val=s.NB)
                        pe.wait_ge(S["oh_copied"][u], i)
                        pe.wait_ge(landed[u], i * 16 * G)
                        pe.wait_ge(S["e_free"][u], i)
                        for j in range(G):
                            nc.tensor.matmul(eps[u][:, j * P:(j + 1) * P], row[u][:, j * D:(j + 1) * D], k["ident"][:, :],
                                             start=True, stop=False)
                            for q in range(3):
                                last = nc.tensor.matmul(eps[u][:, j * P:(j + 1) * P], Pn[q][:, bass.ds(b * D, D)],
                                                        ohT[u][:, j * P:(j + 1) * P], start=False, stop=(q == 2))
                        last.then_inc(S["e_made"][u], 1)

            @block.scalar
            def _(act):
                n = rounds_of(act, L, z)
                for u in R:
                    act.sem_inc(S["e_free"][u], 1)
                with act.Fori(1, n + 1) as i:
                    for u in R:
                        act.wait_ge(S["oh_turned"][u], i + 1)
                        nc.scalar.copy(ohT[u][:, :], tps[u % 2][:, :]).then_inc(S["oh_copied"][u], 1)
                    for u in R:
                        act.wait_ge(S["e_made"][u], i + 1)
                        act.wait_ge(S["stat"][u], i)
                        act.wait_ge(S["e_free"][u], i)
                        nc.scalar.copy(es[u][:, :], eps[u][:, :]).then_inc(S["e_copied"][u], 1)

            @block.sync
            def _(sp):
                n = rounds_of(sp, L, z)
                with sp.Fori(1, n + 1) as i:
                    for u in R:
                        sp.wait_ge(S["e_copied"][u], i)
                        sp.dma_start(e_dram[bass.ds(((i - 1) * U + u) * P, P), :], es[u][:, :]).then_inc(S["stored"][u], 16)
                    for u in R:
                        sp.wait_ge(S["stored"][u], i * 16)
                        sp.sem_inc(S["e_free"][u], 1)


def phase_stats(nc, s, z, k, L, stats, g, b, pad_col, sc, sh, tag):
    with ExitStack() as ctx:
        sb, ps, sem = scope(nc, ctx, k)
        NG2 = z.NGS * 2
        t1, t2 = sb("st1" + tag, NG2), sb("st2" + tag, NG2)
        m, q, v, nf, pd, sd = (sb(f"st_{x}" + tag, 1) for x in ("m", "q", "v", "n", "p", "sd"))
        step, ready, sd_ready = sem("st_step"), sem("st_ready"), sem("st_sd")
        st3 = stats[:, :].rearrange("p (m c) -> p m c", c=3)
        with nc.Block() as block:
            @block.vector
            def _(dve):
                c = Chain(dve, step)
                c.step(nc.vector.tensor_tensor(t1[:, :], st3[:, :, 0], st3[:, :, 1], ALU.mult))
                c.step(nc.vector.tensor_reduce(m[:, :], t1[:, :], AX, ALU.add))
                c.step(nc.vector.tensor_tensor(t2[:, :], t1[:, :], st3[:, :, 1], ALU.mult))
                c.step(nc.vector.tensor_tensor(t2[:, :], t2[:, :], st3[:, :, 2], ALU.add))
                c.step(nc.vector.tensor_reduce(q[:, :], t2[:, :], AX, ALU.add))
                if pad_col is not None:
                    c.step(nc.vector.tensor_reduce(nf[:, :], st3[:, :, 0], AX, ALU.add))
                    c.step(nc.vector.tensor_scalar(nf[:, :], nf[:, :], -float(s.E), None, ALU.add))
                    c.step(nc.vector.tensor_tensor(pd[:, :], nf[:, :], pad_col, ALU.mult))
                    c.step(nc.vector.tensor_tensor(m[:, :], m[:, :], pd[:, :], ALU.subtract))
                    c.step(nc.vector.tensor_tensor(pd[:, :], pd[:, :], pad_col, ALU.mult))
                    c.step(nc.vector.tensor_tensor(q[:, :], q[:, :], pd[:, :], ALU.subtract))
                c.step(nc.vector.tensor_scalar(m[:, :], m[:, :], 1.0 / s.E, None, ALU.mult))
                c.step(nc.vector.tensor_scalar(q[:, :], q[:, :], 1.0 / s.E, None, ALU.mult))
                c.step(nc.vector.tensor_tensor(v[:, :], m[:, :], m[:, :], ALU.mult))
                c.step(nc.vector.tensor_tensor(v[:, :], q[:, :], v[:, :], ALU.subtract))
                c.step(nc.vector.tensor_scalar(v[:, :], v[:, :], 0.0, EPS, ALU.max, ALU.add))
                dve.sem_inc(ready, 1)
                dve.wait_ge(sd_ready, 1)
                c.step(nc.vector.reciprocal(v[:, :], sd[:, :]))
                c.step(nc.vector.tensor_tensor(sc, v[:, :], g, ALU.mult))
                c.step(nc.vector.tensor_tensor(m[:, :], m[:, :], sc, ALU.mult))
                c.step(nc.vector.tensor_tensor(sh, b, m[:, :], ALU.subtract))

            @block.scalar
            def _(act):
                act.wait_ge(ready, 1)
                nc.scalar.activation(sd[:, :], v[:, :], ACT.Sqrt).then_inc(sd_ready, 1)


def phase_fc_stats(nc, s, z, k, L, fcT, sc, sh, e_dram, stats, empty):
    with ExitStack() as ctx:
        sb, ps, sem = scope(nc, ctx, k)
        R = range(U)
        ein = [sb(f"f_e{u}", GE) for u in R]
        act_t = [sb(f"f_a{u}", GE) for u in R]
        zps = [ps(f"f_z{u}", GE) for u in R]
        r0 = sb("f_r0", 1)
        eps_ = ps("f_empty", 1)
        S = {n: [sem(f"f_{n}{u}") for u in R] for n in ("e_in", "a_made", "z_made", "stat")}
        cleared, r0_made, empty_made, empty_out = sem("f_cleared"), sem("f_r0_made"), sem("f_empty_made"), sem("f_empty_out")
        with nc.Block() as block:
            @block.sync
            def _(sp):
                n = rounds_of(sp, L, z)
                for u in R:
                    sp.sem_inc(S["a_made"][u], 1)
                with sp.Fori(1, n + 1) as i:
                    for u in R:
                        sp.wait_ge(S["a_made"][u], i)
                        sp.dma_start(ein[u][:, :], e_dram[bass.ds(((i - 1) * U + u) * P, P), :]).then_inc(S["e_in"][u], 16)

            @block.scalar
            def _(act):
                nc.scalar.activation(r0[:, :], sh, ACT.Relu).then_inc(r0_made, 1)
                n = rounds_of(act, L, z)
                for u in R:
                    act.sem_inc(S["z_made"][u], 1)
                with act.Fori(1, n + 1) as i:
                    for u in R:
                        act.wait_ge(S["e_in"][u], i * 16)
                        act.wait_ge(S["z_made"][u], i)
                        nc.scalar.activation(act_t[u][:, :], ein[u][:, :], ACT.Relu, bias=sh, scale=sc).then_inc(S["a_made"][u], 1)

            @block.tensor
            def _(pe):
                pe.wait_ge(r0_made, 1)
                nc.tensor.matmul(eps_[:, :], fcT[:, :], r0[:, :], start=True, stop=True).then_inc(empty_made, 1)
                n = rounds_of(pe, L, z)
                with pe.Fori(1, n + 1) as i:
                    for u in R:
                        pe.wait_ge(S["a_made"][u], i + 1)
                        pe.wait_ge(S["stat"][u], i)
                        nc.tensor.matmul(zps[u][:, :], fcT[:, :], act_t[u][:, :], start=True, stop=True).then_inc(S["z_made"][u], 1)

            @block.vector
            def _(dve):
                nc.vector.memset(stats[:, :], 0.0).then_inc(cleared, 1)
                dve.wait_ge(cleared, 1)
                dve.wait_ge(empty_made, 1)
                nc.vector.tensor_copy(empty[:, :], eps_[:, :]).then_inc(empty_out, 1)
                n = rounds_of(dve, L, z)
                for u in R:
                    dve.sem_inc(S["stat"][u], 1)
                with dve.Fori(1, n + 1) as i:
                    for u in R:
                        dve.wait_ge(S["z_made"][u], i + 1)
                        nc.vector.bn_stats(stats[:, bass.ds(((i - 1) * U + u) * 6, 6)], zps[u][:, :]).then_inc(S["stat"][u], 1)


def phase_fc_weights(nc, s, k, fc, sc, sh, fcs, shrow):
    with ExitStack() as ctx:
        sb, ps, sem = scope(nc, ctx, k)
        t, dg = sb("w_t", D), sb("w_dg", D)
        p1, p2 = ps("w_p1", D), ps("w_p2", D)
        step, made, done = sem("w_step"), sem("w_made"), sem("w_done")
        with nc.Block() as block:
            @block.vector
            def _(dve):
                c = Chain(dve, step)
                nc.vector.tensor_scalar(t[:, :], fc[:, :], sc, None, ALU.mult).then_inc(made, 1)
                nc.vector.tensor_scalar(dg[:, :], k["ident"][:, :], sh, None, ALU.mult).then_inc(made, 1)
                dve.wait_ge(done, 2)
                c.go(nc.vector.tensor_copy(fcs[:, :], p1[:, :]))
                for j in range(G):
                    c.go(nc.vector.tensor_copy(shrow[:, j * D:(j + 1) * D], p2[:, :]))
                dve.wait_ge(step, c.n)

            @block.tensor
            def _(pe):
                pe.wait_ge(made, 2)
                nc.tensor.transpose(p1[:, :], t[:, :], k["ident"][:, :]).then_inc(done, 1)
                nc.tensor.matmul(p2[:, :], k["ones"][:, :], dg[:, :], start=True, stop=True).then_inc(done, 1)


def phase_edge_out(nc, s, z, k, L, fcs, shrow, sc, sh, e_dram, acc):
    assert z.GMIN >= 2 * U
    with ExitStack() as ctx:
        sb, ps, sem = scope(nc, ctx, k)
        R = range(U)
        ein = [sb(f"o_e{u}", GE) for u in R]
        act_t = [sb(f"o_a{u}", GE) for u in R]
        zs = [sb(f"o_z{u}", G * D) for u in R]
        zr = [sb(f"o_r{u}", G * D) for u in R]
        oh = [sb(f"o_oh{u}", G * P) for u in R]
        zps = [ps(f"o_zps{u}", G * D) for u in R]
        sps = [ps(f"o_sps{u}", D) for u in R]
        sums = [sb(f"o_sum{u}", D) for u in R]
        S = {n: [sem(f"o_{n}{u}") for u in R] for n in ("e_in", "a_made", "z_made", "z_shifted", "z_relu", "oh_made", "summed", "copied")}
        chain, add_go = sem("o_chain"), sem("o_add_go")
        with nc.Block() as block:
            @block.sync
            def _(sp):
                n = rounds_of(sp, L, z)
                for u in R:
                    sp.sem_inc(S["a_made"][u], 1)
                with sp.Fori(1, n + 1) as i:
                    for u in R:
                        sp.wait_ge(S["a_made"][u], i)
                        sp.dma_start(ein[u][:, :], e_dram[bass.ds(((i - 1) * U + u) * P, P), :]).then_inc(S["e_in"][u], 16)

            @block.scalar
            def _(act):
                n = rounds_of(act, L, z)
                for u in R:
                    act.sem_inc(S["z_made"][u], 1)

                def normalise(i):
                    for u in R:
                        act.wait_ge(S["e_in"][u], i * 16)
                        act.wait_ge(S["z_made"][u], i)
                        nc.scalar.activation(act_t[u][:, :], ein[u][:, :], ACT.Relu, bias=sh, scale=sc).then_inc(S["a_made"][u], 1)

                def relu(i):
                    for u in R:
                        act.wait_ge(S["z_shifted"][u], i + 1)
                        act.wait_ge(S["summed"][u], i)
                        nc.scalar.activation(zr[u][:, :], zs[u][:, :], ACT.Relu).then_inc(S["z_relu"][u], 1)

                def copy_sums(i):
                    for u in R:
                        act.wait_ge(S["summed"][u], i + 1)
                        act.wait_ge(chain, i * U + u + 2)
                        nc.scalar.copy(sums[u][:, :], sps[u][:, :]).then_inc(S["copied"][u], 1)

                normalise(1)
                with act.Fori(1, n) as i:
                    relu(i)
                    normalise(i + 1)
                    copy_sums(i)
                relu(n)
                copy_sums(n)

            @block.tensor
            def _(pe):
                n = rounds_of(pe, L, z)
                with pe.Fori(1, n + 1) as i:
                    for u in R:
                        pe.wait_ge(S["a_made"][u], i + 1)
                        pe.wait_ge(S["z_shifted"][u], i)
                        for j in range(G):
                            last = nc.tensor.matmul(zps[u][:, j * D:(j + 1) * D], act_t[u][:, j * P:(j + 1) * P], fcs[:, :],
                                                    start=True, stop=True)
                        last.then_inc(S["z_made"][u], 1)
                    for u in R:
                        pe.wait_ge(S["copied"][u], i)
                        pe.wait_ge(S["oh_made"][u], i)
                        pe.wait_ge(S["z_relu"][u], i + 1)
                        for j in range(G):
                            last = nc.tensor.matmul(sps[u][:, :], oh[u][:, j * P:(j + 1) * P], zr[u][:, j * D:(j + 1) * D],
                                                    start=(j == 0), stop=(j == G - 1))
                        last.then_inc(S["summed"][u], 1)

            @block.vector
            def _(dve):
                nc.vector.memset(acc[:, :], 0.0).then_inc(chain, 1)
                n = rounds_of(dve, L, z)
                for u in R:
                    dve.sem_inc(S["summed"][u], 1)
                    dve.sem_inc(S["z_shifted"][u], 1)
                    dve.sem_inc(S["z_relu"][u], 1)

                def one_hots(i):
                    for u in R:
                        dve.wait_ge(S["summed"][u], i)
                        for j in range(G):
                            last = nc.vector.tensor_scalar(oh[u][:, j * P:(j + 1) * P], k["iota_f"][:, :],
                                                           L["place"][:, bass.ds(((i - 1) * U + u) * G + j, 1)], None, ALU.is_equal)
                        last.then_inc(S["oh_made"][u], 1)

                def shift(i):
                    for u in R:
                        dve.wait_ge(S["z_made"][u], i + 1)
                        dve.wait_ge(S["z_relu"][u], i)
                        nc.vector.tensor_tensor(zs[u][:, :], zps[u][:, :], shrow[:, :], ALU.add).then_inc(S["z_shifted"][u], 1)

                one_hots(1)
                with dve.Fori(1, n) as i:
                    shift(i)
                    one_hots(i + 1)
                shift(n)

            @block.gpsimd
            def _(pool):
                n = rounds_of(pool, L, z)
                pool.sem_inc(chain, 2 * U)
                for u in R:
                    pool.sem_inc(S["copied"][u], 1)
                with pool.Fori(1, n + 1) as i:
                    blocks = [pool.value_load(L["block"][0:1, bass.ds((i - 1) * U + u, 1)], min_val=0, max_val=s.NB) for u in R]
                    for u, b in zip(R, blocks):
                        pool.wait_ge(S["copied"][u], i + 1)
                        pool.wait_ge(chain, (i + 1) * U + u + 1)
                        pool.sem_inc(add_go, 1)
                        nc.gpsimd.tensor_tensor(acc[:, bass.ds(b * D, D)], acc[:, bass.ds(b * D, D)], sums[u][:, :], ALU.add
                                                ).then_inc(chain, 1)


def phase_edge_mean(nc, s, k, acc, counts):
    with ExitStack() as ctx:
        sb, ps, sem = scope(nc, ctx, k)
        rc = sb("em_rc", s.NB1)
        step = sem("em_step")
        with nc.Block() as block:
            @block.vector
            def _(dve):
                c = Chain(dve, step)
                c.step(nc.vector.tensor_scalar(rc[:, :], counts[:, :], 1.0, None, ALU.max))
                c.step(nc.vector.reciprocal(rc[:, :], rc[:, :]))
                c.step(nc.vector.tensor_tensor(blocks(acc), blocks(acc), rc[:, :].unsqueeze(2).broadcast_to([P, s.NB1, D]), ALU.mult))
                c.step(nc.vector.tensor_tensor(acc[:, :], acc[:, :], k["x"][:, :], ALU.add))
                c.step(nc.vector.scalar_tensor_tensor(out=acc[:, :], in0=acc[:, :], scalar=0.0, in1=k["x"][:, :],
                                                      op0=ALU.max, op1=ALU.add))
        phase_layernorm(nc, s, k, acc, "1")


def phase_degrees(nc, s, k, counts, dinv, h):
    with ExitStack() as ctx:
        sb, ps, sem = scope(nc, ctx, k)
        dg, sq = sb("dg_d", s.NB1), sb("dg_s", s.NB1)
        step, ready, rooted = sem("dg_step"), sem("dg_ready"), sem("dg_rooted")
        with nc.Block() as block:
            @block.vector
            def _(dve):
                c = Chain(dve, step)
                nc.vector.tensor_scalar(dg[:, :], counts[:, :], 1.0, None, ALU.add).then_inc(ready, 1)
                dve.wait_ge(rooted, 1)
                c.step(nc.vector.reciprocal(dinv[:, :], sq[:, :]))
                c.step(nc.vector.tensor_tensor(blocks(h), blocks(h), dinv[:, :].unsqueeze(2).broadcast_to([P, s.NB1, D]), ALU.mult))

            @block.scalar
            def _(act):
                act.wait_ge(ready, 1)
                nc.scalar.activation(sq[:, :], dg[:, :], ACT.Sqrt).then_inc(rooted, 1)


def phase_conv_out(nc, s, k, acc, h, dinv, bias, gamma, beta):
    with ExitStack() as ctx:
        sb, ps, sem = scope(nc, ctx, k)
        mask_i, mask = sb("co_mi", s.NB1, I32), sb("co_m", s.NB1)
        part, row = sb("co_part", D), sb("co_row", D)
        tot = [ps(f"co_tot{n}", D) for n in range(2)]
        step, ready, totals, node_id, ready2, rooted = (sem(x) for x in ("co_step", "co_ready", "co_tot", "co_id", "co_ready2", "co_root"))
        sd = sb("co_sd", D)
        with nc.Block() as block:
            @block.gpsimd
            def _(pool):
                nc.gpsimd.iota(mask_i[:, :], pattern=[[P, s.NB1]], base=0, channel_multiplier=1).then_inc(node_id, 1)

            @block.tensor
            def _(pe):
                for n in range(2):
                    pe.wait_ge(ready, n + 1)
                    nc.tensor.matmul(tot[n][:, :], k["ones"][:, :], part[:, :], start=True, stop=True).then_inc(totals, 1)

            @block.scalar
            def _(act):
                act.wait_ge(ready2, 1)
                nc.scalar.activation(sd[:, :], row[:, :], ACT.Sqrt).then_inc(rooted, 1)

            @block.vector
            def _(dve):
                c = Chain(dve, step)
                by_feature = acc[:, :].rearrange("p (b f) -> p f b", f=D)
                sq_feature = h[:, :].rearrange("p (b f) -> p f b", f=D)
                c.step(nc.vector.tensor_tensor(acc[:, :], acc[:, :], h[:, :], ALU.add))
                c.step(nc.vector.tensor_tensor(blocks(acc), blocks(acc), dinv[:, :].unsqueeze(2).broadcast_to([P, s.NB1, D]), ALU.mult))
                c.step(nc.vector.tensor_tensor(blocks(acc), blocks(acc), over_blocks(bias[:, :], s), ALU.add))
                dve.wait_ge(node_id, 1)
                c.step(nc.vector.tensor_copy(mask[:, :], mask_i[:, :]))
                c.step(nc.vector.tensor_scalar(mask[:, :], mask[:, :], float(s.N), None, ALU.is_lt))
                m3 = mask[:, :].unsqueeze(2).broadcast_to([P, s.NB1, D])
                c.step(nc.vector.scalar_tensor_tensor(out=blocks(acc), in0=blocks(acc), scalar=0.0, in1=m3, op0=ALU.max, op1=ALU.mult))
                c.step(nc.vector.tensor_reduce(part[:, :], by_feature, AX, ALU.add))
                dve.sem_inc(ready, 1)
                dve.wait_ge(totals, 1)
                c.step(nc.vector.tensor_scalar(row[:, :], tot[0][:, :], 1.0 / s.N, None, ALU.mult))
                c.step(nc.vector.tensor_tensor(blocks(acc), blocks(acc), over_blocks(row[:, :], s), ALU.subtract))
                c.step(nc.vector.tensor_tensor(blocks(acc), blocks(acc), m3, ALU.mult))
                c.step(nc.vector.tensor_tensor(h[:, :], acc[:, :], acc[:, :], ALU.mult))
                c.step(nc.vector.tensor_reduce(part[:, :], sq_feature, AX, ALU.add))
                dve.sem_inc(ready, 1)
                dve.wait_ge(totals, 2)
                c.step(nc.vector.tensor_scalar(row[:, :], tot[1][:, :], 1.0 / s.N, EPS, ALU.mult, ALU.add))
                dve.sem_inc(ready2, 1)
                dve.wait_ge(rooted, 1)
                c.step(nc.vector.reciprocal(row[:, :], sd[:, :]))
                c.step(nc.vector.tensor_tensor(row[:, :], row[:, :], gamma[:, :], ALU.mult))
                c.step(nc.vector.tensor_tensor(blocks(acc), blocks(acc), over_blocks(row[:, :], s), ALU.mult))
                c.step(nc.vector.tensor_tensor(blocks(acc), blocks(acc), over_blocks(beta[:, :], s), ALU.add))
                c.step(nc.vector.tensor_tensor(acc[:, :], acc[:, :], k["x"][:, :], ALU.add))
        phase_layernorm(nc, s, k, acc, "2")


def phase_add_x(nc, s, k, y):
    with ExitStack() as ctx:
        sb, ps, sem = scope(nc, ctx, k)
        added = sem("x_added")
        with nc.Block() as block:
            @block.vector
            def _(dve):
                nc.vector.tensor_tensor(y[:, :], y[:, :], k["x"][:, :], ALU.add).then_inc(added, 1)
                dve.wait_ge(added, 1)


def phase_turn(nc, k, pairs, tag):
    with ExitStack() as ctx:
        sb, ps, sem = scope(nc, ctx, k)
        tp = ps("t_tp" + tag, len(pairs) * P)
        diff = [sb(f"t_diff{n}" + tag, P) for n in range(len(pairs))]
        made, turned, out = sem("t_made"), sem("t_turned"), sem("t_out")
        with nc.Block() as block:
            @block.vector
            def _(dve):
                for n, (dst, src, minus) in enumerate(pairs):
                    if minus is None:
                        nc.vector.tensor_copy(diff[n][:, :], src[:, :]).then_inc(made, 1)
                    else:
                        nc.vector.tensor_tensor(diff[n][:, :], src[:, :], minus[:, :], ALU.subtract).then_inc(made, 1)
                dve.wait_ge(turned, 1)
                for n, (dst, src, minus) in enumerate(pairs):
                    nc.vector.tensor_copy(dst, tp[:, n * P:(n + 1) * P]).then_inc(out, 1)
                dve.wait_ge(out, len(pairs))

            @block.tensor
            def _(pe):
                pe.wait_ge(made, len(pairs))
                for n in range(len(pairs)):
                    last = nc.tensor.transpose(tp[:, n * P:(n + 1) * P], diff[n][:, :], k["ident"][:, :])
                last.then_inc(turned, 1)


def gnn_kernel(nc, x, src, dst, edge_weight, q_w, q_b, k_w, k_b, v_w, att_bias, theta, phi, fc1, g0, b0, g1, b1,
               conv_w, conv_b, gamma, beta, w1, bias1, w2, bias2, out):
    s = Shapes(x.shape[0], src.shape[0])
    zs, zd = Sorted(s, True), Sorted(s, False)
    NF = s.NB1 * D

    def dram(name, shape):
        return nc.dram_tensor(name, shape, F32).ap()

    def spread(vec, n=P):
        return vec.rearrange("(o f) -> o f", o=1).broadcast_to([n, vec.shape[0]])

    def column(vec):
        return vec.rearrange("(f o) -> f o", o=1)

    with ExitStack() as top:
        def tile(ctx, name, cols, dt=F32, parts=P):
            return ctx.enter_context(nc.sbuf_tensor(name, [parts, cols], dt))
        k = dict(sems=Semaphores(nc, top))
        for name, cols, dt in (("x", NF, F32), ("ones", P, F32), ("zero", P, F32), ("iota_f", P, BF16), ("iota_8", 8 * P, BF16), ("iota_p", 1, F32),
                               ("ident", P, F32), ("ident_b", P, BF16), ("before", 4 * P, F32), ("after", P, F32)):
            k[name] = tile(top, name, cols, dt)
        phase_constants(nc, s, x, k)

        Ld = dict(rounds=tile(top, "rounds_d", 1, I32), block=tile(top, "block_d", zd.NGS, I32, 1), counts=tile(top, "counts_d", s.NB1))
        by_dst = sort_state(nc, s, zd, top, Ld, "_d")
        with ExitStack() as c0:
            L = dict(rounds=tile(c0, "rounds_s", 1, I32), block=tile(c0, "block_s", zs.NGS, I32, 1), counts=tile(c0, "counts_s", s.NB1))
            by_src = sort_state(nc, s, zs, c0, L, "_s")
            with ExitStack() as c1:
                sort_arrays(nc, zd, c1, by_dst, "_d")
                phase_sort_input(nc, s, zd, k, by_dst, dst, src, edge_weight, "_d")
                with ExitStack() as c2:
                    sort_arrays(nc, zs, c2, by_src, "_s")
                    phase_sort_input(nc, s, zs, k, by_src, src, dst, None, "_s")
                    phase_histogram(nc, s, zs, k, by_src, "_s")
                    phase_offsets(nc, s, zs, k, by_src, L, "_s")
                    phase_positions(nc, s, zs, k, by_src, "_s", by_dst)
                phase_offsets(nc, s, zd, k, by_dst, Ld, "_d")
                phase_positions(nc, s, zd, k, by_dst, "_d")
            L.update(place=tile(c0, "place_s", zs.NGS * G), gather=tile(c0, "gather_s", (zs.NGS + U) * G, U32),
                     segment=tile(c0, "segment_s", zs.NGS * G))
            phase_lists(nc, s, zs, k, by_src, L, "_s")
            kv_table, v_dram = dram("kv_table", [s.NB1 * P, 2 * D]), dram("v_edges", [zs.NGS * P, G * D])
            att_dram, ex_dram = dram("att_edges", [zs.NGS * P, G * H]), dram("ex_edges", [zs.NGS * P, G * H])
            seg_dram = dram("segments", [zs.NGS * GE + 16])
            abias = tile(c0, "abias", D)
            att = None
            with ExitStack() as c1:
                Q = [tile(c1, f"q_part{n}", NF, BF16) for n in range(3)]
                with ExitStack() as c2:
                    qf, kvf = tile(c2, "q_full", NF), tile(c2, "kv_full", 2 * NF)
                    w, brow = tile(c2, "qkv_w", 3 * D), tile(c2, "qkv_b", 3 * D, F32, 1)
                    phase_load(nc, k, [(w[:, 0:D], q_w), (w[:, D:2 * D], k_w), (w[:, 2 * D:], v_w), (abias[:, :], spread(att_bias)),
                                       (brow[:, 0:D], spread(q_b, 1)), (brow[:, D:2 * D], spread(k_b, 1))], "w0")
                    phase_zero(nc, k, brow[:, 2 * D:])
                    phase_dense(nc, s, k, k["x"], w[:, :], brow,
                                [(0, D, ACT.Relu, lambda b: qf[:, bass.ds(b * D, D)]),
                                 (D, 2 * D, ACT.Relu, lambda b: kvf[:, bass.ds(b * 2 * D, D)]),
                                 (2 * D, 3 * D, ACT.Copy, lambda b: kvf[:, bass.ds(b * 2 * D + D, D)])], "_qkv")
                    phase_split_and_store(nc, k, qf, Q, [(kv_table, kvf, 2 * D)])
                with ExitStack() as c2:
                    att_a = tile(c2, "att_scores", zs.NGS * G * H)
                    phase_scores(nc, s, zs, k, L, Q, att_a, kv_table, v_dram, att_dram)
            att = tile(c0, "att", zs.NGS * G * H)
            phase_softmax(nc, s, zs, k, L, att, seg_dram, att_dram, ex_dram)
            with ExitStack() as c1:
                acc = tile(c1, "acc0", s.NB1 * (D + H))
                phase_messages(nc, s, zs, k, L, att, acc, v_dram)
                phase_attention_out(nc, s, k, acc, abias)

        L = Ld
        L.update(place=tile(top, "place_d", zd.NGS * G), gather=tile(top, "gather_d", (zd.NGS + U) * G, U32),
                 weight=tile(top, "weight_d", zd.NGS * G))
        phase_lists(nc, s, zd, k, by_dst, L, "_d")
        acc = tile(top, "acc", NF)

        with ExitStack() as c0:
            r_table, e_dram = dram("r_table", [s.NB1 * P, D]), dram("e_edges", [zd.NGS * P, GE])
            stats, fc, fcT, fcs = tile(c0, "stats", zd.NGS * 6), tile(c0, "fc", D), tile(c0, "fcT", D), tile(c0, "fcs", D)
            shrow, cols, empty = tile(c0, "shrow", G * D), tile(c0, "bn_cols", 8), tile(c0, "empty", 1)
            Pn = [tile(c0, f"p_part{n}", NF, BF16) for n in range(3)]
            with ExitStack() as c1:
                th, ph, w = tile(c1, "theta", D), tile(c1, "phi", D), tile(c1, "pr_w", 2 * D)
                pf, rf = tile(c1, "p_full", NF), tile(c1, "r_full", NF)
                phase_load(nc, k, [(th[:, :], theta), (ph[:, :], phi), (fc[:, :], fc1), (cols[:, 0:1], column(g0)),
                                   (cols[:, 1:2], column(b0)), (cols[:, 2:3], column(g1)), (cols[:, 3:4], column(b1))], "w1")
                phase_turn(nc, k, [(w[:, 0:D], th, None), (w[:, D:], ph, th), (fcT[:, :], fc, None)], "_w1")
                phase_dense(nc, s, k, k["x"], w[:, :], None,
                            [(0, D, ACT.Copy, lambda b: pf[:, bass.ds(b * D, D)]),
                             (D, 2 * D, ACT.Copy, lambda b: rf[:, bass.ds(b * D, D)])], "_pr")
                phase_split_and_store(nc, k, pf, Pn, [(r_table, rf, D)])
            phase_edge_sums(nc, s, zd, k, L, Pn, r_table, e_dram, stats)
            phase_stats(nc, s, zd, k, L, stats, cols[:, 0:1], cols[:, 1:2], None, cols[:, 4:5], cols[:, 5:6], "a")
            phase_fc_stats(nc, s, zd, k, L, fcT, cols[:, 4:5], cols[:, 5:6], e_dram, stats, empty)
            phase_stats(nc, s, zd, k, L, stats, cols[:, 2:3], cols[:, 3:4], empty[:, :], cols[:, 6:7], cols[:, 7:8], "b")
            phase_fc_weights(nc, s, k, fc, cols[:, 6:7], cols[:, 7:8], fcs, shrow)
            phase_edge_out(nc, s, zd, k, L, fcs, shrow, cols[:, 4:5], cols[:, 5:6], e_dram, acc)
            phase_edge_mean(nc, s, k, acc, L["counts"])

        with ExitStack() as c0:
            g_table = dram("g_table", [s.NB1 * P, D])
            h, w, dinv = tile(c0, "h", NF), tile(c0, "conv_w", D), tile(c0, "dinv", s.NB1)
            rows3 = [tile(c0, f"conv_row{n}", D) for n in range(3)]
            phase_load(nc, k, [(w[:, :], conv_w)] + [(t[:, :], spread(v)) for t, v in zip(rows3, (conv_b, gamma, beta))], "w2")
            phase_dense(nc, s, k, k["x"], w[:, :], None, [(0, D, ACT.Copy, lambda b: h[:, bass.ds(b * D, D)])], "_h")
            phase_degrees(nc, s, k, L["counts"], dinv, h)
            phase_store(nc, k, [(g_table, h, D)])
            phase_gather_sum(nc, s, zd, k, L, g_table, acc, False, "_g")
            phase_conv_out(nc, s, k, acc, h, dinv, *rows3)

        with ExitStack() as c0:
            x_table = dram("x_table", [s.NB1 * P, D])
            w, brow, y = tile(c0, "mlp_w", 2 * D), tile(c0, "mlp_b", 2 * D, F32, 1), tile(c0, "mlp_y", NF)
            phase_load(nc, k, [(w[:, 0:D], w1), (w[:, D:], w2), (brow[:, 0:D], spread(bias1, 1)), (brow[:, D:], spread(bias2, 1))], "w3")
            phase_store(nc, k, [(x_table, k["x"], D)])
            phase_gather_sum(nc, s, zd, k, L, x_table, acc, True, "_x")
            phase_add_x(nc, s, k, acc)
            phase_dense(nc, s, k, acc, w[:, 0:D], brow[:, 0:D], [(0, D, ACT.Relu, lambda b: y[:, bass.ds(b * D, D)])], "_m1")
            phase_dense(nc, s, k, y, w[:, D:], brow[:, D:], [(0, D, ACT.Copy, lambda b: acc[:, bass.ds(b * D, D)])], "_m2")
            phase_add_x(nc, s, k, acc)
            phase_layernorm(nc, s, k, acc, "3")
            phase_result(nc, s, k, out)


def phase_zero(nc, k, ap):
    with ExitStack() as ctx:
        sb, ps, sem = scope(nc, ctx, k)
        done = sem("zero_done")
        with nc.Block() as block:
            @block.vector
            def _(dve):
                nc.vector.memset(ap, 0.0).then_inc(done, 1)
                dve.wait_ge(done, 1)


def phase_result(nc, s, k, out):
    with ExitStack() as ctx:
        sb, ps, sem = scope(nc, ctx, k)
        stored = sem("result_stored")
        full = s.N // P
        with nc.Block() as block:
            @block.sync
            def _(sp):
                n = 0
                if full:
                    sp.dma_start(out[0:full * P, :].rearrange("(b p) f -> p b f", p=P),
                                 k["x"][:, 0:full * D].rearrange("p (b f) -> p b f", f=D)).then_inc(stored, 16)
                    n += 16
                if s.N > full * P:
                    sp.dma_start(out[full * P:, :], k["x"][0:s.N - full * P, full * D:(full + 1) * D]).then_inc(stored, 16)
                    n += 16
                sp.wait_ge(stored, n)


_INS = ["x", "src", "dst", "edge_weight", "L0_gnn_query_kernel", "L0_gnn_query_bias", "L0_gnn_key_kernel", "L0_gnn_key_bias",
        "L0_gnn_kernel", "L0_gnn_bias", "L1_gnn_theta_w", "L1_gnn_phi_w", "L1_gnn_fc1_w", "L1_gnn_bn0_g", "L1_gnn_bn0_b",
        "L1_gnn_bn1_g", "L1_gnn_bn1_b", "L2_gnn_W", "L2_gnn_b", "L2_gnn_gamma", "L2_gnn_beta",
        "L3_gnn_W1", "L3_gnn_b1", "L3_gnn_W2", "L3_gnn_b2"]


def kernel(**inputs):
    import numpy as _np
    import concourse.bacc as _bacc
    from concourse.bass_utils import run_bass_kernel_spmd as _run

    nc = _bacc.Bacc("TRN2", target_bir_lowering=False, num_devices=1)
    arrays, args = {}, []
    for name in _INS:
        a = _np.ascontiguousarray(inputs[name])
        arrays[f"in_{name}_dram"] = a
        args.append(nc.dram_tensor(f"in_{name}_dram", a.shape, mybir.dt.from_np(a.dtype), kind="ExternalInput").ap())
    args.append(nc.dram_tensor("out_dram", inputs["x"].shape, F32, kind="ExternalOutput").ap())
    gnn_kernel(nc, *args)
    r = _run(nc, [arrays], core_ids=[0])
    return r.results[0]["out_dram"]
```
